# Optimizing a Trainium2 kernel written in Bass

```python
import numpy as np
import jax
import jax.numpy as jnp

def _softmax(x, axis=-1):
    return jax.nn.softmax(x, axis=axis)

def _gelu(x):
    return jax.nn.gelu(x, approximate=True)

def _silu(x):
    return jax.nn.silu(x)

def _sigmoid(x):
    return jax.nn.sigmoid(x)

def _layernorm(x, axis=-1, eps=1e-05):
    m = jnp.mean(x, axis=axis, keepdims=True)
    v = jnp.var(x, axis=axis, keepdims=True)
    return (x - m) / jnp.sqrt(v + eps)

def _scatter_add(tgt, idx, src, axis=0):
    return tgt.at[idx].add(src)

def _segment_sum(src, seg, n):
    return jax.ops.segment_sum(src, seg, n)
kernel_name = 'mk_perceiver_d2_seqx_r8_bd80f6'

def setup_inputs(seed: int=0):
    np.random.seed(seed)
    _w = jnp.asarray

    def _rec_inputs():
        import jax
        import jax.numpy as jnp
        _rk = jax.random.key(seed)
        x = 7.22e-05 + 1 * jax.random.normal(jax.random.fold_in(_rk, 1), (32, 64, 128), jnp.float32)
        _lenS = 64 - jax.random.randint(jax.random.fold_in(_rk, 7), (32,), 0, max(1, 64 // 4) + 1, jnp.int32)
        _lenS2 = 1601 - jax.random.randint(jax.random.fold_in(_rk, 8), (32,), 0, max(1, 1601 // 4) + 1, jnp.int32)
        _ctx_1024P = jax.random.normal(jax.random.fold_in(_rk, 11), (32, 16, 128), jnp.float32)
        _ctx_1024c = jax.random.dirichlet(jax.random.fold_in(_rk, 511), 0.3 * jnp.ones((16,), jnp.float32), (32, 1601))
        _ctx_1024t = jnp.einsum('bsk,bkd->bsd', _ctx_1024c, _ctx_1024P)
        _ctx_1024t = _ctx_1024t * jax.lax.rsqrt(jnp.mean(jnp.square(_ctx_1024t)) + 1e-12) * 0.953939
        ctx_1024 = 4.13588e-05 + 0.999923 * (_ctx_1024t + 0.3 * jax.random.normal(jax.random.fold_in(_rk, 611), (32, 1601, 128), jnp.float32))
        return (x, ctx_1024)
    x, ctx_1024 = _rec_inputs()

    def _L0_xattn_setup():
        import jax, jax.numpy as jnp
        import numpy as np
        D_MODEL = 128
        NHEAD = 16
        H_DIM = D_MODEL // NHEAD
        key = jax.random.key(seed)
        ks = jax.random.split(key, 11)
        B, S = (4, 256)
        s_in = 1.0 / np.sqrt(D_MODEL)
        return {'query': jax.random.normal(ks[0], (B, S, D_MODEL), jnp.float32), 'key': jax.random.normal(ks[1], (B, S, D_MODEL), jnp.float32), 'value': jax.random.normal(ks[2], (B, S, D_MODEL), jnp.float32), 'Wq': jax.random.normal(ks[3], (NHEAD, D_MODEL, H_DIM), jnp.float32) * s_in, 'bq': jax.random.normal(ks[4], (NHEAD, H_DIM), jnp.float32) * 0.01, 'Wk': jax.random.normal(ks[5], (NHEAD, D_MODEL, H_DIM), jnp.float32) * s_in, 'bk': jax.random.normal(ks[6], (NHEAD, H_DIM), jnp.float32) * 0.01, 'Wv': jax.random.normal(ks[7], (NHEAD, D_MODEL, H_DIM), jnp.float32) * s_in, 'bv': jax.random.normal(ks[8], (NHEAD, H_DIM), jnp.float32) * 0.01, 'Wp': jax.random.normal(ks[9], (D_MODEL, D_MODEL), jnp.float32) * s_in, 'bp': jax.random.normal(ks[10], (D_MODEL,), jnp.float32) * 0.01}
    _L0_xattn_all = _L0_xattn_setup()
    _L0_xattn_in = {k: v for k, v in _L0_xattn_all.items() if k in ('Wq', 'bq', 'Wk', 'bk', 'Wv', 'bv', 'Wp', 'bp')}
    del _L0_xattn_all

    def _L0_attn_setup():
        import jax, jax.numpy as jnp
        import numpy as np
        import math
        B, T, E, H = (2, 256, 128, 16)
        D = E // H

        def _l2norm(t):
            n = jnp.linalg.norm(t, axis=-1, keepdims=True)
            return t / jnp.maximum(n, 1e-12)
        key = jax.random.key(seed)
        ks = jax.random.split(key, 8)
        s = 1.0 / math.sqrt(E)
        x = jax.random.normal(ks[0], (B, T, E), dtype=jnp.float32)
        Wq = jax.random.normal(ks[1], (E, E), dtype=jnp.float32) * s
        Wk = jax.random.normal(ks[2], (E, E), dtype=jnp.float32) * s
        Wv = jax.random.normal(ks[3], (E, E), dtype=jnp.float32) * s
        Wa = jax.random.normal(ks[4], (E, H), dtype=jnp.float32) * s
        Wg = jax.random.normal(ks[5], (E, E), dtype=jnp.float32) * s
        Wo = jax.random.normal(ks[6], (E, E), dtype=jnp.float32) * s
        A_log = jnp.linspace(0.0, math.log(16.0), H, dtype=jnp.float32)
        dt_bias = jnp.zeros((H,), dtype=jnp.float32)
        rms_w = jnp.ones((D,), dtype=jnp.float32)
        return {'x': x, 'Wq': Wq, 'Wk': Wk, 'Wv': Wv, 'Wa': Wa, 'Wg': Wg, 'Wo': Wo, 'A_log': A_log, 'dt_bias': dt_bias, 'rms_w': rms_w}
    _L0_attn_all = _L0_attn_setup()
    _L0_attn_in = {k: v for k, v in _L0_attn_all.items() if k in ('Wq', 'Wk', 'Wv', 'Wa', 'Wg', 'Wo', 'A_log', 'dt_bias', 'rms_w')}
    del _L0_attn_all

    def _L0_ffn_setup():
        import jax, jax.numpy as jnp
        import numpy as np
        DIM = 128
        NUM_EXPERTS = 8
        TOP_K = 2
        HIDDEN = 4 * DIM // TOP_K
        BS, SLEN = (1, 256)

        def _moe(x, gate_w, w_up, w_down, expert_bias):
            bs, slen, dim = x.shape
            xf = x.reshape(-1, dim)
            scores = jax.nn.sigmoid(xf @ gate_w.T)
            biased = scores + expert_bias
            _, sel = jax.lax.top_k(biased, TOP_K)
            top_scores = jnp.take_along_axis(scores, sel, axis=-1)

            def body(acc, ew):
                e, wu, wd = ew
                w_t = jnp.sum(jnp.where(sel == e, top_scores, 0.0), axis=-1)
                xe = xf * w_t[:, None]
                h = jnp.square(jax.nn.relu(xe @ wu.T))
                return (acc + h @ wd.T, None)
            out0 = jnp.zeros_like(xf)
            out, _ = jax.lax.scan(body, out0, (jnp.arange(NUM_EXPERTS), w_up, w_down))
            return out.reshape(bs, slen, dim)
        key = jax.random.key(seed)
        k0, k1, k2, k3 = jax.random.split(key, 4)
        x = jax.random.normal(k0, (BS, SLEN, DIM), dtype=jnp.float32)
        gate_w = jax.random.normal(k1, (NUM_EXPERTS, DIM), dtype=jnp.float32) * 0.02
        w_up = jax.random.normal(k2, (NUM_EXPERTS, HIDDEN, DIM), dtype=jnp.float32) * 0.02
        w_down = jax.random.normal(k3, (NUM_EXPERTS, DIM, HIDDEN), dtype=jnp.float32) * 0.02
        expert_bias = jnp.zeros((NUM_EXPERTS,), dtype=jnp.float32)
        return {'x': x, 'gate_w': gate_w, 'w_up': w_up, 'w_down': w_down, 'expert_bias': expert_bias}
    _L0_ffn_all = _L0_ffn_setup()
    _L0_ffn_in = {k: v for k, v in _L0_ffn_all.items() if k in ('gate_w', 'w_up', 'w_down', 'expert_bias')}
    del _L0_ffn_all

    def _L1_xattn_setup():
        import jax, jax.numpy as jnp
        import numpy as np
        B, S, D, DFF = (4, 256, 128, 512)
        EPS = 1e-05

        def layernorm(x, gamma, beta):
            mu = jnp.mean(x, axis=-1, keepdims=True)
            var = jnp.var(x, axis=-1, keepdims=True)
            return (x - mu) * jax.lax.rsqrt(var + EPS) * gamma + beta

        def attention(Q, K, V, causal):
            d_k = Q.shape[-1]
            scores = jnp.einsum('bqd,bkd->bqk', Q, K) / jnp.sqrt(jnp.asarray(d_k, Q.dtype))
            if causal:
                q_len, k_len = (scores.shape[-2], scores.shape[-1])
                mask = jnp.tril(jnp.ones((q_len, k_len), dtype=bool))
                scores = jnp.where(mask[None], scores, jnp.asarray(-jnp.inf, scores.dtype))
            w = jax.nn.softmax(scores, axis=-1)
            return jnp.einsum('bqk,bkd->bqd', w, V)
        key = jax.random.key(seed)
        ks = jax.random.split(key, 12)
        sd = 0.02
        return {'y': jax.random.normal(ks[0], (B, S, D), jnp.float32), 'Z': jax.random.normal(ks[1], (B, S, D), jnp.float32), 'w1': jax.random.normal(ks[2], (D, DFF), jnp.float32) * sd, 'b1': jnp.zeros((DFF,), jnp.float32), 'w2': jax.random.normal(ks[3], (DFF, D), jnp.float32) * sd, 'b2': jnp.zeros((D,), jnp.float32), 'g1': jnp.ones((D,), jnp.float32), 'beta1': jnp.zeros((D,), jnp.float32), 'g2': jnp.ones((D,), jnp.float32), 'beta2': jnp.zeros((D,), jnp.float32), 'g3': jnp.ones((D,), jnp.float32), 'beta3': jnp.zeros((D,), jnp.float32)}
    _L1_xattn_all = _L1_xattn_setup()
    _L1_xattn_in = {k: v for k, v in _L1_xattn_all.items() if k in ('w1', 'b1', 'w2', 'b2', 'g1', 'beta1', 'g2', 'beta2', 'g3', 'beta3')}
    del _L1_xattn_all

    def _L1_attn_setup():
        import jax, jax.numpy as jnp
        import numpy as np
        import math
        D_MODEL = 128
        N_HEADS = 16
        D_HEAD = D_MODEL // N_HEADS
        WINDOW = 32
        SCALE = 1.0 / math.sqrt(D_HEAD)

        def _window_mask(seq_len: int) -> jnp.ndarray:
            i = jnp.arange(seq_len)[:, None]
            j = jnp.arange(seq_len)[None, :]
            allowed = (j <= i) & (j > i - WINDOW)
            return jnp.where(allowed, 0.0, -jnp.inf).astype(jnp.float32)
        key = jax.random.key(seed)
        kx, kqkv, kout = jax.random.split(key, 3)
        x = jax.random.normal(kx, (2, 256, D_MODEL), dtype=jnp.float32)
        lim_qkv = math.sqrt(6.0 / (D_MODEL + 3 * D_MODEL))
        W_qkv = jax.random.uniform(kqkv, (D_MODEL, 3 * D_MODEL), dtype=jnp.float32, minval=-lim_qkv, maxval=lim_qkv)
        lim_out = math.sqrt(6.0 / (D_MODEL + D_MODEL))
        W_out = jax.random.uniform(kout, (D_MODEL, D_MODEL), dtype=jnp.float32, minval=-lim_out, maxval=lim_out)
        return {'x': x, 'W_qkv': W_qkv, 'W_out': W_out}
    _L1_attn_all = _L1_attn_setup()
    _L1_attn_in = {k: v for k, v in _L1_attn_all.items() if k in ('W_qkv', 'W_out')}
    del _L1_attn_all

    def _L1_ffn_setup():
        import jax, jax.numpy as jnp
        import numpy as np
        DIM = 128
        INTER = 128
        E = 32
        K = 4
        G = 8
        LG = 4
        ROUTE_SCALE = 1.0
        CAP_FACTOR = 1.25
        B, S = (4, 256)

        def _gate(xf, wg):
            logits = xf @ wg.T
            scores = jax.nn.softmax(logits, axis=-1)
            sg = scores.reshape(-1, G, E // G)
            group_scores = sg.max(axis=-1)
            _, gtop = jax.lax.top_k(group_scores, LG)
            keep_g = jnp.sum(jax.nn.one_hot(gtop, G, dtype=jnp.float32), axis=1) > 0
            masked = jnp.where(keep_g[:, :, None], sg, -jnp.inf).reshape(-1, E)
            _, idx = jax.lax.top_k(masked, K)
            w = jnp.take_along_axis(scores, idx, axis=1)
            w = w / (w.sum(-1, keepdims=True) + 1e-09) * ROUTE_SCALE
            return (w.astype(xf.dtype), idx)

        def _forward(x, wg, w1, w2, w3, sw1, sw2, sw3):
            shape = x.shape
            xf = x.reshape(-1, DIM)
            N = xf.shape[0]
            cap = max(1, int(CAP_FACTOR * N * K / E))
            w, idx = _gate(xf, wg)
            fe = idx.reshape(-1)
            oh = jax.nn.one_hot(fe, E, dtype=jnp.int32)
            pos = (jnp.cumsum(oh, axis=0) * oh).sum(-1) - 1
            keep = pos < cap
            dest = jnp.where(keep, fe * cap + pos, E * cap)
            tok = jnp.arange(N * K, dtype=jnp.int32) // K
            buf_tok = jnp.full((E * cap + 1,), N, jnp.int32).at[dest].set(tok)[:-1]
            buf_w = jnp.zeros((E * cap + 1,), x.dtype).at[dest].set(w.reshape(-1))[:-1]
            xp = jnp.concatenate([xf, jnp.zeros((1, DIM), x.dtype)], axis=0)
            xe = xp[buf_tok].reshape(E, cap, DIM)
            h = jax.nn.silu(jnp.einsum('ecd,edh->ech', xe, w1)) * jnp.einsum('ecd,edh->ech', xe, w3)
            out = jnp.einsum('ech,ehd->ecd', h, w2) * buf_w.reshape(E, cap, 1)
            y = jnp.zeros((N + 1, DIM), x.dtype).at[buf_tok].add(out.reshape(E * cap, DIM))[:N]
            z = jax.nn.silu(xf @ sw1) * (xf @ sw3) @ sw2
            return (y + z).reshape(shape)
        key = jax.random.key(seed)
        ks = jax.random.split(key, 9)
        sd = DIM ** (-0.5)
        si = INTER ** (-0.5)
        x = jax.random.normal(ks[0], (B, S, DIM), jnp.float32)
        wg = jax.random.normal(ks[1], (E, DIM), jnp.float32) * sd
        w1 = jax.random.normal(ks[2], (E, DIM, INTER), jnp.float32) * sd
        w3 = jax.random.normal(ks[3], (E, DIM, INTER), jnp.float32) * sd
        w2 = jax.random.normal(ks[4], (E, INTER, DIM), jnp.float32) * si
        sw1 = jax.random.normal(ks[5], (DIM, INTER), jnp.float32) * sd
        sw3 = jax.random.normal(ks[6], (DIM, INTER), jnp.float32) * sd
        sw2 = jax.random.normal(ks[7], (INTER, DIM), jnp.float32) * si
        return dict(x=x, wg=wg, w1=w1, w2=w2, w3=w3, sw1=sw1, sw2=sw2, sw3=sw3)
    _L1_ffn_all = _L1_ffn_setup()
    _L1_ffn_in = {k: v for k, v in _L1_ffn_all.items() if k in ('wg', 'w1', 'w2', 'w3', 'sw1', 'sw2', 'sw3')}
    del _L1_ffn_all
    return {'x': x, 'ctx_1024': ctx_1024, 'L0_xattn_Wq': _L0_xattn_in['Wq'], 'L0_xattn_bq': _L0_xattn_in['bq'], 'L0_xattn_Wk': _L0_xattn_in['Wk'], 'L0_xattn_bk': _L0_xattn_in['bk'], 'L0_xattn_Wv': _L0_xattn_in['Wv'], 'L0_xattn_bv': _L0_xattn_in['bv'], 'L0_xattn_Wp': _L0_xattn_in['Wp'], 'L0_xattn_bp': _L0_xattn_in['bp'], 'L0_attn_Wq': _L0_attn_in['Wq'], 'L0_attn_Wk': _L0_attn_in['Wk'], 'L0_attn_Wv': _L0_attn_in['Wv'], 'L0_attn_Wa': _L0_attn_in['Wa'], 'L0_attn_Wg': _L0_attn_in['Wg'], 'L0_attn_Wo': _L0_attn_in['Wo'], 'L0_attn_A_log': _L0_attn_in['A_log'], 'L0_attn_dt_bias': _L0_attn_in['dt_bias'], 'L0_attn_rms_w': _L0_attn_in['rms_w'], 'L0_ffn_gate_w': _L0_ffn_in['gate_w'], 'L0_ffn_w_up': _L0_ffn_in['w_up'], 'L0_ffn_w_down': _L0_ffn_in['w_down'], 'L0_ffn_expert_bias': _L0_ffn_in['expert_bias'], 'L1_xattn_w1': _L1_xattn_in['w1'], 'L1_xattn_b1': _L1_xattn_in['b1'], 'L1_xattn_w2': _L1_xattn_in['w2'], 'L1_xattn_b2': _L1_xattn_in['b2'], 'L1_xattn_g1': _L1_xattn_in['g1'], 'L1_xattn_beta1': _L1_xattn_in['beta1'], 'L1_xattn_g2': _L1_xattn_in['g2'], 'L1_xattn_beta2': _L1_xattn_in['beta2'], 'L1_xattn_g3': _L1_xattn_in['g3'], 'L1_xattn_beta3': _L1_xattn_in['beta3'], 'L1_attn_W_qkv': _L1_attn_in['W_qkv'], 'L1_attn_W_out': _L1_attn_in['W_out'], 'L1_ffn_wg': _L1_ffn_in['wg'], 'L1_ffn_w1': _L1_ffn_in['w1'], 'L1_ffn_w2': _L1_ffn_in['w2'], 'L1_ffn_w3': _L1_ffn_in['w3'], 'L1_ffn_sw1': _L1_ffn_in['sw1'], 'L1_ffn_sw2': _L1_ffn_in['sw2'], 'L1_ffn_sw3': _L1_ffn_in['sw3']}

def reference(x, ctx_1024, L0_xattn_Wq, L0_xattn_bq, L0_xattn_Wk, L0_xattn_bk, L0_xattn_Wv, L0_xattn_bv, L0_xattn_Wp, L0_xattn_bp, L0_attn_Wq, L0_attn_Wk, L0_attn_Wv, L0_attn_Wa, L0_attn_Wg, L0_attn_Wo, L0_attn_A_log, L0_attn_dt_bias, L0_attn_rms_w, L0_ffn_gate_w, L0_ffn_w_up, L0_ffn_w_down, L0_ffn_expert_bias, L1_xattn_w1, L1_xattn_b1, L1_xattn_w2, L1_xattn_b2, L1_xattn_g1, L1_xattn_beta1, L1_xattn_g2, L1_xattn_beta2, L1_xattn_g3, L1_xattn_beta3, L1_attn_W_qkv, L1_attn_W_out, L1_ffn_wg, L1_ffn_w1, L1_ffn_w2, L1_ffn_w3, L1_ffn_sw1, L1_ffn_sw2, L1_ffn_sw3):
    import jax
    import jax.numpy as jnp

    def _L0_xattn_ref(query, key, value, Wq, bq, Wk, bk, Wv, bv, Wp, bp):
        import jax, jax.numpy as jnp
        import numpy as np
        D_MODEL = 128
        NHEAD = 16
        H_DIM = D_MODEL // NHEAD
        q = jnp.einsum('bsd,hdk->bhsk', query, Wq) + bq[None, :, None, :]
        k = jnp.einsum('bsd,hdk->bhsk', key, Wk) + bk[None, :, None, :]
        v = jnp.einsum('bsd,hdk->bhsk', value, Wv) + bv[None, :, None, :]
        scale = 1.0 / jnp.sqrt(jnp.asarray(H_DIM, q.dtype))
        scores = jnp.einsum('bhik,bhjk->bhij', q, k) * scale
        attn = jax.nn.softmax(scores, axis=-1)
        out = jnp.einsum('bhij,bhjk->bhik', attn, v)
        B, H, S, K = out.shape
        out = out.transpose(0, 2, 1, 3).reshape(B, S, H * K)
        return out @ Wp + bp

    def _L0_attn_ref(x, Wq, Wk, Wv, Wa, Wg, Wo, A_log, dt_bias, rms_w):
        import jax, jax.numpy as jnp
        import numpy as np
        import math
        B, T, E, H = (2, 256, 128, 16)
        D = E // H

        def _l2norm(t):
            n = jnp.linalg.norm(t, axis=-1, keepdims=True)
            return t / jnp.maximum(n, 1e-12)
        b, seq_len, e = x.shape
        h = A_log.shape[0]
        d = e // h
        q = _l2norm((x @ Wq).reshape(b, seq_len, h, d)).transpose(0, 2, 1, 3)
        k = _l2norm((x @ Wk).reshape(b, seq_len, h, d)).transpose(0, 2, 1, 3)
        v = (x @ Wv).reshape(b, seq_len, h, d).transpose(0, 2, 1, 3)
        dt = jax.nn.softplus(x @ Wa + dt_bias)
        alpha = jnp.exp(-jnp.exp(A_log) * dt)
        cum_log = jnp.cumsum(jnp.log(alpha + 1e-08), axis=1).transpose(0, 2, 1)
        log_l = cum_log[..., :, None] - cum_log[..., None, :]
        causal = jnp.tril(jnp.ones((seq_len, seq_len), dtype=bool))
        l_mat = jnp.where(causal, jnp.exp(log_l), 0.0)
        scores = jnp.einsum('bhid,bhjd->bhij', q, k) * l_mat
        out = jnp.einsum('bhij,bhjd->bhid', scores, v)
        out = out * jax.lax.rsqrt(jnp.mean(out * out, axis=-1, keepdims=True) + 1e-06) * rms_w
        out = out.transpose(0, 2, 1, 3).reshape(b, seq_len, e)
        gate = jax.nn.silu(x @ Wg)
        return out * gate @ Wo

    def _L0_ffn_ref(x, gate_w, w_up, w_down, expert_bias):
        import jax, jax.numpy as jnp
        import numpy as np
        DIM = 128
        NUM_EXPERTS = 8
        TOP_K = 2
        HIDDEN = 4 * DIM // TOP_K
        BS, SLEN = (1, 256)

        def _moe(x, gate_w, w_up, w_down, expert_bias):
            bs, slen, dim = x.shape
            xf = x.reshape(-1, dim)
            scores = jax.nn.sigmoid(xf @ gate_w.T)
            biased = scores + expert_bias
            _, sel = jax.lax.top_k(biased, TOP_K)
            top_scores = jnp.take_along_axis(scores, sel, axis=-1)

            def body(acc, ew):
                e, wu, wd = ew
                w_t = jnp.sum(jnp.where(sel == e, top_scores, 0.0), axis=-1)
                xe = xf * w_t[:, None]
                h = jnp.square(jax.nn.relu(xe @ wu.T))
                return (acc + h @ wd.T, None)
            out0 = jnp.zeros_like(xf)
            out, _ = jax.lax.scan(body, out0, (jnp.arange(NUM_EXPERTS), w_up, w_down))
            return out.reshape(bs, slen, dim)
        return _moe(x, gate_w, w_up, w_down, expert_bias)

    def _L1_xattn_ref(y, Z, w1, b1, w2, b2, g1, beta1, g2, beta2, g3, beta3):
        import jax, jax.numpy as jnp
        import numpy as np
        B, S, D, DFF = (4, 256, 128, 512)
        EPS = 1e-05

        def layernorm(x, gamma, beta):
            mu = jnp.mean(x, axis=-1, keepdims=True)
            var = jnp.var(x, axis=-1, keepdims=True)
            return (x - mu) * jax.lax.rsqrt(var + EPS) * gamma + beta

        def attention(Q, K, V, causal):
            d_k = Q.shape[-1]
            scores = jnp.einsum('bqd,bkd->bqk', Q, K) / jnp.sqrt(jnp.asarray(d_k, Q.dtype))
            if causal:
                q_len, k_len = (scores.shape[-2], scores.shape[-1])
                mask = jnp.tril(jnp.ones((q_len, k_len), dtype=bool))
                scores = jnp.where(mask[None], scores, jnp.asarray(-jnp.inf, scores.dtype))
            w = jax.nn.softmax(scores, axis=-1)
            return jnp.einsum('bqk,bkd->bqd', w, V)
        sa = attention(y, y, y, causal=True)
        y = layernorm(y + sa, g1, beta1)
        ca = attention(y, Z, Z, causal=False)
        y = layernorm(y + ca, g2, beta2)
        h = jax.nn.relu(jnp.einsum('bsd,df->bsf', y, w1) + b1)
        ff = jnp.einsum('bsf,fd->bsd', h, w2) + b2
        y = layernorm(y + ff, g3, beta3)
        return y

    def _L1_attn_ref(x, W_qkv, W_out):
        import jax, jax.numpy as jnp
        import numpy as np
        import math
        D_MODEL = 128
        N_HEADS = 16
        D_HEAD = D_MODEL // N_HEADS
        WINDOW = 32
        SCALE = 1.0 / math.sqrt(D_HEAD)

        def _window_mask(seq_len: int) -> jnp.ndarray:
            i = jnp.arange(seq_len)[:, None]
            j = jnp.arange(seq_len)[None, :]
            allowed = (j <= i) & (j > i - WINDOW)
            return jnp.where(allowed, 0.0, -jnp.inf).astype(jnp.float32)
        B, S, _ = x.shape
        qkv = x @ W_qkv
        qkv = qkv.reshape(B, S, 3, N_HEADS, D_HEAD)
        qkv = jnp.transpose(qkv, (2, 0, 3, 1, 4))
        q, k, v = (qkv[0], qkv[1], qkv[2])
        scores = jnp.einsum('bhsd,bhtd->bhst', q, k) * SCALE
        scores = scores + _window_mask(S)[None, None]
        weights = jax.nn.softmax(scores, axis=-1)
        out = jnp.einsum('bhst,bhtd->bhsd', weights, v)
        out = jnp.transpose(out, (0, 2, 1, 3)).reshape(B, S, D_MODEL)
        return out @ W_out

    def _L1_ffn_ref(x, wg, w1, w2, w3, sw1, sw2, sw3):
        import jax, jax.numpy as jnp
        import numpy as np
        DIM = 128
        INTER = 128
        E = 32
        K = 4
        G = 8
        LG = 4
        ROUTE_SCALE = 1.0
        CAP_FACTOR = 1.25
        B, S = (4, 256)

        def _gate(xf, wg):
            logits = xf @ wg.T
            scores = jax.nn.softmax(logits, axis=-1)
            sg = scores.reshape(-1, G, E // G)
            group_scores = sg.max(axis=-1)
            _, gtop = jax.lax.top_k(group_scores, LG)
            keep_g = jnp.sum(jax.nn.one_hot(gtop, G, dtype=jnp.float32), axis=1) > 0
            masked = jnp.where(keep_g[:, :, None], sg, -jnp.inf).reshape(-1, E)
            _, idx = jax.lax.top_k(masked, K)
            w = jnp.take_along_axis(scores, idx, axis=1)
            w = w / (w.sum(-1, keepdims=True) + 1e-09) * ROUTE_SCALE
            return (w.astype(xf.dtype), idx)

        def _forward(x, wg, w1, w2, w3, sw1, sw2, sw3):
            shape = x.shape
            xf = x.reshape(-1, DIM)
            N = xf.shape[0]
            cap = max(1, int(CAP_FACTOR * N * K / E))
            w, idx = _gate(xf, wg)
            fe = idx.reshape(-1)
            oh = jax.nn.one_hot(fe, E, dtype=jnp.int32)
            pos = (jnp.cumsum(oh, axis=0) * oh).sum(-1) - 1
            keep = pos < cap
            dest = jnp.where(keep, fe * cap + pos, E * cap)
            tok = jnp.arange(N * K, dtype=jnp.int32) // K
            buf_tok = jnp.full((E * cap + 1,), N, jnp.int32).at[dest].set(tok)[:-1]
            buf_w = jnp.zeros((E * cap + 1,), x.dtype).at[dest].set(w.reshape(-1))[:-1]
            xp = jnp.concatenate([xf, jnp.zeros((1, DIM), x.dtype)], axis=0)
            xe = xp[buf_tok].reshape(E, cap, DIM)
            h = jax.nn.silu(jnp.einsum('ecd,edh->ech', xe, w1)) * jnp.einsum('ecd,edh->ech', xe, w3)
            out = jnp.einsum('ech,ehd->ecd', h, w2) * buf_w.reshape(E, cap, 1)
            y = jnp.zeros((N + 1, DIM), x.dtype).at[buf_tok].add(out.reshape(E * cap, DIM))[:N]
            z = jax.nn.silu(xf @ sw1) * (xf @ sw3) @ sw2
            return (y + z).reshape(shape)
        return _forward(x, wg, w1, w2, w3, sw1, sw2, sw3)
    x = x + _L0_xattn_ref(_layernorm(x, axis=-1), ctx_1024, ctx_1024, L0_xattn_Wq, L0_xattn_bq, L0_xattn_Wk, L0_xattn_bk, L0_xattn_Wv, L0_xattn_bv, L0_xattn_Wp, L0_xattn_bp)
    x = x + _L0_attn_ref(_layernorm(x, axis=-1), L0_attn_Wq, L0_attn_Wk, L0_attn_Wv, L0_attn_Wa, L0_attn_Wg, L0_attn_Wo, L0_attn_A_log, L0_attn_dt_bias, L0_attn_rms_w)
    x = x + _L0_ffn_ref(_layernorm(x, axis=-1), L0_ffn_gate_w, L0_ffn_w_up, L0_ffn_w_down, L0_ffn_expert_bias)
    x = x + _L1_xattn_ref(_layernorm(x, axis=-1), ctx_1024, L1_xattn_w1, L1_xattn_b1, L1_xattn_w2, L1_xattn_b2, L1_xattn_g1, L1_xattn_beta1, L1_xattn_g2, L1_xattn_beta2, L1_xattn_g3, L1_xattn_beta3)
    x = x + _L1_attn_ref(_layernorm(x, axis=-1), L1_attn_W_qkv, L1_attn_W_out)
    x = x + _L1_ffn_ref(_layernorm(x, axis=-1), L1_ffn_wg, L1_ffn_w1, L1_ffn_w2, L1_ffn_w3, L1_ffn_sw1, L1_ffn_sw2, L1_ffn_sw3)
    return x

_drawn_inputs = setup_inputs


def setup_inputs(seed=0):
    import zlib

    import numpy as np

    out = dict(_drawn_inputs(seed))
    spreads = {'L0_attn_dt_bias': (0.0, 0.448),
     'L0_attn_rms_w': (1.0, 0.2),
     'L0_ffn_expert_bias': (0.0, 0.618),
     'L1_xattn_b1': (0.0, 0.348),
     'L1_xattn_b2': (0.0, 0.1),
     'L1_xattn_g1': (1.0, 0.2),
     'L1_xattn_beta1': (0.0, 0.1),
     'L1_xattn_g2': (1.0, 0.2),
     'L1_xattn_beta2': (0.0, 0.1),
     'L1_xattn_g3': (1.0, 0.2),
     'L1_xattn_beta3': (0.0, 0.1)}
    factors = {'L0_xattn_bq': 4.713,
     'L0_xattn_bk': 8.0,
     'L0_ffn_gate_w': 7.055,
     'L0_ffn_w_up': 5.548,
     'L0_ffn_w_down': 5.113}
    for name, (base, spread) in spreads.items():
        noise = np.random.default_rng([zlib.crc32(name.encode()), seed]).standard_normal(out[name].shape)
        drawn = base * np.exp(spread * noise) if base else spread * noise
        out[name] = jnp.asarray(drawn.astype(out[name].dtype))
    for name, factor in factors.items():
        out[name] = (out[name] * factor).astype(out[name].dtype)
    return out
```

```python
from contextlib import ExitStack

import concourse.bass as bass
from concourse import mybir

ALU = mybir.AluOpType
ACT = mybir.ActivationFunctionType
AX = mybir.AxisListType
F32 = mybir.dt.float32
F32R = mybir.dt.float32r

P = 128
B, S, D = 32, 64, 128
TOK = B * S
NT = TOK // P
H, DH = 16, 8
NPAIR = H // 2
K = 1601
KPAD = K + 1
KT = (K + P - 1) // P
BANKS = [(0, 400), (400, 800), (800, 1200), (1200, KPAD)]
QSCALE = DH ** -0.5
EPS = 1e-5
SCALE1 = D ** -0.5
NEVER = -1e30
WINDOW = 32
E1, TOP1 = 8, 2
E2, TOP2, G2, LG2 = 32, 4, 8, 4
CAP = max(1, int(1.25 * TOK * TOP2 / E2))


def clear(nc, semaphores):
    with nc.Block() as block:
        @block.sync
        def _(sp):
            for s in semaphores:
                sp.sem_clear(s)
def first_cross_attention(nc, d, X):
    with ExitStack() as ctx:
        def sb(name, shape, dt=F32):
            return ctx.enter_context(nc.sbuf_tensor(name, shape, dt))

        own = []

        def sem(name):
            own.append(ctx.enter_context(nc.semaphore(name)))
            return own[-1]

        qT = sb("qT", [P, TOK])
        cq = sb("cq", [P, B, NPAIR])
        bvp = sb("bvp", [P, D])
        headmask = sb("headmask", [P, H])
        wkT = sb("wkT", [P, D])
        wv = sb("wv", [P, D])
        ident = sb("ident", [P, P])
        densel = sb("densel", [P, P])
        wp_rows = sb("wp_rows", [P, 2, 2, D])

        with ExitStack() as c0:
            def sb0(name, shape, dt=F32):
                return c0.enter_context(nc.sbuf_tensor(name, shape, dt))

            own0 = []

            def sem0(name):
                own0.append(c0.enter_context(nc.semaphore(name)))
                return own0[-1]

            xn = sb0("xn", [P, NT, D])
            xnT = sb0("xnT", [P, TOK])
            stats = sb0("stats", [P, NT, 6])
            mv = sb0("mv", [P, NT, 2])
            std = sb0("std", [P, NT])
            rstd = sb0("rstd", [P, NT])
            wq = sb0("wq", [P, D])
            wp = sb0("wp", [P, D])
            bq = sb0("bq", [P, 1])
            bk = sb0("bk", [P, 1])
            bv = sb0("bv", [P, 1])
            bp_rows = sb0("bp_rows", [P, D])
            bksel = sb0("bksel", [P, H])
            ps = c0.enter_context(nc.psum_tensor("ps_q", [P, 8, 512], F32))
            x_in, w_in = sem0("x_in"), sem0("w_in")
            stat, aggr, vare, root, inv = (sem0(n) for n in ("stat", "aggr", "vare", "root", "inv"))
            xn_ok, tr_ok, xnT_ok, q_mm, q_ok = (sem0(n) for n in ("xn_ok", "tr_ok", "xnT_ok", "q_mm", "q_ok"))
            sel_ok, c_mm, c_ok, v_mm0, bvp_ok, xres = (sem0(n) for n in ("sel_ok", "c_mm", "c_ok", "v_mm0", "bvp_ok", "xres"))
            loads = [(wq, d["wq"]), (wp, d["wp"]), (bq, d["bq"]), (bk, d["bk"]), (bv, d["bv"]),
                     (bp_rows, d["bp_rows"]), (headmask, d["headmask"]), (wkT, d["wkT"]), (wv, d["wv"]),
                     (ident, d["ident"]), (densel, d["densel"])]
            c0.callback(clear, nc, own0)
            block = c0.enter_context(nc.Block())

            @block.sync
            def _(sp):
                sp.dma_start(X[:, :, :], d["x"].rearrange("(t p) d -> p t d", p=P)).then_inc(x_in, 16)
                for dst, src in loads:
                    sp.dma_start(dst[:, :], src).then_inc(w_in, 16)
                sp.dma_start(wp_rows[:, :, :, :], d["wp_rows"]).then_inc(w_in, 16)

            all_loads = 16 * (len(loads) + 1)

            @block.vector
            def _(dve):
                dve.wait_ge(x_in, 16)
                for t in range(NT):
                    nc.vector.bn_stats(stats[:, t, :], X[:, t, :]).then_inc(stat, 1)
                dve.wait_ge(stat, NT)
                for t in range(NT):
                    nc.vector.bn_aggr(mv[:, t, :], stats[:, t, :]).then_inc(aggr, 1)
                dve.wait_ge(aggr, NT)
                nc.vector.tensor_scalar_add(std[:, :], mv[:, :, 1], EPS).then_inc(vare, 1)
                dve.wait_ge(root, 1)
                nc.vector.reciprocal(rstd[:, :], std[:, :]).then_inc(inv, 1)
                dve.wait_ge(inv, 1)
                for t in range(NT):
                    nc.vector.tensor_scalar(xn[:, t, :], X[:, t, :], mv[:, t, 0:1], rstd[:, t:t + 1],
                                            ALU.subtract, ALU.mult).then_inc(xn_ok, 1)
                dve.wait_ge(w_in, all_loads)
                nc.vector.tensor_scalar(bksel[:, :], headmask[:, :], bk[:, :], None, ALU.mult).then_inc(sel_ok, 1)
                for k in range(4):
                    dve.wait_ge(tr_ok, k + 1)
                    nc.vector.tensor_copy(xnT[:, k * 512:(k + 1) * 512], ps[:, k, :]).then_inc(xnT_ok, 1)
                for k in range(4):
                    dve.wait_ge(q_mm, k + 1)
                    nc.vector.tensor_scalar(qT[:, k * 512:(k + 1) * 512], ps[:, 4 + k, :], bq[:, :], QSCALE,
                                            ALU.add, ALU.mult).then_inc(q_ok, 1)
                dve.wait_ge(c_mm, 1)
                cps = ps[:, 0, :].rearrange("p (b j h) -> p b j h", b=B, h=2)
                nc.vector.tensor_copy(cq[0:64, :, :], cps[0:64, :, :, 0]).then_inc(c_ok, 1)
                nc.vector.tensor_copy(cq[64:128, :, :], cps[64:128, :, :, 1]).then_inc(c_ok, 1)
                dve.wait_ge(v_mm0, 1)
                nc.vector.tensor_tensor(bvp[:, :], ps[:, 1, 0:D], bp_rows[:, :], ALU.add).then_inc(bvp_ok, 1)
                dve.wait_ge(bvp_ok, 1)
                nc.vector.tensor_tensor(X[:, :, :], X[:, :, :], bvp[:, :].unsqueeze(1).broadcast_to([P, NT, D]),
                                        ALU.add).then_inc(xres, 1)

            @block.scalar
            def _(act):
                act.wait_ge(vare, 1)
                nc.scalar.activation(std[:, :], std[:, :], ACT.Sqrt).then_inc(root, 1)

            @block.tensor
            def _(pe):
                pe.wait_ge(w_in, all_loads)
                for t in range(NT):
                    pe.wait_ge(xn_ok, t + 1)
                    last = nc.tensor.transpose(ps[:, t // 4, (t % 4) * P:(t % 4 + 1) * P], xn[:, t, :], ident[:, :])
                    if t % 4 == 3:
                        last.then_inc(tr_ok, 1)
                for k in range(4):
                    pe.wait_ge(xnT_ok, k + 1)
                    nc.tensor.matmul(ps[:, 4 + k, :], wq[:, :], xnT[:, k * 512:(k + 1) * 512],
                                     start=True, stop=True).then_inc(q_mm, 1)
                pe.wait_ge(q_ok, 4)
                pe.wait_ge(sel_ok, 1)
                for b in range(B):
                    for h in range(2):
                        last = nc.tensor.matmul(ps[S * h:S * h + S, 0, b * H:(b + 1) * H], qT[:, b * S:(b + 1) * S],
                                                bksel[:, :], start=True, stop=True)
                last.then_inc(c_mm, 1)
                nc.tensor.matmul(ps[:, 1, 0:D], bv[:, :].broadcast_to([P, P]), wp[:, :],
                                 start=True, stop=True).then_inc(v_mm0, 1)

        raw = sb("ctx_raw", [P, 2, KPAD])
        chi = sb("ctx_hi", [P, 2, KPAD], F32R)
        clo = sb("ctx_lo", [P, 2, KPAD], F32R)
        qbd = sb("qbd", [P, 2, H, S])
        qraw = sb("q_raw", [P, H * S])
        qhi = sb("q_hi", [P, 2, H * S], F32R)
        qlo = sb("q_lo", [P, 2, H * S], F32R)
        V = sb("V", [P, 2, KT, NPAIR, 32])
        E = sb("E", [P, 2, KPAD])
        PT = sb("PT", [P, 2, 4, KT, P])
        mx = sb("mx", [P, 2, 4])
        m = sb("m", [P, 2, 1])
        nb = sb("nb", [P, 2, 1])
        O = sb("O", [P, 2, 2, P])
        rden = sb("rden", [P, 2, P])
        On = sb("On", [P, 2, P])
        psS = ctx.enter_context(nc.psum_tensor("psS", [P, 4, 512], F32))
        psT = ctx.enter_context(nc.psum_tensor("psT", [P, 2, 512], F32))
        psM = ctx.enter_context(nc.psum_tensor("psM", [P, 512], F32))
        psO = ctx.enter_context(nc.psum_tensor("psO", [P, 512], F32))
        ctx_in = [sem("ctx_in0"), sem("ctx_in1")]
        hi_done, split_done, qbd_done = sem("hi_done"), sem("split_done"), sem("qbd_done")
        qt_mm, qr_done, ql_done = sem("qt_mm"), sem("qr_done"), sem("ql_done")
        v_mm, v_done = sem("v_mm"), sem("v_done")
        s_mm, max_done, m_done, nb_done, exp_done = (sem(n) for n in ("s_mm", "max_done", "m_done", "nb_done", "exp_done"))
        t_mm, ta_done, td_done = sem("t_mm"), sem("ta_done"), sem("td_done")
        pv_mm, o_done = sem("pv_mm"), sem("o_done")
        den_mm, rec_done, on_done, fin_mm, x_done = (sem(n) for n in ("den_mm", "rec_done", "on_done", "fin_mm", "x_done"))
        zeroed = sem("zeroed")
        VGROUPS = [range(0, 4), range(4, 8), range(12, 13), range(8, 12)]
        CH = [range(0, 4), range(4, 7), range(7, 10), range(10, 13)]
        ctx.callback(clear, nc, own)
        block = ctx.enter_context(nc.Block())

        def wait(eng, s, v):
            if not isinstance(v, int) or v > 0:
                eng.wait_ge(s, v)

        def known(b):
            return isinstance(b, int)

        def batches(eng, batch):
            batch(0, 0)
            batch(1, 1)
            with eng.Fori(1, B // 2 - 1) as i:
                batch(i * 2, 0)
                batch(i * 2 + 1, 1)
            for b in range(B - 2, B + 2):
                batch(b, b % 2)

        @block.sync
        def _(sp):
            def load(b, par):
                wait(sp, v_mm, (b - 1) * 4)
                wait(sp, split_done, b - 1)
                sp.dma_start(raw[:, par, 0:K], d["ctxT"][b, :, :] if known(b) else
                             d["ctxT"][bass.ds(b, 1), :, :].rearrange("o p k -> (o p) k")).then_inc(ctx_in[par], 16)
            sp.wait_ge(zeroed, 1)
            load(0, 0)
            load(1, 1)
            with sp.Fori(1, B // 2) as i:
                load(i * 2, 0)
                load(i * 2 + 1, 1)

        @block.gpsimd
        def _(pool):
            nc.gpsimd.memset(V[:, :, :, :, :], 0.0).then_inc(zeroed, 1)
            nc.gpsimd.memset(raw[:, :, K:KPAD], 0.0).then_inc(zeroed, 1)
            pool.wait_ge(zeroed, 2)
            nc.gpsimd.memset(V[:, :, :, :, 16:17], 1.0).then_inc(zeroed, 1)

            def queries(b, par):
                wait(pool, qt_mm, 2 * (b - 1))
                q = qT[:, bass.ds(b * S, S)].unsqueeze(1).broadcast_to([P, H, S])
                nc.gpsimd.tensor_tensor(qbd[:, par, :, :], headmask[:, :].unsqueeze(2).broadcast_to([P, H, S]), q,
                                        ALU.mult).then_inc(qbd_done, 1)

            def prepare(b, par, after):
                wait(pool, s_mm, 32 * (b - 1))
                pool.wait_ge(ctx_in[par], 16 * (b // 2 + 1))
                pool.wait_ge(qr_done, 2 * b + 2)
                if after:
                    queries(b + 1, 1 - par)
                nc.gpsimd.tensor_copy(qhi[:, par, :], qraw[:, :]).then_inc(hi_done, 1)
                nc.gpsimd.tensor_copy(chi[:, par, :], raw[:, par, :]).then_inc(hi_done, 1)
                pool.wait_ge(hi_done, 2 * b + 2)
                nc.gpsimd.tensor_tensor(qlo[:, par, :], qraw[:, :], qhi[:, par, :].bitcast(F32),
                                        ALU.subtract).then_inc(ql_done, 1)
                nc.gpsimd.tensor_tensor(clo[:, par, :], raw[:, par, :], chi[:, par, :].bitcast(F32),
                                        ALU.subtract).then_inc(split_done, 1)
            queries(0, 0)
            prepare(0, 0, True)
            prepare(1, 1, True)
            with pool.Fori(1, B // 2 - 1) as i:
                prepare(i * 2, 0, True)
                prepare(i * 2 + 1, 1, True)
            prepare(B - 2, 0, True)
            prepare(B - 1, 1, False)

        @block.tensor
        def _(pe):
            def project_q(b, par, half):
                wait(pe, qbd_done, b + 1)
                nc.tensor.matmul(psM[:, :], wkT[:, :],
                                 qbd[:, par, 8 * half:8 * half + 8, :].rearrange("p h s -> p (h s)"),
                                 start=True, stop=True).then_inc(qt_mm, 1)

            def values(b, par, k):
                if k == 0:
                    pe.wait_ge(ctx_in[par], 16 * (b // 2 + 1))
                for t in VGROUPS[k]:
                    n = min(P, K - t * P)
                    last = nc.tensor.matmul(psM[0:n, (t % 4) * P:(t % 4 + 1) * P], raw[:, par, t * P:t * P + n],
                                            wv[:, :], start=True, stop=True)
                last.then_inc(v_mm, 1)

            def scores(b, par, p, between):
                g = b * NPAIR + p
                wait(pe, ql_done, b + 1)
                if p == 0:
                    wait(pe, split_done, b + 1)
                qs = slice(p * P, (p + 1) * P)
                for n, (k0, k1) in enumerate(BANKS):
                    wait(pe, exp_done, 4 * g - 4 + n + 1)
                    for i, (q, c) in enumerate(((qhi, chi), (qhi, clo), (qlo, chi))):
                        last = nc.tensor.matmul(psS[:, n, 0:k1 - k0], q[:, par, qs], c[:, par, k0:k1],
                                                start=(i == 0), stop=(i == 2))
                    last.then_inc(s_mm, 1)
                    if n == 1:
                        between(0)
                between(1)
                between(2)

            def transposes(g, ep, k):
                wait(pe, exp_done, 4 * g + min(k + 2, 4))
                if k < 2:
                    wait(pe, td_done, 2 * g - 1 + k)
                else:
                    wait(pe, ta_done, 2 * g + k - 1)
                for t in range(4 * k, min(4 * k + 4, KT)):
                    n = min(P, K - t * P)
                    last = nc.tensor.transpose(psT[0:n, k % 2, (t % 4) * P:(t % 4 + 1) * P],
                                               E[:, ep, t * P:t * P + n], ident[:, :])
                last.then_inc(t_mm, 1)

            def weigh_values(q, qpar, vpar, half, chunk):
                if chunk == 0:
                    wait(pe, ta_done, 8 * q + 8)
                    wait(pe, td_done, 8 * q + 8)
                    wait(pe, o_done, q)
                for t in CH[chunk]:
                    n = min(P, K - t * P)
                    for r in range(4):
                        last = nc.tensor.matmul(psO[32 * r:32 * r + 32, 0:P], V[0:n, vpar, t, 4 * half + r, :],
                                                PT[0:n, qpar, r, t, :], start=(t == 0), stop=(t == KT - 1))
                if chunk == 3:
                    last.then_inc(pv_mm, 1)

            def sums(b, par):
                wait(pe, o_done, 2 * b + 2)
                wait(pe, x_done, b)
                wait(pe, v_done, 4 * (b + 2) if not known(b) or b + 2 < B else 4 * B)
                nc.tensor.matmul(psM[:, 0:2 * P], densel[:, :], O[:, par, :, :].rearrange("p a b -> p (a b)"),
                                 start=True, stop=True).then_inc(den_mm, 1)

            def output(b, par):
                wait(pe, on_done, b + 1)
                wait(pe, v_done, 4 * (b + 3) + 2 if not known(b) or b + 3 < B else 4 * B)
                for i in range(4):
                    a, h = i // 2, i % 2
                    last = nc.tensor.matmul(psM[64 * par:64 * par + 64, 3 * P:4 * P], On[:, a, h * S:(h + 1) * S],
                                            wp_rows[:, a, h, :], start=(i == 0), stop=(i == 3))
                last.then_inc(fin_mm, 1)

            def batch(b, par):
                for p in range(NPAIR):
                    live = not known(b) or b < B
                    behind = (p > 0 and live) or (p == 0 and (not known(b) or 0 < b <= B))

                    def turn(k):
                        if behind:
                            transposes(b * NPAIR + p - 1, (p - 1) % 2, k)
                    if live:
                        scores(b, par, p, turn)
                    else:
                        for k in range(3):
                            turn(k)
                    if p == 0 and (not known(b) or 0 < b <= B):
                        weigh_values(2 * b - 2, 0, 1 - par, 0, 3)
                    if 1 <= p <= 4 and (not known(b) or 0 < b <= B):
                        if p == 1:
                            wait(pe, v_done, 4 * b)
                        weigh_values(2 * b - 1, 1, 1 - par, 1, p - 1)
                    if p >= 5 and live:
                        if p == 5:
                            wait(pe, v_done, 4 * b + 4)
                        weigh_values(2 * b, 0, par, 0, p - 5)
                    turn(3)
                    if p == 0 and (not known(b) or b >= 2):
                        sums(b - 2, par)
                    nxt = not known(b) or b + 1 < B
                    if nxt and p in (2, 3):
                        if p == 2:
                            wait(pe, rec_done, b - 1)
                        wait(pe, qr_done, 2 * (b + 1) + p - 2)
                        project_q(b + 1, 1 - par, p - 2)
                    if p == 6 and (not known(b) or b >= 2):
                        output(b - 2, par)
                    if nxt and p >= 4:
                        if p == 4:
                            wait(pe, qr_done, 2 * (b + 2))
                        if p == 7:
                            wait(pe, x_done, b - 1)
                        wait(pe, v_done, 4 * (b + 1) + p - 4)
                        values(b + 1, 1 - par, p - 4)
            for half in range(2):
                wait(pe, qr_done, half)
                project_q(0, 0, half)
            wait(pe, qr_done, 2)
            for k in range(4):
                wait(pe, v_done, k)
                values(0, 0, k)
            batches(pe, batch)

        @block.scalar
        def _(act):
            def q_part(b, half):
                act.wait_ge(qt_mm, 2 * b + half + 1)
                wait(act, ql_done, b)
                nc.scalar.activation(qraw[:, half * 512:(half + 1) * 512], psM[:, :], ACT.Copy).then_inc(qr_done, 1)

            def v_part(b, par, k):
                act.wait_ge(v_mm, 4 * b + k + 1)
                wait(act, pv_mm, 2 * b - 2)
                t0, n = VGROUPS[k].start, len(VGROUPS[k])
                rows = P if n == 4 else K - 12 * P
                nc.scalar.activation(V[0:rows, par, t0:t0 + n, :, 0:16],
                                     psM[0:rows, 0:n * P].rearrange("p (t j c) -> p t j c", t=n, c=16),
                                     ACT.Copy).then_inc(v_done, 1)

            def tiles(g, q, r, qpar):
                wait(act, pv_mm, q - 1)
                for k in (0, 1):
                    act.wait_ge(t_mm, 4 * g + k + 1)
                    nc.scalar.activation(PT[:, qpar, r, 4 * k:4 * k + 4, :],
                                         psT[:, k, :].rearrange("p (t c) -> p t c", t=4), ACT.Copy).then_inc(ta_done, 1)

            def exps(g, ep):
                wait(act, t_mm, 4 * (g - 1))
                act.wait_ge(nb_done, g + 1)
                for n, (k0, k1) in enumerate(BANKS):
                    k1 = min(k1, K)
                    nc.scalar.activation(E[:, ep, k0:k1], psS[:, n, 0:k1 - k0], ACT.Exp,
                                         bias=nb[:, ep, :]).then_inc(exp_done, 1)

            def batch(b, par):
                for p in range(NPAIR):
                    live = not known(b) or b < B
                    if p > 0 and live:
                        tiles(b * NPAIR + p - 1, 2 * b + (p - 1) // 4, (p - 1) % 4, (p - 1) // 4)
                    elif p == 0 and (not known(b) or 0 < b <= B):
                        tiles(b * NPAIR - 1, 2 * b - 1, 3, 1)
                    if live:
                        exps(b * NPAIR + p, p % 2)
                    nxt = not known(b) or b + 1 < B
                    if nxt and p in (2, 3):
                        q_part(b + 1, p - 2)
                    if nxt and p >= 4:
                        v_part(b + 1, 1 - par, p - 4)

            act.wait_ge(zeroed, 3)
            q_part(0, 0)
            q_part(0, 1)
            for k in range(4):
                v_part(0, 0, k)
            batches(act, batch)

        @block.vector
        def _(dve):
            def maxima(b, g, p, ep):
                wait(dve, exp_done, 4 * (g - 1))
                for n, (k0, k1) in enumerate(BANKS):
                    k1 = min(k1, K)
                    dve.wait_ge(s_mm, 4 * g + n + 1)
                    nc.vector.reduce_max(mx[:, ep, n:n + 1], psS[:, n, 0:k1 - k0], AX.X).then_inc(max_done, 1)
                dve.wait_ge(max_done, 4 * g + 4)
                nc.vector.reduce_max(m[:, ep, :], mx[:, ep, :], AX.X).then_inc(m_done, 1)
                dve.wait_ge(m_done, g + 1)
                c = cq[:, bass.ds(b, 1), p:p + 1].rearrange("p a b -> p (a b)") if not known(b) else cq[:, b, p:p + 1]
                nc.vector.scalar_tensor_tensor(out=nb[:, ep, :], in0=m[:, ep, :], scalar=c, in1=c, op0=ALU.add,
                                               op1=ALU.subtract, reverse1=True).then_inc(nb_done, 1)

            def tiles(g, q, r, qpar):
                wait(dve, pv_mm, q - 1)
                for k in (2, 3):
                    dve.wait_ge(t_mm, 4 * g + k + 1)
                    n = 4 if k == 2 else 1
                    rows = P if k == 2 else K - 12 * P
                    nc.vector.tensor_copy(PT[0:rows, qpar, r, 4 * k:4 * k + n, :],
                                          psT[0:rows, k - 2, 0:n * P].rearrange("p (t c) -> p t c", t=n)).then_inc(td_done, 1)

            def take_sums(q, par, half):
                dve.wait_ge(pv_mm, q + 1)
                nc.vector.tensor_copy(O[:, par, half, :], psO[:, 0:P]).then_inc(o_done, 1)

            def normalise(b, par):
                dve.wait_ge(den_mm, b + 1)
                wait(dve, fin_mm, b)
                nc.vector.reciprocal(rden[:, :, :], psM[:, 0:2 * P].rearrange("p (a b) -> p a b", a=2)).then_inc(rec_done, 1)
                dve.wait_ge(rec_done, b + 1)
                nc.vector.tensor_tensor(On[:, :, :], O[:, par, :, :], rden[:, :, :], ALU.mult).then_inc(on_done, 1)

            def residual(b, par):
                dve.wait_ge(fin_mm, b + 1)
                dve.wait_ge(v_done, 4 * (b + 3) + 3 if not known(b) or b + 3 < B else 4 * B)
                r = slice(64 * par, 64 * par + 64)
                x = X[r, b // 2, :] if known(b) else X[r, bass.ds(b // 2, 1), :].rearrange("p a b -> p (a b)")
                nc.vector.tensor_tensor(x, psM[r, 3 * P:4 * P], x, ALU.add).then_inc(x_done, 1)

            def batch(b, par):
                for p in range(NPAIR):
                    live = not known(b) or b < B
                    after = not known(b) or 0 < b <= B
                    if live:
                        maxima(b, b * NPAIR + p, p, p % 2)
                    if not known(b) or b >= 2:
                        if p == 1:
                            normalise(b - 2, par)
                        if p == 7:
                            residual(b - 2, par)
                    if p > 0 and live:
                        tiles(b * NPAIR + p - 1, 2 * b + (p - 1) // 4, (p - 1) % 4, (p - 1) // 4)
                    elif p == 0 and after:
                        tiles(b * NPAIR - 1, 2 * b - 1, 3, 1)
                    if p == 0 and after:
                        take_sums(2 * b - 2, 1 - par, 0)
                    if p == 4 and after:
                        take_sums(2 * b - 1, 1 - par, 1)

            batches(dve, batch)


G = 4
NG = NT // G
GT = G * P


def tiles_of(X, i):
    return X[:, bass.ds(i * G, G), :]


def load_all(nc, sp, pairs, sem):
    for dst, src in pairs:
        sp.dma_start(dst[tuple(slice(None) for _ in dst.shape)], src).then_inc(sem, 16)
    return 16 * len(pairs)


class Norm:

    def __init__(self, nc, sb, sem, name):
        self.nc = nc
        self.stats, self.mv = sb(name + "_stats", [P, G, 6]), sb(name + "_mv", [P, G, 2])
        self.std, self.rstd = sb(name + "_std", [P, G]), sb(name + "_rstd", [P, G])
        self.stat, self.aggr, self.vare = sem(name + "_stat"), sem(name + "_aggr"), sem(name + "_vare")
        self.root, self.inv = sem(name + "_root"), sem(name + "_inv")
        self.cleared = sem(name + "_cleared")

    def spread(self, act, i):
        act.wait_ge(self.vare, i + 1)
        self.nc.scalar.activation(self.std[:, :], self.std[:, :], ACT.Sqrt).then_inc(self.root, 1)

    def moments(self, dve, i, x):
        v = self.nc.vector
        for t in range(G):
            v.bn_stats(self.stats[:, t, :], x(t)).then_inc(self.stat, 1)
        dve.wait_ge(self.stat, i * G + G)
        v.memset(self.std[:, :], 0.0).then_inc(self.cleared, 1)
        for t in range(G):
            v.bn_aggr(self.mv[:, t, :], self.stats[:, t, :]).then_inc(self.aggr, 1)
        dve.wait_ge(self.aggr, i * G + G)
        v.tensor_scalar_add(self.std[:, :], self.mv[:, :, 1], EPS).then_inc(self.vare, 1)
        dve.wait_ge(self.root, i + 1)
        v.reciprocal(self.rstd[:, :], self.std[:, :]).then_inc(self.inv, 1)
        dve.wait_ge(self.inv, i + 1)

    def apply(self, out, x, t):
        return self.nc.vector.tensor_scalar(out, x, self.mv[:, t, 0:1], self.rstd[:, t:t + 1],
                                            ALU.subtract, ALU.mult)


def linear_attention(nc, d, X):
    with ExitStack() as ctx:
        def sb(name, shape, dt=F32):
            return ctx.enter_context(nc.sbuf_tensor("la_" + name, shape, dt))

        own = []

        def sem(name):
            own.append(ctx.enter_context(nc.semaphore("la_" + name)))
            return own[-1]

        names = ("wq2", "wk2", "wg2", "wv2", "wo2", "wa", "dtb", "alog", "rmsw", "upto", "after", "hlmask", "headmask",
                 "blockones", "ident")
        w = {n: sb(n, list(d[n].shape)) for n in names}
        nega = sb("nega", [P, H])
        ln = Norm(nc, sb, sem, "ln")
        xn = sb("xn", [P, G, D])
        xnT = sb("xnT", [P, GT])
        sq = sb("sq", [P, 2, GT])
        nrm = sb("nrm", [P, 2, GT])
        qk = sb("qk", [P, 2, GT])
        v = sb("v", [P, 2, G, D])
        gate = sb("gate", [P, GT])
        z, nz, sp_, la = (sb(n, [P, G, H]) for n in ("z", "nz", "sp", "la"))
        LM = sb("LM", [P, 2, H, S])
        qbd = sb("qbd", [P, 2, 2, H, S])
        Ex = sb("Ex", [P, 2, H, S])
        ST = sb("ST", [P, 2, H, S])
        mo = sb("mo", [P, 2, 2, 4, S])
        oT = sb("oT", [P, GT])
        y = sb("y", [P, GT])
        ps = ctx.enter_context(nc.psum_tensor("la_ps", [P, 8, 512], F32))
        (w_in, neg_ok, neg2_ok, xn_ok, tr_mm, xnT_ok, qk_mm, g_mm, v_mm, a_mm, sq_ok, ss_mm, ssroot, mx_ok, rc_ok, qk_ok,
         v_ok, gate_ok, z_ok, e_ok, sp_ok, la_ok, lm_ok, qb0, qb1, d_mm, ex_ok, exm_ok, s_mm, st_ok, o_mm, mo_ok, oT_ok,
         osq, ms_mm, mroot, mrec, y1_ok, y_ok, out_mm, x_ok, zc, ec, zeroed) = (sem(n) for n in (
            "w_in", "neg_ok", "neg2_ok", "xn_ok", "tr_mm", "xnT_ok", "qk_mm", "g_mm", "v_mm", "a_mm", "sq_ok", "ss_mm",
            "ssroot", "mx_ok", "rc_ok", "qk_ok", "v_ok", "gate_ok", "z_ok", "e_ok", "sp_ok", "la_ok", "lm_ok", "qb0",
            "qb1", "d_mm", "ex_ok", "exm_ok", "s_mm", "st_ok", "o_mm", "mo_ok", "oT_ok", "osq", "ms_mm", "mroot",
            "mrec", "y1_ok", "y_ok", "out_mm", "x_ok", "zc", "ec", "zeroed"))
        ctx.callback(clear, nc, own)
        block = ctx.enter_context(nc.Block())
        loaded = 16 * len(names)

        @block.sync
        def _(sp):
            load_all(nc, sp, [(w[n], d[n]) for n in names], w_in)

        @block.gpsimd
        def _(pool):
            nc.gpsimd.memset(v[:, :, :, :], 0.0).then_inc(zeroed, 1)
            pool.wait_ge(w_in, loaded)
            with pool.Fori(0, NG) as i:
                for t in range(G):
                    u = t % 2
                    pool.wait_ge(qk_ok, i * 2 + 1)
                    if t >= 2:
                        pool.wait_ge(s_mm, i * G + t - 1)
                    q = qk[:, 0, t * P + S:t * P + P].unsqueeze(1).broadcast_to([P, H, S])
                    nc.gpsimd.tensor_tensor(qbd[:, u, 1, :, :], w["headmask"][:, :].unsqueeze(2).broadcast_to([P, H, S]),
                                            q, ALU.mult).then_inc(qb1, 1)
                    pool.wait_ge(ex_ok, i * G + t + 1)
                    nc.gpsimd.tensor_tensor(Ex[:, u, :, :], Ex[:, u, :, :],
                                            w["upto"][:, :].unsqueeze(1).broadcast_to([P, H, S]),
                                            ALU.mult).then_inc(exm_ok, 1)

        @block.scalar
        def _(act):
            act.wait_ge(w_in, loaded)
            act.wait_ge(zeroed, 1)
            nc.scalar.activation(nega[:, :], w["alog"][:, :], ACT.Exp).then_inc(neg_ok, 1)
            with act.Fori(0, NG) as i:
                ln.spread(act, i)
                act.wait_ge(tr_mm, i + 1)
                nc.scalar.activation(xnT[:, :], ps[:, 0, :], ACT.Copy).then_inc(xnT_ok, 1)
                act.wait_ge(qk_mm, i * 2 + 1)
                nc.scalar.activation(sq[:, 0, :], ps[:, 1, :], ACT.Square).then_inc(sq_ok, 1)
                act.wait_ge(qk_mm, i * 2 + 2)
                nc.scalar.activation(sq[:, 1, :], ps[:, 2, :], ACT.Square).then_inc(sq_ok, 1)
                act.wait_ge(v_mm, i + 1)
                for b in range(2):
                    r = slice(S * b, S * b + S)
                    nc.scalar.activation(v[r, b, :, :], ps[r, 4, :].rearrange("p (t d) -> p t d", t=G),
                                         ACT.Copy).then_inc(v_ok, 1)
                act.wait_ge(ss_mm, i * 2 + 2)
                nc.scalar.activation(nrm[:, :, :], ps[:, 6:8, :], ACT.Sqrt).then_inc(ssroot, 1)
                act.wait_ge(g_mm, i + 1)
                nc.scalar.activation(gate[:, :], ps[:, 3, :], ACT.Silu).then_inc(gate_ok, 1)
                act.wait_ge(z_ok, i + 1)
                nc.scalar.activation(nz[:, :, :], nz[:, :, :], ACT.Exp).then_inc(ec, 1)
                act.wait_ge(ec, i * 3 + 1)
                nc.scalar.activation(nz[:, :, :], nz[:, :, :], ACT.Ln, bias=1.0).then_inc(e_ok, 1)
                act.wait_ge(sp_ok, i + 1)
                nc.scalar.activation(la[:, :, :], sp_[:, :, :], ACT.Exp).then_inc(ec, 1)
                act.wait_ge(ec, i * 3 + 2)
                nc.scalar.activation(sp_[:, :, :], la[:, :, :], ACT.Copy, bias=1e-8).then_inc(ec, 1)
                act.wait_ge(ec, i * 3 + 3)
                nc.scalar.activation(la[:, :, :], sp_[:, :, :], ACT.Ln).then_inc(la_ok, 1)
                for t in range(G):
                    act.wait_ge(d_mm, i * G + t + 1)
                    if t >= 2:
                        act.wait_ge(st_ok, i * G + t - 1)
                    nc.scalar.activation(Ex[:, t % 2, :, :], ps[:, 6:8, :].rearrange("p a (h s) -> p (a h) s", s=S),
                                         ACT.Exp).then_inc(ex_ok, 1)
                act.wait_ge(oT_ok, i * G + G)
                nc.scalar.activation(sq[:, 0, :], oT[:, :], ACT.Square).then_inc(osq, 1)
                act.wait_ge(ms_mm, i + 1)
                nc.scalar.activation(nrm[:, 0, :], ps[:, 0, :], ACT.Copy, scale=1.0 / DH, bias=1e-6).then_inc(zc, 1)
                act.wait_ge(zc, i + 1)
                nc.scalar.activation(nrm[:, 0, :], nrm[:, 0, :], ACT.Sqrt).then_inc(mroot, 1)

        @block.tensor
        def _(pe):
            pe.wait_ge(w_in, loaded)
            with pe.Fori(0, NG) as i:
                for t in range(G):
                    pe.wait_ge(xn_ok, i * G + t + 1)
                    last = nc.tensor.transpose(ps[:, 0, t * P:(t + 1) * P], xn[:, t, :], w["ident"][:, :])
                last.then_inc(tr_mm, 1)
                pe.wait_ge(xnT_ok, i + 1)
                nc.tensor.matmul(ps[:, 1, :], w["wq2"][:, :], xnT[:, :], start=True, stop=True).then_inc(qk_mm, 1)
                nc.tensor.matmul(ps[:, 2, :], w["wk2"][:, :], xnT[:, :], start=True, stop=True).then_inc(qk_mm, 1)
                nc.tensor.matmul(ps[:, 3, :], w["wg2"][:, :], xnT[:, :], start=True, stop=True).then_inc(g_mm, 1)
                for t in range(G):
                    last = nc.tensor.matmul(ps[:, 5, t * H:(t + 1) * H], xnT[:, t * P:(t + 1) * P], w["wa"][:, :],
                                            start=True, stop=True)
                last.then_inc(a_mm, 1)
                for t in range(G):
                    last = nc.tensor.matmul(ps[:, 4, t * P:(t + 1) * P], xnT[:, t * P:(t + 1) * P], w["wv2"][:, :],
                                            start=True, stop=True)
                last.then_inc(v_mm, 1)
                for k in range(2):
                    pe.wait_ge(sq_ok, i * 2 + k + 1)
                    nc.tensor.matmul(ps[:, 6 + k, :], w["blockones"][:, :], sq[:, k, :], start=True, stop=True).then_inc(ss_mm, 1)
                for t in range(G):
                    u = t % 2
                    pe.wait_ge(lm_ok, i * G + t + 1)
                    if t == 0:
                        pe.wait_ge(ssroot, i + 1)
                    else:
                        pe.wait_ge(ex_ok, i * G + t)
                    for k in range(2):
                        last = nc.tensor.matmul(ps[:, 6 + k, :], w["after"][:, :],
                                                LM[:, u, 8 * k:8 * k + 8, :].rearrange("p h s -> p (h s)"),
                                                start=True, stop=True)
                    last.then_inc(d_mm, 1)
                    pe.wait_ge(qk_ok, i * 2 + 2)
                    pe.wait_ge(qb0, i * G + t + 1)
                    pe.wait_ge(qb1, i * G + t + 1)
                    if t > 0:
                        pe.wait_ge(st_ok, i * G + t)
                    for k in range(2):
                        for b in range(2):
                            last = nc.tensor.matmul(ps[S * b:S * b + S, 1 + k, :], qk[:, 1, t * P + S * b:t * P + S * b + S],
                                                    qbd[:, u, b, 8 * k:8 * k + 8, :].rearrange("p h s -> p (h s)"),
                                                    start=True, stop=True)
                    last.then_inc(s_mm, 1)
                    pe.wait_ge(st_ok, i * G + t + 1)
                    if t == 0:
                        pe.wait_ge(gate_ok, i + 1)
                        pe.wait_ge(v_ok, i * 2 + 2)
                    else:
                        pe.wait_ge(mo_ok, i * G + t)
                    for b in range(2):
                        for g in range(4):
                            last = nc.tensor.matmul(ps[32 * g:32 * g + 32, 3 + b, 0:4 * S], v[:, b, t, 32 * g:32 * g + 32],
                                                    ST[:, u, 4 * g:4 * g + 4, :].rearrange("p h s -> p (h s)"),
                                                    start=True, stop=True)
                    last.then_inc(o_mm, 1)
                pe.wait_ge(osq, i + 1)
                nc.tensor.matmul(ps[:, 0, :], w["blockones"][:, :], sq[:, 0, :], start=True, stop=True).then_inc(ms_mm, 1)
                pe.wait_ge(y_ok, i + 1)
                for t in range(G):
                    last = nc.tensor.matmul(ps[:, 5, t * P:(t + 1) * P], y[:, t * P:(t + 1) * P], w["wo2"][:, :],
                                            start=True, stop=True)
                last.then_inc(out_mm, 1)

        @block.vector
        def _(dve):
            dve.wait_ge(w_in, loaded)
            dve.wait_ge(neg_ok, 1)
            nc.vector.tensor_scalar(nega[:, :], nega[:, :], -1.0, None, ALU.mult).then_inc(neg2_ok, 1)
            with dve.Fori(0, NG) as i:
                ln.moments(dve, i, lambda t: X[:, bass.ds(i * G + t, 1), :].rearrange("p a b -> p (a b)"))
                for t in range(G):
                    ln.apply(xn[:, t, :], X[:, bass.ds(i * G + t, 1), :].rearrange("p a b -> p (a b)"), t).then_inc(xn_ok, 1)
                dve.wait_ge(a_mm, i + 1)
                hb = lambda a: a[:, :].unsqueeze(1).broadcast_to([P, G, H])
                nc.vector.tensor_tensor(z[:, :, :], ps[:, 5, 0:G * H].rearrange("p (t h) -> p t h", t=G), hb(w["dtb"]),
                                        ALU.add).then_inc(e_ok if False else rc_ok, 1)
                dve.wait_ge(rc_ok, i * 4 + 1)
                nc.vector.tensor_scalar(la[:, :, :], z[:, :, :], -1.0, None, ALU.mult).then_inc(rc_ok, 1)
                dve.wait_ge(rc_ok, i * 4 + 2)
                nc.vector.tensor_tensor(nz[:, :, :], z[:, :, :], la[:, :, :], ALU.min).then_inc(z_ok, 1)
                dve.wait_ge(ssroot, i + 1)
                nc.vector.tensor_scalar(nrm[:, :, :], nrm[:, :, :], 1e-12, None, ALU.max).then_inc(mx_ok, 1)
                dve.wait_ge(mx_ok, i + 1)
                nc.vector.reciprocal(nrm[:, :, :], nrm[:, :, :]).then_inc(rc_ok, 1)
                dve.wait_ge(rc_ok, i * 4 + 3)
                for k in range(2):
                    nc.vector.tensor_tensor(qk[:, k, :], ps[:, 1 + k, :], nrm[:, k, :], ALU.mult).then_inc(qk_ok, 1)
                dve.wait_ge(e_ok, i + 1)
                nc.vector.scalar_tensor_tensor(out=z[:, :, :], in0=z[:, :, :], scalar=0.0, in1=nz[:, :, :], op0=ALU.max,
                                               op1=ALU.add).then_inc(rc_ok, 1)
                dve.wait_ge(rc_ok, i * 4 + 4)
                nc.vector.tensor_tensor(sp_[:, :, :], z[:, :, :], hb(nega), ALU.mult).then_inc(sp_ok, 1)

                def before(t):
                    u = t % 2
                    if t >= 2:
                        dve.wait_ge(d_mm, i * G + t - 1)
                    nc.vector.tensor_tensor(LM[:, u, :, :], la[:, t, :].unsqueeze(2).broadcast_to([P, H, S]),
                                            w["upto"][:, :].unsqueeze(1).broadcast_to([P, H, S]), ALU.mult).then_inc(lm_ok, 1)
                    if t >= 2:
                        dve.wait_ge(s_mm, i * G + t - 1)
                    q = qk[:, 0, t * P:t * P + S].unsqueeze(1).broadcast_to([P, H, S])
                    nc.vector.tensor_tensor(qbd[:, u, 0, :, :], w["headmask"][:, :].unsqueeze(2).broadcast_to([P, H, S]), q,
                                            ALU.mult).then_inc(qb0, 1)

                def after(t):
                    u = t % 2
                    dve.wait_ge(exm_ok, i * G + t + 1)
                    dve.wait_ge(s_mm, i * G + t + 1)
                    nc.vector.tensor_tensor(ST[:, u, :, :], ps[:, 1:3, :].rearrange("p a (h s) -> p (a h) s", s=S),
                                            Ex[:, u, :, :], ALU.mult).then_inc(st_ok, 1)

                def finish(t):
                    u = t % 2
                    dve.wait_ge(o_mm, i * G + t + 1)
                    nc.vector.tensor_tensor(mo[:, u, :, :, :], ps[:, 3:5, 0:4 * S].rearrange("p b (h s) -> p b h s", s=S),
                                            w["hlmask"][:, :].unsqueeze(1).unsqueeze(3).broadcast_to([P, 2, 4, S]),
                                            ALU.mult).then_inc(mo_ok, 1)
                    dve.wait_ge(mo_ok, i * G + t + 1)
                    nc.vector.reduce_sum(oT[:, t * P:(t + 1) * P].rearrange("p (b s) -> p b s", s=S),
                                         mo[:, u, :, :, :].rearrange("p b h s -> p b s h"), AX.X).then_inc(oT_ok, 1)

                dve.wait_ge(qk_ok, i * 2 + 2)
                dve.wait_ge(la_ok, i + 1)
                before(0)
                for t in range(G):
                    if t + 1 < G:
                        before(t + 1)
                    after(t)
                    finish(t)
                dve.wait_ge(mroot, i + 1)
                nc.vector.reciprocal(nrm[:, 0, :], nrm[:, 0, :]).then_inc(mrec, 1)
                dve.wait_ge(mrec, i * 2 + 1)
                nc.vector.scalar_tensor_tensor(out=nrm[:, 1, :], in0=oT[:, :], scalar=w["rmsw"][:, :], in1=nrm[:, 0, :],
                                               op0=ALU.mult, op1=ALU.mult).then_inc(mrec, 1)
                dve.wait_ge(mrec, i * 2 + 2)
                nc.vector.tensor_tensor(y[:, :], nrm[:, 1, :], gate[:, :], ALU.mult).then_inc(y_ok, 1)
                dve.wait_ge(out_mm, i + 1)
                nc.vector.tensor_tensor(tiles_of(X, i), ps[:, 5, :].rearrange("p (t d) -> p t d", t=G), tiles_of(X, i),
                                        ALU.add).then_inc(x_ok, 1)
                dve.wait_ge(x_ok, i + 1)


def first_experts(nc, d, X):
    with ExitStack() as ctx:
        def sb(name, shape, dt=F32):
            return ctx.enter_context(nc.sbuf_tensor("m1_" + name, shape, dt))

        own = []

        def sem(name):
            own.append(ctx.enter_context(nc.semaphore("m1_" + name)))
            return own[-1]

        names = ("ident", "gate1", "ebias", "before8")
        w = {n: sb(n, list(d[n].shape)) for n in names}
        ln = Norm(nc, sb, sem, "ln")
        xn = sb("xn", [P, 2, G, D])
        xnT = sb("xnT", [P, TOK])
        sc, bi, rank, w2 = (sb(n, [P, NT, E1]) for n in ("sc", "bi", "rank", "w2"))
        gt, eq = sb("gt", [P, NT, E1, E1]), sb("eq", [P, NT, E1, E1])
        up = sb("up", [P, 2, 2 * P])
        down = sb("down", [P, 2, 2, D])
        relu = sb("relu", [P, 4, GT])
        h = sb("h", [P, 4, GT])
        ps = ctx.enter_context(nc.psum_tensor("m1_ps", [P, 8, 512], F32))
        w_in, xn_ok, tr_mm, xnT_ok, lg_mm, sg, rt, r_ok, h_mm, relu_ok, h_ok, out_mm, x_ok = (sem(n) for n in (
            "w_in", "xn_ok", "tr_mm", "xnT_ok", "lg_mm", "sg", "rt", "r_ok", "h_mm", "relu_ok", "h_ok", "out_mm", "x_ok"))
        ex_in = [sem("ex_in0"), sem("ex_in1")]
        ctx.callback(clear, nc, own)
        block = ctx.enter_context(nc.Block())
        loaded = 16 * len(names)
        PAIRS = E1 // 2

        def wait(eng, s, v):
            if not isinstance(v, int) or v > 0:
                eng.wait_ge(s, v)

        def pairs_of_experts(eng, body):
            body(0, False)
            with eng.Fori(1, PAIRS - 1) as i:
                body(i, False)
            body(PAIRS - 1, True)

        @block.sync
        def _(sp):
            load_all(nc, sp, [(w[n], d[n]) for n in names], w_in)

            def body(i, last):
                for u in range(2):
                    wait(sp, out_mm, i * 8 + 4 * u - 4)
                    e = bass.ds(i * 2 + u, 1)
                    sp.dma_start(up[:, u, :], d["up1"][e, :, :].rearrange("o p k -> (o p) k")).then_inc(ex_in[u], 16)
                    sp.dma_start(down[:, u, :, :], d["down1"][e, :, :, :].rearrange("o p k c -> (o p) k c")).then_inc(ex_in[u], 16)
            pairs_of_experts(sp, body)

        @block.gpsimd
        def _(pool):
            def body(i, last):
                for q in range(16):
                    n, m = i * 16 + q, i * 8 + q // 2
                    pool.wait_ge(relu_ok, n + 1)
                    wait(pool, out_mm, m - 1)
                    nc.gpsimd.tensor_tensor(h[:, q % 4, :], relu[:, q % 4, :], relu[:, q % 4, :], ALU.mult).then_inc(h_ok, 1)
            pairs_of_experts(pool, body)

        @block.scalar
        def _(act):
            for i in range(NG):
                ln.spread(act, i)
                act.wait_ge(tr_mm, i + 1)
                nc.scalar.activation(xnT[:, i * GT:(i + 1) * GT], ps[:, i % 2, :], ACT.Copy).then_inc(xnT_ok, 1)
            act.wait_ge(lg_mm, 1)
            nc.scalar.activation(sc[:, :, :], ps[:, 2, 0:NT * E1].rearrange("p (t e) -> p t e", e=E1),
                                 ACT.Sigmoid).then_inc(sg, 1)

            def body(i, last):
                for q in range(16):
                    n = i * 16 + q
                    act.wait_ge(h_mm, n + 1)
                    wait(act, h_ok, n - 3)
                    nc.scalar.activation(relu[:, q % 4, :], ps[:, 4 + q % 4, :], ACT.Relu).then_inc(relu_ok, 1)
            pairs_of_experts(act, body)

        @block.tensor
        def _(pe):
            pe.wait_ge(w_in, loaded)
            for i in range(NG):
                if i >= 2:
                    pe.wait_ge(xnT_ok, i - 1)
                for t in range(G):
                    pe.wait_ge(xn_ok, i * G + t + 1)
                    last = nc.tensor.transpose(ps[:, i % 2, t * P:(t + 1) * P], xn[:, i % 2, t, :], w["ident"][:, :])
                last.then_inc(tr_mm, 1)
            pe.wait_ge(xnT_ok, NG)
            for t in range(NT):
                last = nc.tensor.matmul(ps[:, 2, t * E1:(t + 1) * E1], xnT[:, t * P:(t + 1) * P], w["gate1"][:, :],
                                        start=True, stop=True)
            last.then_inc(lg_mm, 1)

            def hidden(i, q):
                u, c = q // 4 % 2, q % 4
                if c == 0:
                    pe.wait_ge(ex_in[u], i * 32 + (32 if q < 8 else 64))
                for k in range(2):
                    n = i * 16 + 2 * q + k
                    wait(pe, relu_ok, n - 3)
                    nc.tensor.matmul(ps[:, 4 + (2 * q + k) % 4, :], up[:, u, k * P:(k + 1) * P],
                                     xnT[:, c * GT:(c + 1) * GT], start=True, stop=True).then_inc(h_mm, 1)

            def body(i, last_pair):
                for q in range(8):
                    m = i * 8 + q
                    if not (last_pair and q == 7):
                        hidden(i, q + 1)
                    pe.wait_ge(h_ok, m * 2 + 2)
                    wait(pe, x_ok, m * 4 - 4)
                    for t in range(G):
                        for k in range(2):
                            last = nc.tensor.matmul(ps[:, 2 + q % 2, t * P:(t + 1) * P],
                                                    h[:, (2 * q + k) % 4, t * P:(t + 1) * P], down[:, q // 4, k, :],
                                                    start=(k == 0), stop=(k == 1))
                    last.then_inc(out_mm, 1)
            pe.wait_ge(sg, 1)
            hidden(0, 0)
            pairs_of_experts(pe, body)

        @block.vector
        def _(dve):
            for i in range(NG):
                ln.moments(dve, i, lambda t: X[:, i * G + t, :])
                if i >= 2:
                    dve.wait_ge(tr_mm, i - 1)
                for t in range(G):
                    ln.apply(xn[:, i % 2, t, :], X[:, i * G + t, :], t).then_inc(xn_ok, 1)
            dve.wait_ge(sg, 1)
            rows = lambda a: a[:, :].unsqueeze(1).broadcast_to([P, NT, E1])
            nc.vector.tensor_tensor(bi[:, :, :], sc[:, :, :], rows(w["ebias"]), ALU.add).then_inc(rt, 1)
            dve.wait_ge(rt, 1)
            other, own = bi[:, :, :].unsqueeze(2).broadcast_to([P, NT, E1, E1]), bi[:, :, :].unsqueeze(3).broadcast_to([P, NT, E1, E1])
            nc.vector.tensor_tensor(gt[:, :, :, :], other, own, ALU.is_gt).then_inc(rt, 1)
            nc.vector.tensor_tensor(eq[:, :, :, :], other, own, ALU.is_equal).then_inc(rt, 1)
            dve.wait_ge(rt, 3)
            nc.vector.tensor_tensor(eq[:, :, :, :], eq[:, :, :, :],
                                    w["before8"][:, :, :].unsqueeze(1).broadcast_to([P, NT, E1, E1]), ALU.mult).then_inc(rt, 1)
            dve.wait_ge(rt, 4)
            nc.vector.tensor_tensor(gt[:, :, :, :], gt[:, :, :, :], eq[:, :, :, :], ALU.add).then_inc(rt, 1)
            dve.wait_ge(rt, 5)
            nc.vector.reduce_sum(rank[:, :, :], gt[:, :, :, :], AX.X).then_inc(rt, 1)
            dve.wait_ge(rt, 6)
            nc.vector.scalar_tensor_tensor(out=w2[:, :, :], in0=rank[:, :, :], scalar=float(TOP1), in1=sc[:, :, :],
                                           op0=ALU.is_lt, op1=ALU.mult).then_inc(rt, 1)
            dve.wait_ge(rt, 7)
            nc.vector.tensor_tensor(w2[:, :, :], w2[:, :, :], w2[:, :, :], ALU.mult).then_inc(rt, 1)
            dve.wait_ge(rt, 8)

            def body(i, last):
                for q in range(8):
                    m = i * 8 + q
                    dve.wait_ge(out_mm, m + 1)
                    wait(dve, x_ok, m * 4 - 12)
                    for t in range(G):
                        x = X[:, G * (q % 4) + t, :]
                        we = w2[:, G * (q % 4) + t, bass.ds(i * 2 + q // 4, 1)]
                        nc.vector.scalar_tensor_tensor(out=x, in0=ps[:, 2 + q % 2, t * P:(t + 1) * P], scalar=we, in1=x,
                                                       op0=ALU.mult, op1=ALU.add).then_inc(x_ok, 1)
            pairs_of_experts(dve, body)


def row_tiles(a):
    return a[:, :].unsqueeze(1).broadcast_to([P, G, D])


def decoder_self_attention(nc, d, X, Y, YT):
    with ExitStack() as ctx:
        def sb(name, shape, dt=F32):
            return ctx.enter_context(nc.sbuf_tensor("sa_" + name, shape, dt))

        own = []

        def sem(name):
            own.append(ctx.enter_context(nc.semaphore("sa_" + name)))
            return own[-1]

        names = ("ident", "causal2", "g1", "beta1")
        w = {n: sb(n, list(d[n].shape)) for n in names}
        ln, ln1 = Norm(nc, sb, sem, "ln"), Norm(nc, sb, sem, "ln1")
        y, sm, pm, y1p, n1, y1 = (sb(n, [P, G, D]) for n in ("y", "sm", "pm", "y1p", "n1", "y1"))
        yT, pmT = sb("yT", [P, GT]), sb("pmT", [P, GT])
        mx, nb, sums, rs = (sb(n, [P, G]) for n in ("mx", "nb", "sums", "rs"))
        ps = ctx.enter_context(nc.psum_tensor("sa_ps", [P, 8, 512], F32))
        (w_in, y_ok, tr_mm, yT_ok, s_mm, sm_ok, mx_ok, nb_ok, p_ok, pt_mm, pmT_ok, sa_mm, rs_ok, y1p_ok, n1_ok, m_ok, y1_ok,
         y1t_mm, yt_ok, yy_ok) = (sem(n) for n in (
            "w_in", "y_ok", "tr_mm", "yT_ok", "s_mm", "sm_ok", "mx_ok", "nb_ok", "p_ok", "pt_mm", "pmT_ok", "sa_mm",
            "rs_ok", "y1p_ok", "n1_ok", "m_ok", "y1_ok", "y1t_mm", "yt_ok", "yy_ok"))
        ctx.callback(clear, nc, own)
        block = ctx.enter_context(nc.Block())
        loaded = 16 * len(names)

        @block.sync
        def _(sp):
            load_all(nc, sp, [(w[n], d[n]) for n in names], w_in)

        @block.scalar
        def _(act):
            with act.Fori(0, NG) as i:
                ln.spread(act, i)
                act.wait_ge(tr_mm, i + 1)
                nc.scalar.activation(yT[:, :], ps[:, 0, :], ACT.Copy).then_inc(yT_ok, 1)
                act.wait_ge(nb_ok, i + 1)
                for t in range(G):
                    nc.scalar.activation(pm[:, t, :], sm[:, t, :], ACT.Exp, bias=nb[:, t:t + 1], scale=SCALE1,
                                         accum_out=sums[:, t:t + 1]).then_inc(p_ok, 1)
                act.wait_ge(pt_mm, i + 1)
                nc.scalar.activation(pmT[:, :], ps[:, 2, :], ACT.Copy).then_inc(pmT_ok, 1)
                ln1.spread(act, i)
                act.wait_ge(y1t_mm, i + 1)
                nc.scalar.activation(YT[:, bass.ds(i * GT, GT)], ps[:, 4, :], ACT.Copy).then_inc(yt_ok, 1)

        @block.tensor
        def _(pe):
            pe.wait_ge(w_in, loaded)
            with pe.Fori(0, NG) as i:
                for t in range(G):
                    pe.wait_ge(y_ok, i * G + t + 1)
                    last = nc.tensor.transpose(ps[:, 0, t * P:(t + 1) * P], y[:, t, :], w["ident"][:, :])
                last.then_inc(tr_mm, 1)
                pe.wait_ge(yT_ok, i + 1)
                for t in range(G):
                    yt = yT[:, t * P:(t + 1) * P]
                    last = nc.tensor.matmul(ps[:, 1, t * P:(t + 1) * P], yt, yt, start=True, stop=True)
                last.then_inc(s_mm, 1)
                for t in range(G):
                    pe.wait_ge(p_ok, i * G + t + 1)
                    last = nc.tensor.transpose(ps[:, 2, t * P:(t + 1) * P], pm[:, t, :], w["ident"][:, :])
                last.then_inc(pt_mm, 1)
                pe.wait_ge(pmT_ok, i + 1)
                for t in range(G):
                    last = nc.tensor.matmul(ps[:, 3, t * P:(t + 1) * P], pmT[:, t * P:(t + 1) * P], y[:, t, :],
                                            start=True, stop=True)
                last.then_inc(sa_mm, 1)
                pe.wait_ge(y1_ok, i + 1)
                for t in range(G):
                    last = nc.tensor.transpose(ps[:, 4, t * P:(t + 1) * P], y1[:, t, :], w["ident"][:, :])
                last.then_inc(y1t_mm, 1)

        @block.vector
        def _(dve):
            dve.wait_ge(w_in, loaded)
            with dve.Fori(0, NG) as i:
                xt = lambda t: X[:, bass.ds(i * G + t, 1), :].rearrange("p a b -> p (a b)")
                ln.moments(dve, i, xt)
                for t in range(G):
                    ln.apply(y[:, t, :], xt(t), t).then_inc(y_ok, 1)
                dve.wait_ge(s_mm, i + 1)
                nc.vector.tensor_tensor(sm[:, :, :], ps[:, 1, :].rearrange("p (t d) -> p t d", t=G), row_tiles(w["causal2"]),
                                        ALU.add).then_inc(sm_ok, 1)
                dve.wait_ge(sm_ok, i + 1)
                nc.vector.reduce_max(mx[:, :], sm[:, :, :], AX.X).then_inc(mx_ok, 1)
                dve.wait_ge(mx_ok, i + 1)
                nc.vector.tensor_scalar(nb[:, :], mx[:, :], -SCALE1, None, ALU.mult).then_inc(nb_ok, 1)
                dve.wait_ge(p_ok, i * G + G)
                nc.vector.reciprocal(rs[:, :], sums[:, :]).then_inc(rs_ok, 1)
                dve.wait_ge(rs_ok, i + 1)
                dve.wait_ge(sa_mm, i + 1)
                dve.wait_ge(y_ok, i * G + G)
                for t in range(G):
                    nc.vector.scalar_tensor_tensor(out=y1p[:, t, :], in0=ps[:, 3, t * P:(t + 1) * P], scalar=rs[:, t:t + 1],
                                                   in1=y[:, t, :], op0=ALU.mult, op1=ALU.add).then_inc(y1p_ok, 1)
                dve.wait_ge(y1p_ok, i * G + G)
                ln1.moments(dve, i, lambda t: y1p[:, t, :])
                for t in range(G):
                    ln1.apply(n1[:, t, :], y1p[:, t, :], t).then_inc(n1_ok, 1)
                dve.wait_ge(n1_ok, i * G + G)
                nc.vector.tensor_tensor(n1[:, :, :], n1[:, :, :], row_tiles(w["g1"]), ALU.mult).then_inc(m_ok, 1)
                dve.wait_ge(m_ok, i + 1)
                nc.vector.tensor_tensor(y1[:, :, :], n1[:, :, :], row_tiles(w["beta1"]), ALU.add).then_inc(y1_ok, 1)
                nc.vector.tensor_tensor(tiles_of(Y, i), n1[:, :, :], row_tiles(w["beta1"]), ALU.add).then_inc(yy_ok, 1)


def decoder_cross_attention(nc, d, Y, YT):
    with ExitStack() as ctx:
        def sb(name, shape, dt=F32):
            return ctx.enter_context(nc.sbuf_tensor("ca_" + name, shape, dt))

        own = []

        def sem(name):
            own.append(ctx.enter_context(nc.semaphore("ca_" + name)))
            return own[-1]

        ident = sb("ident", [P, P])
        C = sb("C", [P, 2, 2, KT, D])
        cT = sb("cT", [P, 2, 2, KT * P])
        yT = sb("yT", [P, 2, P])
        E = sb("E", [P, 2, KPAD])
        PT = sb("PT", [P, KT, P])
        mx, sums = sb("mx", [P, 2, 4]), sb("sums", [P, 2, 4])
        m, nb, tot, rs = (sb(n, [P, 2, 1]) for n in ("m", "nb", "tot", "rs"))
        psS = ctx.enter_context(nc.psum_tensor("ca_psS", [P, 4, 512], F32))
        psT = ctx.enter_context(nc.psum_tensor("ca_psT", [P, 2, 512], F32))
        psO = ctx.enter_context(nc.psum_tensor("ca_psO", [P, 512], F32))
        (w_in, y_ok, s_mm, mx_ok, m_ok, nb_ok, p_ok, t_mm, ta, td, o_mm, tot_ok, rs_ok, o_ok) = (sem(n) for n in (
            "w_in", "y_ok", "s_mm", "mx_ok", "m_ok", "nb_ok", "p_ok", "t_mm", "ta", "td", "o_mm", "tot_ok", "rs_ok",
            "o_ok"))
        c_in = [sem("c_in0"), sem("c_in1")]
        ctx.callback(clear, nc, own)
        block = ctx.enter_context(nc.Block())
        LAST = K - 12 * P
        GROUPS = 12

        def wait(eng, s, v):
            if not isinstance(v, int) or v > 0:
                eng.wait_ge(s, v)

        def tiles(eng, body):
            body(0, 0, False)
            body(1, 1, False)
            with eng.Fori(1, NT // 2 - 1) as i:
                body(i * 2, 0, False)
                body(i * 2 + 1, 1, False)
            body(NT - 2, 0, False)
            body(NT - 1, 1, True)

        def before(j, last=False):
            return 0 if isinstance(j, int) and j < 0 else j * GROUPS + (0 if last else 8)

        def copies(j, last_tile):
            return j * 6 + (6 if last_tile else 10)

        def transposed(k, u, nxt):
            n = 4 if k % 4 < 3 else 1
            cols = slice(512 * (k % 4), 512 * (k % 4) + n * P)
            if k < 8:
                width = n * P if n == 4 else LAST
                return psT[:, k % 2, 0:width], cT[:, nxt, k // 4, 512 * (k % 4):512 * (k % 4) + width]
            rows = P if n == 4 else LAST
            t = 4 * (k % 4)
            return (psT[0:rows, k % 2, 0:n * P].rearrange("p (t q) -> p t q", t=n), PT[0:rows, t:t + n, :])

        @block.sync
        def _(sp):
            sp.dma_start(ident[:, :], d["ident"]).then_inc(w_in, 16)

            def body(j, u, last):
                wait(sp, o_mm, j - 1)
                for b in range(2):
                    c = d["ctx"][bass.ds(j * 2 + b, 1), :, :].rearrange("o k d -> (o k) d")
                    sp.dma_start(C[:, u, b, 0:12, :], c[0:12 * P, :].rearrange("(p t) d -> p t d", t=12)).then_inc(c_in[u], 16)
                    sp.dma_start(C[0:LAST, u, b, 12, :], c[12 * P:K, :]).then_inc(c_in[u], 16)
            tiles(sp, body)

        @block.tensor
        def _(pe):
            def group(j, k, u, last=False):
                count = before(j, last) // 2 + k // 2
                wait(pe, (ta, td)[k % 2], count)
                for t in range(4 * (k % 4), min(4 * (k % 4) + 4, KT)):
                    n = P if t < 12 else LAST
                    s = t % 4 * P
                    if k < 8:
                        last = nc.tensor.transpose(psT[:, k % 2, s:s + n], C[0:n, 1 - u, k // 4, t, :], ident[0:n, 0:n])
                    else:
                        last = nc.tensor.transpose(psT[0:n, k % 2, s:s + P], E[:, u, t * P:t * P + n], ident[:, :])
                last.then_inc(t_mm, 1)

            pe.wait_ge(w_in, 16)
            pe.wait_ge(c_in[0], 64)
            for k in range(8):
                group(-1, k, 1)

            def body(j, u, last_tile):
                pe.wait_ge(y_ok, j + 1)
                wait(pe, ta, j * 6 + 4 if isinstance(j, int) and j == 0 else j * 6 + 2)
                wait(pe, td, j * 6 + 4 if isinstance(j, int) and j == 0 else j * 6 + 2)
                for n in range(4):
                    wait(pe, p_ok, 4 * j - 4 + n + 1)
                    k0, k1 = n * 400, min(n * 400 + 400, K) if n < 3 else K
                    for b in range(2):
                        last = nc.tensor.matmul(psS[S * b:S * b + S, n, 0:k1 - k0], yT[:, u, S * b:S * b + S],
                                                cT[:, u, b, k0:k1], start=True, stop=True)
                    last.then_inc(s_mm, 1)
                if not last_tile:
                    pe.wait_ge(c_in[1 - u], (j + 1) // 2 * 64 + 64)
                    for k in range(8):
                        group(j, k, u)
                pe.wait_ge(p_ok, 4 * j + 4)
                for k in range(8, 12):
                    group(j, k, u, last_tile)
                pe.wait_ge(ta, copies(j, last_tile))
                pe.wait_ge(td, copies(j, last_tile))
                wait(pe, o_ok, j)
                for t in range(KT):
                    n = P if t < 12 else LAST
                    for b in range(2):
                        last = nc.tensor.matmul(psO[S * b:S * b + S, 0:D], PT[0:n, t, S * b:S * b + S], C[0:n, u, b, t, :],
                                                start=(t == 0), stop=(t == KT - 1))
                last.then_inc(o_mm, 1)
            tiles(pe, body)

        @block.scalar
        def _(act):
            def copy(j, k, u, last=False):
                act.wait_ge(t_mm, before(j, last) + k + 1)
                src, dst = transposed(k, u, 1 - u)
                nc.scalar.activation(dst, src, ACT.Copy).then_inc(ta, 1)

            for k in range(0, 8, 2):
                copy(-1, k, 1)

            def body(j, u, last):
                if not last:
                    wait(act, s_mm, 4 * j)
                    for k in range(0, 8, 2):
                        copy(j, k, u)
                act.wait_ge(nb_ok, j + 1)
                wait(act, t_mm, (j - 1) * GROUPS + 8)
                for n in range(4):
                    k0, k1 = n * 400, n * 400 + 400 if n < 3 else K
                    nc.scalar.activation(E[:, u, k0:k1], psS[:, n, 0:k1 - k0], ACT.Exp, bias=nb[:, u, :], scale=SCALE1,
                                         accum_out=sums[:, u, n:n + 1]).then_inc(p_ok, 1)
                wait(act, o_mm, j)
                for k in (8, 10):
                    copy(j, k, u, last)
            tiles(act, body)

        @block.vector
        def _(dve):
            def queries(j, u):
                wait(dve, s_mm, 4 * (j - 1))
                ytile = YT[:, bass.ds(j * P, P)]
                nc.vector.tensor_tensor(yT[:, u, :], ytile, ytile, ALU.max).then_inc(y_ok, 1)

            def copy(j, k, u, last=False):
                dve.wait_ge(t_mm, before(j, last) + k + 1)
                src, dst = transposed(k, u, 1 - u)
                nc.vector.tensor_copy(dst, src).then_inc(td, 1)

            queries(0, 0)
            for k in range(1, 8, 2):
                copy(-1, k, 1)

            def body(j, u, last):
                if not last:
                    queries(j + 1, 1 - u)
                wait(dve, p_ok, 4 * (j - 1))
                for n in range(4):
                    k0, k1 = n * 400, n * 400 + 400 if n < 3 else K
                    dve.wait_ge(s_mm, 4 * j + n + 1)
                    nc.vector.reduce_max(mx[:, u, n:n + 1], psS[:, n, 0:k1 - k0], AX.X).then_inc(mx_ok, 1)
                dve.wait_ge(mx_ok, 4 * j + 4)
                nc.vector.reduce_max(m[:, u, :], mx[:, u, :], AX.X).then_inc(m_ok, 1)
                dve.wait_ge(m_ok, j + 1)
                nc.vector.tensor_scalar(nb[:, u, :], m[:, u, :], -SCALE1, None, ALU.mult).then_inc(nb_ok, 1)
                if not last:
                    for k in range(1, 8, 2):
                        copy(j, k, u)
                wait(dve, o_mm, j)
                for k in (9, 11):
                    copy(j, k, u, last)
                dve.wait_ge(p_ok, 4 * j + 4)
                nc.vector.reduce_sum(tot[:, u, :], sums[:, u, :], AX.X).then_inc(tot_ok, 1)
                dve.wait_ge(tot_ok, j + 1)
                nc.vector.reciprocal(rs[:, u, :], tot[:, u, :]).then_inc(rs_ok, 1)
                dve.wait_ge(rs_ok, j + 1)
                dve.wait_ge(o_mm, j + 1)
                yj = Y[:, bass.ds(j, 1), :].rearrange("p a b -> p (a b)")
                nc.vector.scalar_tensor_tensor(out=yj, in0=psO[:, 0:D], scalar=rs[:, u, :], in1=yj, op0=ALU.mult,
                                               op1=ALU.add).then_inc(o_ok, 1)
            tiles(dve, body)


def decoder_feed_forward(nc, d, X, Y):
    with ExitStack() as ctx:
        def sb(name, shape, dt=F32):
            return ctx.enter_context(nc.sbuf_tensor("ff_" + name, shape, dt))

        own = []

        def sem(name):
            own.append(ctx.enter_context(nc.semaphore("ff_" + name)))
            return own[-1]

        names = ("ident", "g2", "beta2", "g3", "beta3", "b2", "b1", "w1", "w2")
        w = {n: sb(n, list(d[n].shape)) for n in names}
        NF = 4
        ln2, ln3 = Norm(nc, sb, sem, "ln2"), Norm(nc, sb, sem, "ln3")
        n2, y2, y2b, y3p, n3 = (sb(n, [P, G, D]) for n in ("n2", "y2", "y2b", "y3p", "n3"))
        yT, hT = sb("yT", [P, GT]), sb("hT", [P, NF, GT])
        ps = ctx.enter_context(nc.psum_tensor("ff_ps", [P, 8, 512], F32))
        (w_in, n2_ok, m_ok, y2_ok, b_ok, tr_mm, yT_ok, h_mm, h_ok, f_mm, y3_ok, n3_ok, x_ok) = (sem(n) for n in (
            "w_in", "n2_ok", "m_ok", "y2_ok", "b_ok", "tr_mm", "yT_ok", "h_mm", "h_ok", "f_mm", "y3_ok", "n3_ok", "x_ok"))
        ctx.callback(clear, nc, own)
        block = ctx.enter_context(nc.Block())
        loaded = 16 * len(names)

        @block.sync
        def _(sp):
            load_all(nc, sp, [(w[n], d[n]) for n in names], w_in)

        @block.scalar
        def _(act):
            act.wait_ge(w_in, loaded)
            with act.Fori(0, NG) as i:
                ln2.spread(act, i)
                act.wait_ge(tr_mm, i + 1)
                nc.scalar.activation(yT[:, :], ps[:, 0, :], ACT.Copy).then_inc(yT_ok, 1)
                for f in range(NF):
                    act.wait_ge(h_mm, i * NF + f + 1)
                    nc.scalar.activation(hT[:, f, :], ps[:, 1 + f, :], ACT.Relu, bias=w["b1"][:, f:f + 1]).then_inc(h_ok, 1)
                ln3.spread(act, i)

        @block.tensor
        def _(pe):
            pe.wait_ge(w_in, loaded)
            with pe.Fori(0, NG) as i:
                pe.wait_ge(y2_ok, i + 1)
                for t in range(G):
                    last = nc.tensor.transpose(ps[:, 0, t * P:(t + 1) * P], y2[:, t, :], w["ident"][:, :])
                last.then_inc(tr_mm, 1)
                pe.wait_ge(yT_ok, i + 1)
                for f in range(NF):
                    nc.tensor.matmul(ps[:, 1 + f, :], w["w1"][:, f * P:(f + 1) * P], yT[:, :], start=True,
                                     stop=True).then_inc(h_mm, 1)
                pe.wait_ge(h_ok, i * NF + NF)
                for t in range(G):
                    for f in range(NF):
                        last = nc.tensor.matmul(ps[:, 5, t * P:(t + 1) * P], hT[:, f, t * P:(t + 1) * P], w["w2"][:, f, :],
                                                start=(f == 0), stop=(f == NF - 1))
                last.then_inc(f_mm, 1)

        @block.vector
        def _(dve):
            dve.wait_ge(w_in, loaded)
            with dve.Fori(0, NG) as i:
                yt = lambda t: Y[:, bass.ds(i * G + t, 1), :].rearrange("p a b -> p (a b)")
                ln2.moments(dve, i, yt)
                for t in range(G):
                    ln2.apply(n2[:, t, :], yt(t), t).then_inc(n2_ok, 1)
                dve.wait_ge(n2_ok, i * G + G)
                nc.vector.tensor_tensor(n2[:, :, :], n2[:, :, :], row_tiles(w["g2"]), ALU.mult).then_inc(m_ok, 1)
                dve.wait_ge(m_ok, i * 3 + 1)
                nc.vector.tensor_tensor(y2[:, :, :], n2[:, :, :], row_tiles(w["beta2"]), ALU.add).then_inc(y2_ok, 1)
                dve.wait_ge(y2_ok, i + 1)
                nc.vector.tensor_tensor(y2b[:, :, :], y2[:, :, :], row_tiles(w["b2"]), ALU.add).then_inc(b_ok, 1)
                dve.wait_ge(b_ok, i + 1)
                dve.wait_ge(f_mm, i + 1)
                nc.vector.tensor_tensor(y3p[:, :, :], ps[:, 5, :].rearrange("p (t d) -> p t d", t=G), y2b[:, :, :],
                                        ALU.add).then_inc(y3_ok, 1)
                dve.wait_ge(y3_ok, i + 1)
                ln3.moments(dve, i, lambda t: y3p[:, t, :])
                for t in range(G):
                    ln3.apply(n3[:, t, :], y3p[:, t, :], t).then_inc(n3_ok, 1)
                dve.wait_ge(n3_ok, i * G + G)
                nc.vector.tensor_tensor(n3[:, :, :], n3[:, :, :], row_tiles(w["g3"]), ALU.mult).then_inc(m_ok, 1)
                dve.wait_ge(m_ok, i * 3 + 2)
                nc.vector.tensor_tensor(n3[:, :, :], n3[:, :, :], row_tiles(w["beta3"]), ALU.add).then_inc(m_ok, 1)
                dve.wait_ge(m_ok, i * 3 + 3)
                nc.vector.tensor_tensor(tiles_of(X, i), n3[:, :, :], tiles_of(X, i), ALU.add).then_inc(x_ok, 1)
                dve.wait_ge(x_ok, i + 1)


def decoder_layer(nc, d, X):
    with ExitStack() as ctx:
        Y = ctx.enter_context(nc.sbuf_tensor("Y", [P, NT, D], F32))
        YT = ctx.enter_context(nc.sbuf_tensor("YT", [P, TOK], F32))
        decoder_self_attention(nc, d, X, Y, YT)
        decoder_cross_attention(nc, d, Y, YT)
        decoder_feed_forward(nc, d, X, Y)


def windowed_attention(nc, d, X):
    with ExitStack() as ctx:
        def sb(name, shape, dt=F32):
            return ctx.enter_context(nc.sbuf_tensor("wa_" + name, shape, dt))

        own = []

        def sem(name):
            own.append(ctx.enter_context(nc.semaphore("wa_" + name)))
            return own[-1]

        names = ("ident", "wq3", "wk3", "wv3", "wout", "window", "headmask")
        w = {n: sb(n, list(d[n].shape)) for n in names}
        ln = Norm(nc, sb, sem, "ln")
        xn = sb("xn", [P, G, D])
        xnT, qT, kT, oT = (sb(n, [P, GT]) for n in ("xnT", "qT", "kT", "oT"))
        Vb = sb("Vb", [P, 2 * G, NPAIR, 32])
        kbd = sb("kbd", [P, 2, 2, H, S])
        E = sb("E", [P, 2, H, S])
        PT = sb("PT", [P, NPAIR, P])
        mx, tot, rs = (sb(n, [P, 2, H]) for n in ("mx", "tot", "rs"))
        ps = ctx.enter_context(nc.psum_tensor("wa_ps", [P, 8, 512], F32))
        (w_in, zeroed, xn_ok, tr_mm, xnT_ok, qk_mm, q_ok, k_ok, v_mm, va_ok, kb0, kb1, s_mm, sm_ok, mx_ok, sub_ok, e_ok,
         tot_ok, rs_ok, en_ok, t_mm, pt_ok, o_mm, o_ok, out_mm, x_ok) = (sem(n) for n in (
            "w_in", "zeroed", "xn_ok", "tr_mm", "xnT_ok", "qk_mm", "q_ok", "k_ok", "v_mm", "va_ok", "kb0", "kb1", "s_mm",
            "sm_ok", "mx_ok", "sub_ok", "e_ok", "tot_ok", "rs_ok", "en_ok", "t_mm", "pt_ok", "o_mm", "o_ok", "out_mm",
            "x_ok"))
        ctx.callback(clear, nc, own)
        block = ctx.enter_context(nc.Block())
        loaded = 16 * len(names)
        heads = lambda a: a.unsqueeze(2).broadcast_to([P, H, S])

        def wait(eng, s, v):
            if not isinstance(v, int) or v > 0:
                eng.wait_ge(s, v)

        def groups(eng, body):
            body(0)
            with eng.Fori(1, NG) as i:
                body(i)

        @block.sync
        def _(sp):
            load_all(nc, sp, [(w[n], d[n]) for n in names], w_in)

        @block.gpsimd
        def _(pool):
            nc.gpsimd.memset(Vb[:, :, :, :], 0.0).then_inc(zeroed, 1)
            pool.wait_ge(w_in, loaded)

            def body(i):
                def diagonal(t):
                    wait(pool, s_mm, i * G + t - 1)
                    pool.wait_ge(k_ok, i + 1)
                    k = kT[:, t * P + S:t * P + P].unsqueeze(1).broadcast_to([P, H, S])
                    nc.gpsimd.tensor_tensor(kbd[:, t % 2, 1, :, :], heads(w["headmask"][:, :]), k, ALU.mult).then_inc(kb1, 1)
                diagonal(0)
                for t in range(G):
                    if t + 1 < G:
                        diagonal(t + 1)
                    pool.wait_ge(rs_ok, i * G + t + 1)
                    nc.gpsimd.tensor_tensor(E[:, t % 2, :, :], E[:, t % 2, :, :], heads(rs[:, t % 2, :]),
                                            ALU.mult).then_inc(en_ok, 1)
            groups(pool, body)

        @block.scalar
        def _(act):
            act.wait_ge(zeroed, 1)

            def body(i):
                ln.spread(act, i)
                act.wait_ge(tr_mm, i + 1)
                nc.scalar.activation(xnT[:, :], ps[:, 0, :], ACT.Copy).then_inc(xnT_ok, 1)
                act.wait_ge(v_mm, i + 1)
                wait(act, o_mm, i * G)
                v = ps[:, 3:5, :].rearrange("p a (b g c e) -> p (a b) g c e", b=4, g=4, e=16)
                vb = Vb[:, :, :, :].rearrange("p b (g c) e -> p b g c e", c=2)
                for hh in range(2):
                    r = slice(S * hh, S * hh + S)
                    for c in range(2):
                        at = 16 * c + 8 * hh
                        nc.scalar.activation(vb[r, :, :, c, at:at + DH], v[r, :, :, c, 8 * hh:8 * hh + DH],
                                             ACT.Copy).then_inc(va_ok, 1)
                for t in range(G):
                    act.wait_ge(sub_ok, i * G + t + 1)
                    nc.scalar.activation(E[:, t % 2, :, :], E[:, t % 2, :, :], ACT.Exp).then_inc(e_ok, 1)
                    if t > 0:
                        after(i, t - 1)
                after(i, G - 1)

            def after(i, t):
                act.wait_ge(t_mm, i * G + t + 1)
                wait(act, o_mm, i * G + t)
                nc.scalar.activation(PT[:, :, :], ps[:, 1:3, :].rearrange("p a (b q) -> p (a b) q", q=P),
                                     ACT.Copy).then_inc(pt_ok, 1)
                act.wait_ge(o_mm, i * G + t + 1)
                wait(act, out_mm, i)
                nc.scalar.activation(oT[:, t * P:(t + 1) * P], ps[:, 7, 0:P], ACT.Copy).then_inc(o_ok, 1)
            groups(act, body)

        @block.tensor
        def _(pe):
            pe.wait_ge(w_in, loaded)

            def body(i):
                wait(pe, x_ok, i)
                for t in range(G):
                    pe.wait_ge(xn_ok, i * G + t + 1)
                    last = nc.tensor.transpose(ps[:, 0, t * P:(t + 1) * P], xn[:, t, :], w["ident"][:, :])
                last.then_inc(tr_mm, 1)
                pe.wait_ge(xnT_ok, i + 1)
                wait(pe, pt_ok, i * G)
                nc.tensor.matmul(ps[:, 1, :], w["wq3"][:, :], xnT[:, :], start=True, stop=True).then_inc(qk_mm, 1)
                nc.tensor.matmul(ps[:, 2, :], w["wk3"][:, :], xnT[:, :], start=True, stop=True).then_inc(qk_mm, 1)
                wait(pe, va_ok, i * 4)
                for b in range(2 * G):
                    for half in range(2):
                        last = nc.tensor.matmul(ps[S * half:S * half + S, 3 + b // 4, b % 4 * P:(b % 4 + 1) * P],
                                                xnT[:, b * S:(b + 1) * S], w["wv3"][:, :], start=True, stop=True)
                last.then_inc(v_mm, 1)

                def scores(t):
                    pe.wait_ge(q_ok, i + 1)
                    pe.wait_ge(kb0, i * G + t + 1)
                    pe.wait_ge(kb1, i * G + t + 1)
                    wait(pe, sm_ok, i * G + t)
                    for k in range(2):
                        for b in range(2):
                            last = nc.tensor.matmul(ps[S * b:S * b + S, 5 + k, :], qT[:, t * P + S * b:t * P + S * b + S],
                                                    kbd[:, t % 2, b, 8 * k:8 * k + 8, :].rearrange("p h s -> p (h s)"),
                                                    start=True, stop=True)
                    last.then_inc(s_mm, 1)
                scores(0)
                for t in range(G):
                    if t + 1 < G:
                        scores(t + 1)
                    pe.wait_ge(en_ok, i * G + t + 1)
                    if t == 0:
                        pe.wait_ge(k_ok, i + 1)
                    else:
                        pe.wait_ge(pt_ok, i * G + t)
                    for p in range(NPAIR):
                        last = nc.tensor.transpose(ps[:, 1 + p // 4, p % 4 * P:(p % 4 + 1) * P],
                                                   E[:, t % 2, 2 * p:2 * p + 2, :].rearrange("p h s -> p (h s)"),
                                                   w["ident"][:, :])
                    last.then_inc(t_mm, 1)
                    pe.wait_ge(pt_ok, i * G + t + 1)
                    wait(pe, o_ok, i * G + t)
                    if t == 0:
                        pe.wait_ge(va_ok, i * 4 + 4)
                    for b in range(2):
                        for c in range(2):
                            for g in range(4):
                                p = 2 * g + c
                                last = nc.tensor.matmul(ps[32 * g:32 * g + 32, 7, S * b:S * b + S], Vb[:, 2 * t + b, p, :],
                                                        PT[:, p, S * b:S * b + S], start=(c == 0), stop=(c == 1))
                    last.then_inc(o_mm, 1)
                pe.wait_ge(o_ok, i * G + G)
                for t in range(G):
                    last = nc.tensor.matmul(ps[:, 0, t * P:(t + 1) * P], oT[:, t * P:(t + 1) * P], w["wout"][:, :],
                                            start=True, stop=True)
                last.then_inc(out_mm, 1)
            groups(pe, body)

        @block.vector
        def _(dve):
            dve.wait_ge(w_in, loaded)

            def body(i):
                xt = lambda t: X[:, bass.ds(i * G + t, 1), :].rearrange("p a b -> p (a b)")
                ln.moments(dve, i, xt)
                for t in range(G):
                    ln.apply(xn[:, t, :], xt(t), t).then_inc(xn_ok, 1)
                dve.wait_ge(qk_mm, i * 2 + 1)
                nc.vector.tensor_scalar(qT[:, :], ps[:, 1, :], QSCALE, None, ALU.mult).then_inc(q_ok, 1)
                dve.wait_ge(qk_mm, i * 2 + 2)
                nc.vector.tensor_copy(kT[:, :], ps[:, 2, :]).then_inc(k_ok, 1)
                dve.wait_ge(k_ok, i + 1)

                def diagonal(t):
                    wait(dve, s_mm, i * G + t - 1)
                    k = kT[:, t * P:t * P + S].unsqueeze(1).broadcast_to([P, H, S])
                    nc.vector.tensor_tensor(kbd[:, t % 2, 0, :, :], heads(w["headmask"][:, :]), k, ALU.mult).then_inc(kb0, 1)
                diagonal(0)
                for t in range(G):
                    u, n = t % 2, i * G + t
                    if t + 1 < G:
                        diagonal(t + 1)
                    dve.wait_ge(s_mm, n + 1)
                    wait(dve, t_mm, n - 1)
                    nc.vector.tensor_tensor(E[:, u, :, :], ps[:, 5:7, :].rearrange("p a (h s) -> p (a h) s", s=S),
                                            w["window"][:, :].unsqueeze(1).broadcast_to([P, H, S]), ALU.add).then_inc(sm_ok, 1)
                    dve.wait_ge(sm_ok, n + 1)
                    nc.vector.reduce_max(mx[:, u, :], E[:, u, :, :], AX.X).then_inc(mx_ok, 1)
                    dve.wait_ge(mx_ok, n + 1)
                    nc.vector.tensor_tensor(E[:, u, :, :], E[:, u, :, :], heads(mx[:, u, :]), ALU.subtract).then_inc(sub_ok, 1)
                    dve.wait_ge(e_ok, n + 1)
                    nc.vector.reduce_sum(tot[:, u, :], E[:, u, :, :], AX.X).then_inc(tot_ok, 1)
                    dve.wait_ge(tot_ok, n + 1)
                    nc.vector.reciprocal(rs[:, u, :], tot[:, u, :]).then_inc(rs_ok, 1)
                dve.wait_ge(out_mm, i + 1)
                nc.vector.tensor_tensor(tiles_of(X, i), ps[:, 0, :].rearrange("p (t d) -> p t d", t=G), tiles_of(X, i),
                                        ALU.add).then_inc(x_ok, 1)
                dve.wait_ge(x_ok, i + 1)
            groups(dve, body)


def second_experts(nc, d, X):
    with ExitStack() as ctx:
        def sb(name, shape, dt=F32):
            return ctx.enter_context(nc.sbuf_tensor("m2_" + name, shape, dt))

        own = []

        def sem(name):
            own.append(ctx.enter_context(nc.semaphore("m2_" + name)))
            return own[-1]

        names = ("ident", "gate2", "before8", "upto128", "ones")
        w = {n: sb(n, list(d[n].shape)) for n in names}
        ln = Norm(nc, sb, sem, "ln")
        xn = sb("xn", [P, 2, G, D])
        xnT = sb("xnT", [P, TOK])
        sc, mk, gtm, ties, pa, pb_ = (sb(n, [P, NT, E2]) for n in ("sc", "mk", "gtm", "ties", "pa", "pb"))
        wt = sb("wt", [P, NT, E2 + 1])
        mx, tot, rs, need = (sb(n, [P, NT]) for n in ("mx", "tot", "rs", "need"))
        gm, grank, kept = (sb(n, [P, NT, G2]) for n in ("gm", "grank", "kept"))
        gt, eq = sb("gt", [P, NT, G2, G2]), sb("eq", [P, NT, G2, G2])
        best = sb("best", [P, NT, 8])
        w13 = sb("w13", [P, 2, 2 * P])
        w2 = sb("w2", [P, 2, D])
        sl, h = sb("sl", [P, 2, GT]), sb("h", [P, 2, GT])
        ps = ctx.enter_context(nc.psum_tensor("m2_ps", [P, 8, 512], F32))
        w_in, xn_ok, tr_mm, xnT_ok, lg_mm, sub_ok, e_ok, rt, sel_ok, cum_mm, h_mm, sl_ok, h_ok, out_mm, x_ok = (
            sem(n) for n in ("w_in", "xn_ok", "tr_mm", "xnT_ok", "lg_mm", "sub_ok", "e_ok", "rt", "sel_ok", "cum_mm", "h_mm",
                             "sl_ok", "h_ok", "out_mm", "x_ok"))
        ex_in = [sem("ex_in0"), sem("ex_in1")]
        ctx.callback(clear, nc, own)
        block = ctx.enter_context(nc.Block())
        loaded = 16 * len(names)
        PAIRS = E2 // 2

        def wait(eng, s, v):
            if not isinstance(v, int) or v > 0:
                eng.wait_ge(s, v)

        def all_experts(eng, body):
            body(0, 8)
            with eng.Fori(1, PAIRS) as i:
                body(i, 8)
            body(PAIRS, 4)

        @block.sync
        def _(sp):
            load_all(nc, sp, [(w[n], d[n]) for n in names], w_in)

            def body(i, n):
                for u in range(n // 4):
                    wait(sp, out_mm, i * 8 + 4 * u - 4)
                    e = bass.ds(i * 2 + u, 1)
                    sp.dma_start(w13[:, u, :], d["w13"][e, :, :].rearrange("o p k -> (o p) k")).then_inc(ex_in[u], 16)
                    sp.dma_start(w2[:, u, :], d["w2e"][e, :, :].rearrange("o p k -> (o p) k")).then_inc(ex_in[u], 16)
            all_experts(sp, body)

        @block.scalar
        def _(act):
            for i in range(NG):
                ln.spread(act, i)
                act.wait_ge(tr_mm, i + 1)
                nc.scalar.activation(xnT[:, i * GT:(i + 1) * GT], ps[:, i % 2, :], ACT.Copy).then_inc(xnT_ok, 1)
            act.wait_ge(sub_ok, 1)
            nc.scalar.activation(sc[:, :, :], sc[:, :, :], ACT.Exp).then_inc(e_ok, 1)

            def body(i, n):
                for q in range(n):
                    m = i * 8 + q
                    act.wait_ge(h_mm, m * 2 + 1)
                    wait(act, h_ok, m - 1)
                    nc.scalar.activation(sl[:, q % 2, :], ps[:, 4 + (2 * q) % 4, :], ACT.Silu).then_inc(sl_ok, 1)
            all_experts(act, body)

        @block.tensor
        def _(pe):
            pe.wait_ge(w_in, loaded)
            for i in range(NG):
                if i >= 2:
                    pe.wait_ge(xnT_ok, i - 1)
                for t in range(G):
                    pe.wait_ge(xn_ok, i * G + t + 1)
                    last = nc.tensor.transpose(ps[:, i % 2, t * P:(t + 1) * P], xn[:, i % 2, t, :], w["ident"][:, :])
                last.then_inc(tr_mm, 1)
            pe.wait_ge(xnT_ok, NG)
            for t in range(NT):
                last = nc.tensor.matmul(ps[:, 2, t * E2:(t + 1) * E2], xnT[:, t * P:(t + 1) * P], w["gate2"][:, :],
                                        start=True, stop=True)
            last.then_inc(lg_mm, 1)

            def hidden(i, q):
                u, c = q // 4 % 2, q % 4
                if c == 0:
                    pe.wait_ge(ex_in[u], i * 32 + (32 if q < 8 else 64))
                wait(pe, h_ok, i * 8 + q - 1)
                for k in range(2):
                    nc.tensor.matmul(ps[:, 4 + (2 * q + k) % 4, :], w13[:, u, k * P:(k + 1) * P],
                                     xnT[:, c * GT:(c + 1) * GT], start=True, stop=True).then_inc(h_mm, 1)

            hidden(0, 0)
            pe.wait_ge(sel_ok, 1)
            sel = gtm[:, :, :].rearrange("p t e -> p (t e)")
            nc.tensor.matmul(ps[:, 0, :], w["upto128"][:, :], sel, start=True, stop=True).then_inc(cum_mm, 1)
            nc.tensor.matmul(ps[:, 1, :], w["ones"][:, :], sel, start=True, stop=True).then_inc(cum_mm, 1)

            def body(i, n):
                for q in range(n):
                    m = i * 8 + q
                    if n == 8 or q < n - 1:
                        hidden(i, q + 1)
                    pe.wait_ge(h_ok, m + 1)
                    wait(pe, x_ok, m * 4 - 4)
                    for t in range(G):
                        last = nc.tensor.matmul(ps[:, 2 + q % 2, t * P:(t + 1) * P], h[:, q % 2, t * P:(t + 1) * P],
                                                w2[:, q // 4, :], start=True, stop=True)
                    last.then_inc(out_mm, 1)
            all_experts(pe, body)

        @block.vector
        def _(dve):
            v = nc.vector
            steps = [0]

            def then(instruction):
                steps[0] += 1
                instruction.then_inc(rt, 1)
                dve.wait_ge(rt, steps[0])

            for i in range(NG):
                ln.moments(dve, i, lambda t: X[:, i * G + t, :])
                if i >= 2:
                    dve.wait_ge(tr_mm, i - 1)
                for t in range(G):
                    ln.apply(xn[:, i % 2, t, :], X[:, i * G + t, :], t).then_inc(xn_ok, 1)
            dve.wait_ge(w_in, loaded)
            each = lambda a, n: a.unsqueeze(2).broadcast_to([P, NT, n])
            dve.wait_ge(lg_mm, 1)
            logits = ps[:, 2, :].rearrange("p (t e) -> p t e", e=E2)
            then(v.reduce_max(mx[:, :], logits, AX.X))
            v.tensor_tensor(sc[:, :, :], logits, each(mx[:, :], E2), ALU.subtract).then_inc(sub_ok, 1)
            dve.wait_ge(e_ok, 1)
            then(v.reduce_sum(tot[:, :], sc[:, :, :], AX.X))
            then(v.reciprocal(rs[:, :], tot[:, :]))
            then(v.tensor_tensor(sc[:, :, :], sc[:, :, :], each(rs[:, :], E2), ALU.mult))
            then(v.reduce_max(gm[:, :, :], sc[:, :, :].rearrange("p t (g e) -> p t g e", g=G2), AX.X))
            square = [P, NT, G2, G2]
            other, own = gm[:, :, :].unsqueeze(2).broadcast_to(square), gm[:, :, :].unsqueeze(3).broadcast_to(square)
            then(v.tensor_tensor(gt[:, :, :, :], other, own, ALU.is_gt))
            then(v.tensor_tensor(eq[:, :, :, :], other, own, ALU.is_equal))
            then(v.tensor_tensor(eq[:, :, :, :], eq[:, :, :, :], w["before8"][:, :, :].unsqueeze(1).broadcast_to(square),
                                 ALU.mult))
            then(v.tensor_tensor(gt[:, :, :, :], gt[:, :, :, :], eq[:, :, :, :], ALU.add))
            then(v.reduce_sum(grank[:, :, :], gt[:, :, :, :], AX.X))
            then(v.tensor_scalar(kept[:, :, :], grank[:, :, :], float(LG2), None, ALU.is_lt))
            in_groups = lambda a: a[:, :, :].rearrange("p t (g e) -> p t g e", g=G2)
            kept4 = kept[:, :, :].unsqueeze(3).broadcast_to([P, NT, G2, E2 // G2])
            then(v.tensor_tensor(in_groups(mk), in_groups(sc), kept4, ALU.mult))
            then(v.tensor_scalar(kept[:, :, :], kept[:, :, :], 1.0, None, ALU.subtract))
            then(v.tensor_tensor(in_groups(mk), in_groups(mk), kept4, ALU.add))
            for t in range(NT):
                last = v.max(best[:, t, :], mk[:, t, :])
                last.then_inc(rt, 1)
                steps[0] += 1
            dve.wait_ge(rt, steps[0])
            fourth = best[:, :, TOP2 - 1:TOP2].broadcast_to([P, NT, E2])
            then(v.tensor_tensor(gtm[:, :, :], mk[:, :, :], fourth, ALU.is_gt))
            then(v.tensor_tensor(ties[:, :, :], mk[:, :, :], fourth, ALU.is_equal))
            then(v.reduce_sum(tot[:, :], gtm[:, :, :], AX.X))
            then(v.tensor_scalar(need[:, :], tot[:, :], -1.0, float(TOP2), ALU.mult, ALU.add))
            src, dst, k = ties, pa, 1
            while k < E2:
                then(v.tensor_copy(dst[:, :, 0:k], src[:, :, 0:k]))
                then(v.tensor_tensor(dst[:, :, k:E2], src[:, :, k:E2], src[:, :, 0:E2 - k], ALU.add))
                src, dst, k = dst, (pb_ if dst is pa else pa), 2 * k
            then(v.tensor_tensor(dst[:, :, :], src[:, :, :], each(need[:, :], E2), ALU.is_le))
            then(v.tensor_tensor(dst[:, :, :], dst[:, :, :], ties[:, :, :], ALU.mult))
            v.tensor_tensor(gtm[:, :, :], gtm[:, :, :], dst[:, :, :], ALU.add).then_inc(sel_ok, 1)
            dve.wait_ge(sel_ok, 1)
            then(v.tensor_tensor(mk[:, :, :], sc[:, :, :], gtm[:, :, :], ALU.mult))
            then(v.reduce_sum(tot[:, :], mk[:, :, :], AX.X))
            then(v.tensor_scalar(tot[:, :], tot[:, :], 1e-9, None, ALU.add))
            then(v.reciprocal(rs[:, :], tot[:, :]))
            then(v.tensor_tensor(mk[:, :, :], mk[:, :, :], each(rs[:, :], E2), ALU.mult))
            dve.wait_ge(cum_mm, 2)
            then(v.memset(pa[:, 0:1, :], 0.0))
            then(v.tensor_copy(pa[:, 1:NT, :], ps[:, 1, 0:(NT - 1) * E2].rearrange("p (t e) -> p t e", e=E2)))
            src, dst, k = pa, pb_, 1
            while k < NT:
                then(v.tensor_copy(dst[:, 0:k, :], src[:, 0:k, :]))
                then(v.tensor_tensor(dst[:, k:NT, :], src[:, k:NT, :], src[:, 0:NT - k, :], ALU.add))
                src, dst, k = dst, (pb_ if dst is pa else pa), 2 * k
            then(v.tensor_tensor(dst[:, :, :], ps[:, 0, :].rearrange("p (t e) -> p t e", e=E2), src[:, :, :], ALU.add))
            then(v.scalar_tensor_tensor(out=wt[:, :, 0:E2], in0=dst[:, :, :], scalar=float(CAP), in1=mk[:, :, :],
                                        op0=ALU.is_le, op1=ALU.mult))
            then(v.memset(wt[:, :, E2:E2 + 1], 1.0))

            def gated(i, q):
                m = i * 8 + q
                dve.wait_ge(sl_ok, m + 1)
                dve.wait_ge(h_mm, m * 2 + 2)
                wait(dve, out_mm, m - 1)
                v.tensor_tensor(h[:, q % 2, :], ps[:, 4 + (2 * q + 1) % 4, :], sl[:, q % 2, :], ALU.mult).then_inc(h_ok, 1)

            gated(0, 0)

            def body(i, n):
                for q in range(n):
                    m = i * 8 + q
                    if n == 8 or q < n - 1:
                        gated(i, q + 1)
                    dve.wait_ge(out_mm, m + 1)
                    wait(dve, x_ok, m * 4 - 12)
                    for t in range(G):
                        x = X[:, G * (q % 4) + t, :]
                        we = wt[:, G * (q % 4) + t, bass.ds(i * 2 + q // 4, 1)]
                        v.scalar_tensor_tensor(out=x, in0=ps[:, 2 + q % 2, t * P:(t + 1) * P], scalar=we, in1=x,
                                               op0=ALU.mult, op1=ALU.add).then_inc(x_ok, 1)
            all_experts(dve, body)


def load_x(nc, d, X):
    with ExitStack() as ctx:
        x_in = ctx.enter_context(nc.semaphore("x_in"))
        block = ctx.enter_context(nc.Block())

        @block.sync
        def _(sp):
            sp.dma_start(X[:, :, :], d["x"].rearrange("(t p) d -> p t d", p=P)).then_inc(x_in, 16)
            sp.wait_ge(x_in, 16)


def build(nc, d, out):
    with ExitStack() as ctx:
        X = ctx.enter_context(nc.sbuf_tensor("X", [P, NT, D], F32))
        first_cross_attention(nc, d, X)
        linear_attention(nc, d, X)
        first_experts(nc, d, X)
        decoder_layer(nc, d, X)
        windowed_attention(nc, d, X)
        second_experts(nc, d, X)
        stored = ctx.enter_context(nc.semaphore("stored"))
        block = ctx.enter_context(nc.Block())

        @block.sync
        def _(sp):
            sp.dma_start(out.rearrange("(t p) d -> p t d", p=P), X[:, :, :]).then_inc(stored, 16)
            sp.wait_ge(stored, 16)


def layouts(i):
    import numpy as np
    a = {k: np.asarray(v) for k, v in i.items()}
    f = np.float32
    g = {"x": a["x"].reshape(TOK, D), "ctxT": a["ctx_1024"].transpose(0, 2, 1)}
    flat = lambda w: w.transpose(1, 0, 2).reshape(D, D)
    g["wq"], g["wv"] = flat(a["L0_xattn_Wq"]), flat(a["L0_xattn_Wv"])
    g["wkT"] = flat(a["L0_xattn_Wk"]).T
    g["wp"] = a["L0_xattn_Wp"]
    for n in ("bq", "bk", "bv"):
        g[n] = a["L0_xattn_" + n].reshape(P, 1)
    g["bp_rows"] = np.broadcast_to(a["L0_xattn_bp"], (P, D))
    rows = np.zeros((4, 32, 2, 2, D), f)
    w = a["L0_xattn_Wp"].reshape(2, 4, 2, DH, D)
    for h in range(2):
        rows[:, DH * h:DH * h + DH, :, h, :] = w[:, :, h].transpose(1, 2, 0, 3)
    g["wp_rows"] = rows.reshape(P, 2, 2, D)
    g["ident"] = np.eye(P, dtype=f)
    r = np.arange(P)
    g["headmask"] = (r[:, None] // DH == np.arange(H)[None]).astype(f)
    g["densel"] = ((r[:, None] % 32 == 16) & (r[:, None] // 32 == r[None] // 32)).astype(f)
    for n in ("q", "k", "g", "v", "o"):
        g["w" + n + "2"] = a["L0_attn_W" + n]
    g["wa"] = a["L0_attn_Wa"]
    g["dtb"], g["alog"] = np.broadcast_to(a["L0_attn_dt_bias"], (P, H)), np.broadcast_to(a["L0_attn_A_log"], (P, H))
    g["rmsw"] = np.tile(a["L0_attn_rms_w"], H).reshape(P, 1)
    s = np.arange(S)
    g["upto"] = (r[:, None] % S <= s[None]).astype(f)
    g["after"] = ((r[:, None] // S == r[None] // S) & (r[:, None] > r[None])).astype(f)
    g["hlmask"] = (r[:, None] // DH % 4 == np.arange(4)[None]).astype(f)
    g["blockones"] = (r[:, None] // DH == r[None] // DH).astype(f)
    g["gate1"] = a["L0_ffn_gate_w"].T
    g["ebias"] = np.broadcast_to(a["L0_ffn_expert_bias"], (P, E1))
    e = np.arange(E1)
    g["before8"] = np.broadcast_to((e[None] < e[:, None]).astype(f), (P, E1, E1))
    g["up1"] = a["L0_ffn_w_up"].transpose(0, 2, 1)
    g["down1"] = a["L0_ffn_w_down"].transpose(0, 2, 1).reshape(E1, 2, P, D).transpose(0, 2, 1, 3)
    for n in ("g1", "g2", "g3", "beta1", "beta2", "beta3", "b2"):
        g[n] = np.broadcast_to(a["L1_xattn_" + n], (P, D))
    g["w1"] = a["L1_xattn_w1"]
    g["b1"] = a["L1_xattn_b1"].reshape(4, P).T
    g["w2"] = a["L1_xattn_w2"].reshape(4, P, D).transpose(1, 0, 2)
    g["ctx"] = a["ctx_1024"]
    allowed = (r[:, None] // S == r[None] // S) & (r[None] <= r[:, None])
    g["causal2"] = np.where(allowed, 0, NEVER).astype(f)
    for n, c in zip("qkv", range(3)):
        g["w" + n + "3"] = a["L1_attn_W_qkv"][:, c * D:(c + 1) * D]
    g["wout"] = a["L1_attn_W_out"]
    i, j = r[:, None] % S, s[None]
    g["window"] = np.where((j <= i) & (j > i - WINDOW), 0, NEVER).astype(f)
    g["gate2"] = a["L1_ffn_wg"].T
    both = lambda n, s: np.concatenate([a["L1_ffn_" + n], a["L1_ffn_" + s][None]])
    g["w13"] = np.concatenate([both("w1", "sw1"), both("w3", "sw3")], axis=2)
    g["w2e"] = both("w2", "sw2")
    g["upto128"] = (r[:, None] <= r[None]).astype(f)
    g["ones"] = np.ones((P, P), f)
    return {k: np.ascontiguousarray(v) for k, v in g.items()}


def kernel(**inputs):
    import concourse.bacc as bacc
    from concourse.bass_utils import run_bass_kernel_spmd
    nc = bacc.Bacc("TRN2", target_bir_lowering=False, num_devices=1)
    arrays = layouts(inputs)
    d = {n: nc.dram_tensor("in_" + n, v.shape, mybir.dt.from_np(v.dtype), kind="ExternalInput").ap()
         for n, v in arrays.items()}
    out = nc.dram_tensor("out", (TOK, D), F32, kind="ExternalOutput").ap()
    build(nc, d, out)
    r = run_bass_kernel_spmd(nc, [{"in_" + n: v for n, v in arrays.items()}], core_ids=[0])
    return r.results[0]["out"].reshape(B, S, D)
```

```python
from contextlib import ExitStack

import concourse.bass as bass
from concourse import mybir

ALU = mybir.AluOpType
ACT = mybir.ActivationFunctionType
AX = mybir.AxisListType
F32 = mybir.dt.float32
F32R = mybir.dt.float32r

P = 128
B, S, D = 32, 64, 128
TOK = B * S
NT = TOK // P
H, DH = 16, 8
NPAIR = H // 2
K = 1601
KPAD = K + 1
KT = (K + P - 1) // P
BANKS = [(0, 400), (400, 800), (800, 1200), (1200, KPAD)]
QSCALE = DH ** -0.5
EPS = 1e-5
SCALE1 = D ** -0.5
NEVER = -1e30
WINDOW = 32
E1, TOP1 = 8, 2
E2, TOP2, G2, LG2 = 32, 4, 8, 4
CAP = max(1, int(1.25 * TOK * TOP2 / E2))


def clear(nc, semaphores):
    with nc.Block() as block:
        @block.sync
        def _(sp):
            for s in semaphores:
                sp.sem_clear(s)
def first_cross_attention(nc, d, X):
    with ExitStack() as ctx:
        def sb(name, shape, dt=F32):
            return ctx.enter_context(nc.sbuf_tensor(name, shape, dt))

        own = []

        def sem(name):
            own.append(ctx.enter_context(nc.semaphore(name)))
            return own[-1]

        qT = sb("qT", [P, TOK])
        cq = sb("cq", [P, B, NPAIR])
        bvp = sb("bvp", [P, D])
        headmask = sb("headmask", [P, H])
        wkT = sb("wkT", [P, D])
        wv = sb("wv", [P, D])
        ident = sb("ident", [P, P])
        densel = sb("densel", [P, P])
        wp_rows = sb("wp_rows", [P, 2, 2, D])
        raw = sb("ctx_raw", [P, 2, KPAD])
        chi = sb("ctx_hi", [P, 2, KPAD], F32R)
        clo = sb("ctx_lo", [P, 2, KPAD], F32R)
        V = sb("V", [P, 2, KT, NPAIR, 32])
        ctx_in = [sem("ctx_in0"), sem("ctx_in1")]
        chi_done, split_done = sem("chi_done"), sem("split_done")

        with ExitStack() as c0:
            def sb0(name, shape, dt=F32):
                return c0.enter_context(nc.sbuf_tensor(name, shape, dt))

            own0 = []

            def sem0(name):
                own0.append(c0.enter_context(nc.semaphore(name)))
                return own0[-1]

            xn = sb0("xn", [P, NT, D])
            xnT = sb0("xnT", [P, TOK])
            stats = sb0("stats", [P, NT, 6])
            mv = sb0("mv", [P, NT, 2])
            std = sb0("std", [P, NT])
            rstd = sb0("rstd", [P, NT])
            wq = sb0("wq", [P, D])
            wp = sb0("wp", [P, D])
            bq = sb0("bq", [P, 1])
            bk = sb0("bk", [P, 1])
            bv = sb0("bv", [P, 1])
            bp_rows = sb0("bp_rows", [P, D])
            bksel = sb0("bksel", [P, H])
            ps = c0.enter_context(nc.psum_tensor("ps_q", [P, 8, 512], F32))
            x_in, w_in = sem0("x_in"), sem0("w_in")
            zeroed = sem0("zeroed")
            stat, aggr, vare, root, inv = (sem0(n) for n in ("stat", "aggr", "vare", "root", "inv"))
            xn_ok, tr_ok, xnT_ok, q_mm, q_ok = (sem0(n) for n in ("xn_ok", "tr_ok", "xnT_ok", "q_mm", "q_ok"))
            sel_ok, c_mm, c_ok, v_mm0, bvp_ok, xres = (sem0(n) for n in ("sel_ok", "c_mm", "c_ok", "v_mm0", "bvp_ok", "xres"))
            loads = [(wq, d["wq"]), (wp, d["wp"]), (bq, d["bq"]), (bk, d["bk"]), (bv, d["bv"]),
                     (bp_rows, d["bp_rows"]), (headmask, d["headmask"]), (wkT, d["wkT"]), (wv, d["wv"]),
                     (ident, d["ident"]), (densel, d["densel"])]
            c0.callback(clear, nc, own0)
            block = c0.enter_context(nc.Block())

            @block.sync
            def _(sp):
                sp.dma_start(X[:, :, :], d["x"].rearrange("(t p) d -> p t d", p=P)).then_inc(x_in, 16)
                for dst, src in loads:
                    sp.dma_start(dst[:, :], src).then_inc(w_in, 16)
                sp.dma_start(wp_rows[:, :, :, :], d["wp_rows"]).then_inc(w_in, 16)
                for b in range(2):
                    sp.dma_start(raw[:, b, 0:K], d["ctxT"][b, :, :]).then_inc(ctx_in[b], 16)

            all_loads = 16 * (len(loads) + 1)

            @block.gpsimd
            def _(pool):
                nc.gpsimd.memset(V[:, :, :, :, :], 0.0).then_inc(zeroed, 1)
                nc.gpsimd.memset(raw[:, :, K:KPAD], 0.0).then_inc(zeroed, 1)
                pool.wait_ge(zeroed, 2)
                nc.gpsimd.memset(V[:, :, :, :, 16:17], 1.0).then_inc(zeroed, 1)
                pool.wait_ge(zeroed, 3)
                for b in range(2):
                    pool.wait_ge(ctx_in[b], 16)
                    nc.gpsimd.tensor_copy(chi[:, b, :], raw[:, b, :]).then_inc(chi_done, 1)
                    pool.wait_ge(chi_done, b + 1)
                    nc.gpsimd.tensor_tensor(clo[:, b, :], raw[:, b, :], chi[:, b, :].bitcast(F32),
                                            ALU.subtract).then_inc(split_done, 1)

            @block.vector
            def _(dve):
                dve.wait_ge(x_in, 16)
                for t in range(NT):
                    nc.vector.bn_stats(stats[:, t, :], X[:, t, :]).then_inc(stat, 1)
                dve.wait_ge(stat, NT)
                for t in range(NT):
                    nc.vector.bn_aggr(mv[:, t, :], stats[:, t, :]).then_inc(aggr, 1)
                dve.wait_ge(aggr, NT)
                nc.vector.tensor_scalar_add(std[:, :], mv[:, :, 1], EPS).then_inc(vare, 1)
                dve.wait_ge(root, 1)
                nc.vector.reciprocal(rstd[:, :], std[:, :]).then_inc(inv, 1)
                dve.wait_ge(inv, 1)
                for t in range(NT):
                    nc.vector.tensor_scalar(xn[:, t, :], X[:, t, :], mv[:, t, 0:1], rstd[:, t:t + 1],
                                            ALU.subtract, ALU.mult).then_inc(xn_ok, 1)
                dve.wait_ge(w_in, all_loads)
                nc.vector.tensor_scalar(bksel[:, :], headmask[:, :], bk[:, :], None, ALU.mult).then_inc(sel_ok, 1)
                for k in range(4):
                    dve.wait_ge(tr_ok, k + 1)
                    nc.vector.tensor_copy(xnT[:, k * 512:(k + 1) * 512], ps[:, k, :]).then_inc(xnT_ok, 1)
                for k in range(4):
                    dve.wait_ge(q_mm, k + 1)
                    nc.vector.tensor_scalar(qT[:, k * 512:(k + 1) * 512], ps[:, 4 + k, :], bq[:, :], QSCALE,
                                            ALU.add, ALU.mult).then_inc(q_ok, 1)
                dve.wait_ge(c_mm, 1)
                cps = ps[:, 0, :].rearrange("p (b j h) -> p b j h", b=B, h=2)
                nc.vector.tensor_copy(cq[0:64, :, :], cps[0:64, :, :, 0]).then_inc(c_ok, 1)
                nc.vector.tensor_copy(cq[64:128, :, :], cps[64:128, :, :, 1]).then_inc(c_ok, 1)
                dve.wait_ge(v_mm0, 1)
                nc.vector.tensor_tensor(bvp[:, :], ps[:, 1, 0:D], bp_rows[:, :], ALU.add).then_inc(bvp_ok, 1)
                dve.wait_ge(bvp_ok, 1)
                nc.vector.tensor_tensor(X[:, :, :], X[:, :, :], bvp[:, :].unsqueeze(1).broadcast_to([P, NT, D]),
                                        ALU.add).then_inc(xres, 1)

            @block.scalar
            def _(act):
                act.wait_ge(vare, 1)
                nc.scalar.activation(std[:, :], std[:, :], ACT.Sqrt).then_inc(root, 1)

            @block.tensor
            def _(pe):
                pe.wait_ge(w_in, all_loads)
                for t in range(NT):
                    pe.wait_ge(xn_ok, t + 1)
                    last = nc.tensor.transpose(ps[:, t // 4, (t % 4) * P:(t % 4 + 1) * P], xn[:, t, :], ident[:, :])
                    if t % 4 == 3:
                        last.then_inc(tr_ok, 1)
                for k in range(4):
                    pe.wait_ge(xnT_ok, k + 1)
                    nc.tensor.matmul(ps[:, 4 + k, :], wq[:, :], xnT[:, k * 512:(k + 1) * 512],
                                     start=True, stop=True).then_inc(q_mm, 1)
                pe.wait_ge(q_ok, 4)
                pe.wait_ge(sel_ok, 1)
                for b in range(B):
                    for h in range(2):
                        last = nc.tensor.matmul(ps[S * h:S * h + S, 0, b * H:(b + 1) * H], qT[:, b * S:(b + 1) * S],
                                                bksel[:, :], start=True, stop=True)
                last.then_inc(c_mm, 1)
                nc.tensor.matmul(ps[:, 1, 0:D], bv[:, :].broadcast_to([P, P]), wp[:, :],
                                 start=True, stop=True).then_inc(v_mm0, 1)

        qbd = sb("qbd", [P, 2, H, S])
        qraw = sb("q_raw", [P, H * S])
        qhi = sb("q_hi", [P, 2, H * S], F32R)
        qlo = sb("q_lo", [P, 2, H * S], F32R)
        E = sb("E", [P, 2, KPAD])
        PT = sb("PT", [P, 2, 4, KT, P])
        mx = sb("mx", [P, 2, 4])
        m = sb("m", [P, 2, 1])
        nb = sb("nb", [P, 2, 1])
        O = sb("O", [P, 2, 2, P])
        rden = sb("rden", [P, 2, P])
        On = sb("On", [P, 2, P])
        psS = ctx.enter_context(nc.psum_tensor("psS", [P, 4, 512], F32))
        psT = ctx.enter_context(nc.psum_tensor("psT", [P, 2, 512], F32))
        psM = ctx.enter_context(nc.psum_tensor("psM", [P, 512], F32))
        psO = ctx.enter_context(nc.psum_tensor("psO", [P, 512], F32))
        qhi_done, qbd_done = sem("qhi_done"), sem("qbd_done")
        qt_mm, qr_done, ql_done = sem("qt_mm"), sem("qr_done"), sem("ql_done")
        v_mm, v_done = sem("v_mm"), sem("v_done")
        s_mm, max_done, m_done, nb_done, exp_done = (sem(n) for n in ("s_mm", "max_done", "m_done", "nb_done", "exp_done"))
        t_mm, ta_done, td_done = sem("t_mm"), sem("ta_done"), sem("td_done")
        pv_mm, o_done = sem("pv_mm"), sem("o_done")
        den_mm, rec_done, on_done, fin_mm, x_done = (sem(n) for n in ("den_mm", "rec_done", "on_done", "fin_mm", "x_done"))
        VGROUPS = [range(0, 4), range(4, 8), range(12, 13), range(8, 12)]
        CH = [range(0, 4), range(4, 7), range(7, 10), range(10, 13)]
        ctx.callback(clear, nc, own)
        block = ctx.enter_context(nc.Block())

        def wait(eng, s, v):
            if not isinstance(v, int) or v > 0:
                eng.wait_ge(s, v)

        def known(b):
            return isinstance(b, int)

        def batches(eng, batch):
            batch(0, 0)
            batch(1, 1)
            with eng.Fori(1, B // 2 - 1) as i:
                batch(i * 2, 0)
                batch(i * 2 + 1, 1)
            for b in range(B - 2, B + 2):
                batch(b, b % 2)

        @block.sync
        def _(sp):
            def load(b, par):
                wait(sp, v_mm, (b - 1) * 4)
                wait(sp, split_done, b - 1)
                sp.dma_start(raw[:, par, 0:K], d["ctxT"][b, :, :] if known(b) else
                             d["ctxT"][bass.ds(b, 1), :, :].rearrange("o p k -> (o p) k")).then_inc(ctx_in[par], 16)
            load(2, 0)
            load(3, 1)
            with sp.Fori(2, B // 2) as i:
                load(i * 2, 0)
                load(i * 2 + 1, 1)

        @block.gpsimd
        def _(pool):
            def queries(b, par):
                wait(pool, qt_mm, 2 * (b - 1))
                q = qT[:, bass.ds(b * S, S)].unsqueeze(1).broadcast_to([P, H, S])
                nc.gpsimd.tensor_tensor(qbd[:, par, :, :], headmask[:, :].unsqueeze(2).broadcast_to([P, H, S]), q,
                                        ALU.mult).then_inc(qbd_done, 1)

            def prepare(b, par, after):
                wait(pool, s_mm, 32 * (b - 1))
                pool.wait_ge(ctx_in[par], 16 * (b // 2 + 1))
                pool.wait_ge(qr_done, 2 * b + 2)
                if after and not (known(b) and b == 0):
                    queries(b + 1, 1 - par)
                nc.gpsimd.tensor_copy(qhi[:, par, :], qraw[:, :]).then_inc(qhi_done, 1)
                later = not known(b) or b >= 2
                if later:
                    nc.gpsimd.tensor_copy(chi[:, par, :], raw[:, par, :]).then_inc(chi_done, 1)
                    pool.wait_ge(chi_done, b + 1)
                pool.wait_ge(qhi_done, b + 1)
                nc.gpsimd.tensor_tensor(qlo[:, par, :], qraw[:, :], qhi[:, par, :].bitcast(F32),
                                        ALU.subtract).then_inc(ql_done, 1)
                if later:
                    nc.gpsimd.tensor_tensor(clo[:, par, :], raw[:, par, :], chi[:, par, :].bitcast(F32),
                                            ALU.subtract).then_inc(split_done, 1)
                if known(b) and b == 0:
                    queries(1, 1)
            queries(0, 0)
            prepare(0, 0, True)
            prepare(1, 1, True)
            with pool.Fori(1, B // 2 - 1) as i:
                prepare(i * 2, 0, True)
                prepare(i * 2 + 1, 1, True)
            prepare(B - 2, 0, True)
            prepare(B - 1, 1, False)

        @block.tensor
        def _(pe):
            def project_q(b, par, half):
                wait(pe, qbd_done, b + 1)
                nc.tensor.matmul(psM[:, :], wkT[:, :],
                                 qbd[:, par, 8 * half:8 * half + 8, :].rearrange("p h s -> p (h s)"),
                                 start=True, stop=True).then_inc(qt_mm, 1)

            def values(b, par, k):
                if k == 0:
                    pe.wait_ge(ctx_in[par], 16 * (b // 2 + 1))
                for t in VGROUPS[k]:
                    n = min(P, K - t * P)
                    last = nc.tensor.matmul(psM[0:n, (t % 4) * P:(t % 4 + 1) * P], raw[:, par, t * P:t * P + n],
                                            wv[:, :], start=True, stop=True)
                last.then_inc(v_mm, 1)

            def scores(b, par, p, between):
                g = b * NPAIR + p
                wait(pe, ql_done, b + 1)
                if p == 0:
                    wait(pe, split_done, b + 1)
                qs = slice(p * P, (p + 1) * P)
                for n, (k0, k1) in enumerate(BANKS):
                    wait(pe, exp_done, 4 * g - 4 + n + 1)
                    for i, (q, c) in enumerate(((qhi, chi), (qhi, clo), (qlo, chi))):
                        last = nc.tensor.matmul(psS[:, n, 0:k1 - k0], q[:, par, qs], c[:, par, k0:k1],
                                                start=(i == 0), stop=(i == 2))
                    last.then_inc(s_mm, 1)
                    if n == 1:
                        between(0)
                between(1)
                between(2)

            def transposes(g, ep, k):
                wait(pe, exp_done, 4 * g + min(k + 2, 4))
                if k < 2:
                    wait(pe, td_done, 2 * g - 1 + k)
                else:
                    wait(pe, ta_done, 2 * g + k - 1)
                for t in range(4 * k, min(4 * k + 4, KT)):
                    n = min(P, K - t * P)
                    last = nc.tensor.transpose(psT[0:n, k % 2, (t % 4) * P:(t % 4 + 1) * P],
                                               E[:, ep, t * P:t * P + n], ident[:, :])
                last.then_inc(t_mm, 1)

            def weigh_values(q, qpar, vpar, half, chunk):
                if chunk == 0:
                    wait(pe, ta_done, 8 * q + 8)
                    wait(pe, td_done, 8 * q + 8)
                    wait(pe, o_done, q)
                for t in CH[chunk]:
                    n = min(P, K - t * P)
                    for r in range(4):
                        last = nc.tensor.matmul(psO[32 * r:32 * r + 32, 0:P], V[0:n, vpar, t, 4 * half + r, :],
                                                PT[0:n, qpar, r, t, :], start=(t == 0), stop=(t == KT - 1))
                if chunk == 3:
                    last.then_inc(pv_mm, 1)

            def sums(b, par):
                wait(pe, o_done, 2 * b + 2)
                wait(pe, x_done, b)
                wait(pe, v_done, 4 * (b + 2) if not known(b) or b + 2 < B else 4 * B)
                nc.tensor.matmul(psM[:, 0:2 * P], densel[:, :], O[:, par, :, :].rearrange("p a b -> p (a b)"),
                                 start=True, stop=True).then_inc(den_mm, 1)

            def output(b, par):
                wait(pe, on_done, b + 1)
                wait(pe, v_done, 4 * (b + 3) + 2 if not known(b) or b + 3 < B else 4 * B)
                for i in range(4):
                    a, h = i // 2, i % 2
                    last = nc.tensor.matmul(psM[64 * par:64 * par + 64, 3 * P:4 * P], On[:, a, h * S:(h + 1) * S],
                                            wp_rows[:, a, h, :], start=(i == 0), stop=(i == 3))
                last.then_inc(fin_mm, 1)

            def batch(b, par):
                for p in range(NPAIR):
                    live = not known(b) or b < B
                    behind = (p > 0 and live) or (p == 0 and (not known(b) or 0 < b <= B))

                    def turn(k):
                        if behind:
                            transposes(b * NPAIR + p - 1, (p - 1) % 2, k)
                    if live:
                        scores(b, par, p, turn)
                    else:
                        for k in range(3):
                            turn(k)
                    if p == 0 and (not known(b) or 0 < b <= B):
                        weigh_values(2 * b - 2, 0, 1 - par, 0, 3)
                    if 1 <= p <= 4 and (not known(b) or 0 < b <= B):
                        if p == 1:
                            wait(pe, v_done, 4 * b)
                        weigh_values(2 * b - 1, 1, 1 - par, 1, p - 1)
                    if p >= 5 and live:
                        if p == 5:
                            wait(pe, v_done, 4 * b + 4)
                        weigh_values(2 * b, 0, par, 0, p - 5)
                    turn(3)
                    if p == 0 and (not known(b) or b >= 2):
                        sums(b - 2, par)
                    nxt = not known(b) or b + 1 < B
                    if nxt and p in (2, 3):
                        if p == 2:
                            wait(pe, rec_done, b - 1)
                        wait(pe, qr_done, 2 * (b + 1) + p - 2)
                        project_q(b + 1, 1 - par, p - 2)
                    if p == 6 and (not known(b) or b >= 2):
                        output(b - 2, par)
                    if nxt and p >= 4:
                        if p == 4:
                            wait(pe, qr_done, 2 * (b + 2))
                        if p == 7:
                            wait(pe, x_done, b - 1)
                        wait(pe, v_done, 4 * (b + 1) + p - 4)
                        values(b + 1, 1 - par, p - 4)
            for half in range(2):
                wait(pe, qr_done, half)
                project_q(0, 0, half)
            wait(pe, qr_done, 2)
            for k in range(4):
                wait(pe, v_done, k)
                values(0, 0, k)
            batches(pe, batch)

        @block.scalar
        def _(act):
            def q_part(b, half):
                act.wait_ge(qt_mm, 2 * b + half + 1)
                wait(act, ql_done, b)
                nc.scalar.activation(qraw[:, half * 512:(half + 1) * 512], psM[:, :], ACT.Copy).then_inc(qr_done, 1)

            def v_part(b, par, k):
                act.wait_ge(v_mm, 4 * b + k + 1)
                wait(act, pv_mm, 2 * b - 2)
                t0, n = VGROUPS[k].start, len(VGROUPS[k])
                rows = P if n == 4 else K - 12 * P
                nc.scalar.activation(V[0:rows, par, t0:t0 + n, :, 0:16],
                                     psM[0:rows, 0:n * P].rearrange("p (t j c) -> p t j c", t=n, c=16),
                                     ACT.Copy).then_inc(v_done, 1)

            def tiles(g, q, r, qpar):
                wait(act, pv_mm, q - 1)
                for k in (0, 1):
                    act.wait_ge(t_mm, 4 * g + k + 1)
                    nc.scalar.activation(PT[:, qpar, r, 4 * k:4 * k + 4, :],
                                         psT[:, k, :].rearrange("p (t c) -> p t c", t=4), ACT.Copy).then_inc(ta_done, 1)

            def exps(g, ep):
                wait(act, t_mm, 4 * (g - 1))
                act.wait_ge(nb_done, g + 1)
                for n, (k0, k1) in enumerate(BANKS):
                    k1 = min(k1, K)
                    nc.scalar.activation(E[:, ep, k0:k1], psS[:, n, 0:k1 - k0], ACT.Exp,
                                         bias=nb[:, ep, :]).then_inc(exp_done, 1)

            def batch(b, par):
                for p in range(NPAIR):
                    live = not known(b) or b < B
                    if p > 0 and live:
                        tiles(b * NPAIR + p - 1, 2 * b + (p - 1) // 4, (p - 1) % 4, (p - 1) // 4)
                    elif p == 0 and (not known(b) or 0 < b <= B):
                        tiles(b * NPAIR - 1, 2 * b - 1, 3, 1)
                    if live:
                        exps(b * NPAIR + p, p % 2)
                    nxt = not known(b) or b + 1 < B
                    if nxt and p in (2, 3):
                        q_part(b + 1, p - 2)
                    if nxt and p >= 4:
                        v_part(b + 1, 1 - par, p - 4)

            q_part(0, 0)
            q_part(0, 1)
            for k in range(4):
                v_part(0, 0, k)
            batches(act, batch)

        @block.vector
        def _(dve):
            def maxima(b, g, p, ep):
                wait(dve, exp_done, 4 * (g - 1))
                for n, (k0, k1) in enumerate(BANKS):
                    k1 = min(k1, K)
                    dve.wait_ge(s_mm, 4 * g + n + 1)
                    nc.vector.reduce_max(mx[:, ep, n:n + 1], psS[:, n, 0:k1 - k0], AX.X).then_inc(max_done, 1)
                dve.wait_ge(max_done, 4 * g + 4)
                nc.vector.reduce_max(m[:, ep, :], mx[:, ep, :], AX.X).then_inc(m_done, 1)
                dve.wait_ge(m_done, g + 1)
                c = cq[:, bass.ds(b, 1), p:p + 1].rearrange("p a b -> p (a b)") if not known(b) else cq[:, b, p:p + 1]
                nc.vector.scalar_tensor_tensor(out=nb[:, ep, :], in0=m[:, ep, :], scalar=c, in1=c, op0=ALU.add,
                                               op1=ALU.subtract, reverse1=True).then_inc(nb_done, 1)

            def tiles(g, q, r, qpar):
                wait(dve, pv_mm, q - 1)
                for k in (2, 3):
                    dve.wait_ge(t_mm, 4 * g + k + 1)
                    n = 4 if k == 2 else 1
                    rows = P if k == 2 else K - 12 * P
                    nc.vector.tensor_copy(PT[0:rows, qpar, r, 4 * k:4 * k + n, :],
                                          psT[0:rows, k - 2, 0:n * P].rearrange("p (t c) -> p t c", t=n)).then_inc(td_done, 1)

            def take_sums(q, par, half):
                dve.wait_ge(pv_mm, q + 1)
                nc.vector.tensor_copy(O[:, par, half, :], psO[:, 0:P]).then_inc(o_done, 1)

            def normalise(b, par):
                dve.wait_ge(den_mm, b + 1)
                wait(dve, fin_mm, b)
                nc.vector.reciprocal(rden[:, :, :], psM[:, 0:2 * P].rearrange("p (a b) -> p a b", a=2)).then_inc(rec_done, 1)
                dve.wait_ge(rec_done, b + 1)
                nc.vector.tensor_tensor(On[:, :, :], O[:, par, :, :], rden[:, :, :], ALU.mult).then_inc(on_done, 1)

            def residual(b, par):
                dve.wait_ge(fin_mm, b + 1)
                dve.wait_ge(v_done, 4 * (b + 3) + 3 if not known(b) or b + 3 < B else 4 * B)
                r = slice(64 * par, 64 * par + 64)
                x = X[r, b // 2, :] if known(b) else X[r, bass.ds(b // 2, 1), :].rearrange("p a b -> p (a b)")
                nc.vector.tensor_tensor(x, psM[r, 3 * P:4 * P], x, ALU.add).then_inc(x_done, 1)

            def batch(b, par):
                for p in range(NPAIR):
                    live = not known(b) or b < B
                    after = not known(b) or 0 < b <= B
                    if live:
                        maxima(b, b * NPAIR + p, p, p % 2)
                    if not known(b) or b >= 2:
                        if p == 1:
                            normalise(b - 2, par)
                        if p == 7:
                            residual(b - 2, par)
                    if p > 0 and live:
                        tiles(b * NPAIR + p - 1, 2 * b + (p - 1) // 4, (p - 1) % 4, (p - 1) // 4)
                    elif p == 0 and after:
                        tiles(b * NPAIR - 1, 2 * b - 1, 3, 1)
                    if p == 0 and after:
                        take_sums(2 * b - 2, 1 - par, 0)
                    if p == 4 and after:
                        take_sums(2 * b - 1, 1 - par, 1)

            batches(dve, batch)


G = 4
NG = NT // G
GT = G * P


def tiles_of(X, i):
    return X[:, bass.ds(i * G, G), :]


def load_all(nc, sp, pairs, sem):
    for dst, src in pairs:
        sp.dma_start(dst[tuple(slice(None) for _ in dst.shape)], src).then_inc(sem, 16)
    return 16 * len(pairs)


class Norm:

    def __init__(self, nc, sb, sem, name):
        self.nc = nc
        self.stats, self.mv = sb(name + "_stats", [P, G, 6]), sb(name + "_mv", [P, G, 2])
        self.var, self.rstd, self.power = (sb(name + n, [P, G]) for n in ("_var", "_rstd", "_power"))
        self.stat, self.aggr, self.vare = sem(name + "_stat"), sem(name + "_aggr"), sem(name + "_vare")
        self.inv, self.cleared, self.power_set = sem(name + "_inv"), sem(name + "_cleared"), sem(name + "_power_set")

    def prepare(self, pool):
        self.nc.gpsimd.memset(self.power[:, :], -0.5).then_inc(self.power_set, 1)
        pool.wait_ge(self.power_set, 1)

    def root(self, pool, i):
        pool.wait_ge(self.vare, i + 1)
        self.nc.gpsimd.tensor_tensor(self.rstd[:, :], self.var[:, :], self.power[:, :], ALU.pow).then_inc(self.inv, 1)

    def moments(self, dve, i, x):
        v = self.nc.vector
        for t in range(G):
            v.bn_stats(self.stats[:, t, :], x(t)).then_inc(self.stat, 1)
        dve.wait_ge(self.stat, i * G + G)
        v.memset(self.var[:, :], 0.0).then_inc(self.cleared, 1)
        for t in range(G):
            v.bn_aggr(self.mv[:, t, :], self.stats[:, t, :]).then_inc(self.aggr, 1)
        dve.wait_ge(self.aggr, i * G + G)
        v.tensor_scalar(self.var[:, :], self.mv[:, :, 1], EPS, None, ALU.add).then_inc(self.vare, 1)
        dve.wait_ge(self.inv, i + 1)

    def apply(self, out, x, t):
        return self.nc.vector.tensor_scalar(out, x, self.mv[:, t, 0:1], self.rstd[:, t:t + 1],
                                            ALU.subtract, ALU.mult)


def linear_attention(nc, d, X):
    with ExitStack() as ctx:
        def sb(name, shape, dt=F32):
            return ctx.enter_context(nc.sbuf_tensor("la_" + name, shape, dt))

        names = ("rmsw", "wo2", "upto", "after", "hlmask", "headmask", "blockones", "halves")
        w = {n: sb(n, list(d[n].shape)) for n in names}
        qk = sb("qk", [P, 2, TOK])
        v = sb("v", [P, NT, D])
        gate = sb("gate", [P, TOK])
        la = sb("la", [P, NT, H])
        oT = sb("oT", [P, TOK])
        linear_attention_project(nc, d, X, w, names, qk, v, gate, la)
        linear_attention_tiles(nc, w, qk, v, gate, la, oT)
        linear_attention_output(nc, X, w, gate, oT)


def linear_attention_project(nc, d, X, shared, shared_names, qk, v, gate, la):
    with ExitStack() as ctx:
        def sb(name, shape, dt=F32):
            return ctx.enter_context(nc.sbuf_tensor("lp_" + name, shape, dt))

        own = []

        def sem(name):
            own.append(ctx.enter_context(nc.semaphore("lp_" + name)))
            return own[-1]

        names = ("ident", "wq2", "wk2", "wg2", "wv2", "wa", "dtb", "alog")
        w = {n: sb(n, list(d[n].shape)) for n in names}
        nega = sb("nega", [P, H])
        ln = Norm(nc, sb, sem, "ln")
        xn = sb("xn", [P, 2, G, D])
        xnT = sb("xnT", [P, 2, GT])
        sq = sb("sq", [P, 2, GT])
        nrm = sb("nrm", [P, 2, G, H])
        rq = sb("rq", [P, G, D])
        rqT = sb("rqT", [P, GT])
        z, nz, low, t1 = (sb(n, [P, NT, H]) for n in ("z", "nz", "low", "t1"))
        ps = ctx.enter_context(nc.psum_tensor("lp_ps", [P, 8, 512], F32))
        (w_in, mx_ok, neg_ok, neg2_ok, xn_ok, tr_mm, xnT_ok, qk_mm, g_mm, v_mm, a_mm, sq_ok, k_ok, v_ok, gate_ok, ss_mm,
         ss_ok, nrm_ok, rq_ok, rt_mm, rt_ok, q_ok, z_ok, e_ok, sp_ok, la_ok) = (sem(n) for n in (
            "w_in", "mx_ok", "neg_ok", "neg2_ok", "xn_ok", "tr_mm", "xnT_ok", "qk_mm", "g_mm", "v_mm", "a_mm", "sq_ok",
            "k_ok", "v_ok", "gate_ok", "ss_mm", "ss_ok", "nrm_ok", "rq_ok", "rt_mm", "rt_ok", "q_ok", "z_ok", "e_ok",
            "sp_ok", "la_ok"))
        ctx.callback(clear, nc, own)
        block = ctx.enter_context(nc.Block())
        loads = [(w[n], d[n]) for n in names] + [(shared[n], d[n]) for n in shared_names]
        loaded = 16 * len(loads)

        @block.sync
        def _(sp):
            load_all(nc, sp, loads, w_in)

        @block.gpsimd
        def _(pool):
            ln.prepare(pool)
            for i in range(NG):
                ln.root(pool, i)

        @block.scalar
        def _(act):
            for i in range(NG):
                act.wait_ge(tr_mm, i + 1)
                if i >= 2:
                    act.wait_ge(v_mm, i - 1)
                nc.scalar.activation(xnT[:, i % 2, :], ps[:, 0, :], ACT.Copy).then_inc(xnT_ok, 1)
                for k in range(2):
                    act.wait_ge(qk_mm, i * 2 + k + 1)
                    if i > 0:
                        act.wait_ge(ss_mm, i)
                    nc.scalar.activation(sq[:, k, :], ps[:, 1 + k, :], ACT.Square).then_inc(sq_ok, 1)
                nc.scalar.activation(qk[:, 1, i * GT:(i + 1) * GT], ps[:, 2, :], ACT.Copy).then_inc(k_ok, 1)
                act.wait_ge(g_mm, i + 1)
                nc.scalar.activation(gate[:, i * GT:(i + 1) * GT], ps[:, 3, :], ACT.Copy).then_inc(gate_ok, 1)
                act.wait_ge(ss_mm, i + 1)
                if i > 0:
                    act.wait_ge(v_ok, i)
                nc.scalar.activation(nrm[:, :, :, :], ps[:, 6, 0:2 * G * H].rearrange("p (k t h) -> p k t h", k=2, t=G),
                                     ACT.Sqrt).then_inc(ss_ok, 1)
                act.wait_ge(rt_mm, i + 1)
                if i > 0:
                    act.wait_ge(q_ok, i)
                nc.scalar.activation(rqT[:, :], ps[:, 7, :], ACT.Copy).then_inc(rt_ok, 1)
            nc.scalar.activation(nega[:, :], w["alog"][:, :], ACT.Exp).then_inc(neg_ok, 1)
            act.wait_ge(z_ok, 3)
            nc.scalar.activation(low[:, :, :], nz[:, :, :], ACT.Exp).then_inc(e_ok, 1)
            act.wait_ge(e_ok, 1)
            nc.scalar.activation(nz[:, :, :], low[:, :, :], ACT.Ln, bias=1.0).then_inc(e_ok, 1)
            act.wait_ge(sp_ok, 2)
            nc.scalar.activation(low[:, :, :], t1[:, :, :], ACT.Exp).then_inc(e_ok, 1)
            act.wait_ge(e_ok, 3)
            nc.scalar.activation(nz[:, :, :], low[:, :, :], ACT.Copy, bias=1e-8).then_inc(e_ok, 1)
            act.wait_ge(e_ok, 4)
            nc.scalar.activation(la[:, :, :], nz[:, :, :], ACT.Ln).then_inc(la_ok, 1)

        @block.tensor
        def _(pe):
            def transposes(i):
                if i > 0:
                    pe.wait_ge(xnT_ok, i)
                for t in range(G):
                    pe.wait_ge(xn_ok, i * G + t + 1)
                    last = nc.tensor.transpose(ps[:, 0, t * P:(t + 1) * P], xn[:, i % 2, t, :], w["ident"][:, :])
                last.then_inc(tr_mm, 1)

            pe.wait_ge(w_in, loaded)
            transposes(0)
            for i in range(NG):
                pe.wait_ge(xnT_ok, i + 1)
                for k, n in enumerate(("wq2", "wk2")):
                    if i > 0:
                        pe.wait_ge((q_ok, k_ok)[k], i)
                    nc.tensor.matmul(ps[:, 1 + k, :], w[n][:, :], xnT[:, i % 2, :], start=True, stop=True).then_inc(qk_mm, 1)
                if i > 0:
                    pe.wait_ge(gate_ok, i)
                nc.tensor.matmul(ps[:, 3, :], w["wg2"][:, :], xnT[:, i % 2, :], start=True, stop=True).then_inc(g_mm, 1)
                for t in range(G):
                    last = nc.tensor.matmul(ps[:, 5, (i * G + t) * H:(i * G + t + 1) * H], xnT[:, i % 2, t * P:(t + 1) * P],
                                            w["wa"][:, :], start=True, stop=True)
                last.then_inc(a_mm, 1)
                if i > 0:
                    pe.wait_ge(v_ok, i)
                for t in range(G):
                    last = nc.tensor.matmul(ps[:, 4, t * P:(t + 1) * P], xnT[:, i % 2, t * P:(t + 1) * P], w["wv2"][:, :],
                                            start=True, stop=True)
                last.then_inc(v_mm, 1)
                pe.wait_ge(sq_ok, i * 2 + 2)
                if i > 0:
                    pe.wait_ge(ss_ok, i)
                for k in range(2):
                    for t in range(G):
                        c = (k * G + t) * H
                        last = nc.tensor.matmul(ps[:, 6, c:c + H], sq[:, k, t * P:(t + 1) * P], shared["headmask"][:, :],
                                                start=True, stop=True)
                last.then_inc(ss_mm, 1)
                if i + 1 < NG:
                    transposes(i + 1)
                pe.wait_ge(rq_ok, i + 1)
                if i > 0:
                    pe.wait_ge(rt_ok, i)
                for t in range(G):
                    last = nc.tensor.transpose(ps[:, 7, t * P:(t + 1) * P], rq[:, t, :], w["ident"][:, :])
                last.then_inc(rt_mm, 1)

        @block.vector
        def _(dve):
            def tokens(i):
                ln.moments(dve, i, lambda t: X[:, i * G + t, :])
                if i >= 2:
                    dve.wait_ge(tr_mm, i - 1)
                for t in range(G):
                    ln.apply(xn[:, i % 2, t, :], X[:, i * G + t, :], t).then_inc(xn_ok, 1)

            tokens(0)
            for i in range(NG):
                if i + 1 < NG:
                    tokens(i + 1)
                dve.wait_ge(ss_ok, i + 1)
                nc.vector.tensor_scalar(nrm[:, :, :, :], nrm[:, :, :, :], 1e-12, None, ALU.max).then_inc(mx_ok, 1)
                dve.wait_ge(mx_ok, i + 1)
                nc.vector.reciprocal(nrm[:, :, :, :], nrm[:, :, :, :]).then_inc(nrm_ok, 1)
                dve.wait_ge(nrm_ok, i + 1)
                features = lambda a: a.unsqueeze(3).broadcast_to([P, G, H, DH])
                by_head = lambda a: a.rearrange("p t (h e) -> p t h e", h=H)
                if i > 0:
                    dve.wait_ge(rt_mm, i)
                nc.vector.tensor_copy(by_head(rq[:, :, :]), features(nrm[:, 0, :, :])).then_inc(rq_ok, 1)
                dve.wait_ge(v_mm, i + 1)
                nc.vector.tensor_tensor(by_head(v[:, i * G:(i + 1) * G, :]),
                                        ps[:, 4, :].rearrange("p (t h e) -> p t h e", t=G, h=H),
                                        features(nrm[:, 1, :, :]), ALU.mult).then_inc(v_ok, 1)
                dve.wait_ge(rt_ok, i + 1)
                nc.vector.tensor_tensor(qk[:, 0, i * GT:(i + 1) * GT], ps[:, 1, :], rqT[:, :], ALU.mult).then_inc(q_ok, 1)
            hb = lambda a: a[:, :].unsqueeze(1).broadcast_to([P, NT, H])
            dve.wait_ge(a_mm, NG)
            nc.vector.tensor_tensor(z[:, :, :], ps[:, 5, 0:NT * H].rearrange("p (t h) -> p t h", t=NT), hb(w["dtb"]),
                                    ALU.add).then_inc(z_ok, 1)
            dve.wait_ge(z_ok, 1)
            nc.vector.tensor_scalar(low[:, :, :], z[:, :, :], -1.0, None, ALU.mult).then_inc(z_ok, 1)
            dve.wait_ge(z_ok, 2)
            nc.vector.tensor_tensor(nz[:, :, :], z[:, :, :], low[:, :, :], ALU.min).then_inc(z_ok, 1)
            dve.wait_ge(neg_ok, 1)
            nc.vector.tensor_scalar(nega[:, :], nega[:, :], -1.0, None, ALU.mult).then_inc(neg2_ok, 1)
            dve.wait_ge(e_ok, 2)
            nc.vector.scalar_tensor_tensor(out=z[:, :, :], in0=z[:, :, :], scalar=0.0, in1=nz[:, :, :], op0=ALU.max,
                                           op1=ALU.add).then_inc(sp_ok, 1)
            dve.wait_ge(sp_ok, 1)
            dve.wait_ge(neg2_ok, 1)
            nc.vector.tensor_tensor(t1[:, :, :], z[:, :, :], hb(nega), ALU.mult).then_inc(sp_ok, 1)


def linear_attention_tiles(nc, w, qk, v, gate, la, oT):
    with ExitStack() as ctx:
        def sb(name, shape, dt=F32):
            return ctx.enter_context(nc.sbuf_tensor("lt_" + name, shape, dt))

        own = []

        def sem(name):
            own.append(ctx.enter_context(nc.semaphore("lt_" + name)))
            return own[-1]

        LM = sb("LM", [P, 2, H, S])
        qbd = sb("qbd", [P, 2, 2, H, S])
        keys = sb("keys", [P, 2, P])
        values = sb("values", [P, 2, 2, D])
        Ex = sb("Ex", [P, 2, H, S])
        ST = sb("ST", [P, 2, H, S])
        mo = sb("mo", [P, 2, 2, 4, S])
        psD = ctx.enter_context(nc.psum_tensor("lt_psD", [P, 2, 2, 512], F32))
        psS = ctx.enter_context(nc.psum_tensor("lt_psS", [P, 2, 512], F32))
        psO = ctx.enter_context(nc.psum_tensor("lt_psO", [P, 2, 512], F32))
        (gate_ok, lm_ok, qb0, qb1, keys_ok, values_ok, d_mm, ex_ok, exm_ok, s_mm, st_ok, o_mm, mo_ok, oT_ok) = (sem(n) for n in (
            "gate_ok", "lm_ok", "qb0", "qb1", "keys_ok", "values_ok", "d_mm", "ex_ok", "exm_ok", "s_mm", "st_ok", "o_mm", "mo_ok",
            "oT_ok"))
        ctx.callback(clear, nc, own)
        block = ctx.enter_context(nc.Block())
        one_tile = lambda a: a.rearrange("p a b -> p (a b)")

        def wait(eng, s, n):
            if not isinstance(n, int) or n > 0:
                eng.wait_ge(s, n)

        def steps(eng, step):
            step(0, 0, 2)
            step(1, 1, 2)
            with eng.Fori(1, NT // 2 - 1) as i:
                step(i * 2, 0, 2)
                step(i * 2 + 1, 1, 2)
            step(NT - 2, 0, 1)
            step(NT - 1, 1, 0)

        def block_diagonal(engine, T, u, b, done):
            q = qk[:, 0, bass.ds(T * P + b * S, S)].unsqueeze(1).broadcast_to([P, H, S])
            engine.tensor_tensor(qbd[:, u, b, :, :], w["headmask"][:, :].unsqueeze(2).broadcast_to([P, H, S]), q,
                                 ALU.mult).then_inc(done, 1)

        @block.gpsimd
        def _(pool):
            def prepare(T, u):
                wait(pool, s_mm, T - 1)
                block_diagonal(nc.gpsimd, T, u, 1, qb1)
                wait(pool, o_mm, T - 1)
                nc.gpsimd.tensor_tensor(values[:, u, :, :], v[:, bass.ds(T, 1), :].broadcast_to([P, 2, D]),
                                        w["halves"][:, :].unsqueeze(2).broadcast_to([P, 2, D]), ALU.mult).then_inc(values_ok, 1)
                pool.wait_ge(ex_ok, T + 1)
                nc.gpsimd.tensor_tensor(Ex[:, u, :, :], Ex[:, u, :, :], w["upto"][:, :].unsqueeze(1).broadcast_to([P, H, S]),
                                        ALU.mult).then_inc(exm_ok, 1)
            prepare(0, 0)

            def step(T, u, more):
                if more:
                    prepare(T + 1, 1 - u)
            steps(pool, step)

        @block.scalar
        def _(act):
            def decays(T, u):
                act.wait_ge(d_mm, T + 1)
                wait(act, st_ok, T - 1)
                nc.scalar.activation(Ex[:, u, :, :], psD[:, u, :, :].rearrange("p a (h s) -> p (a h) s", s=S),
                                     ACT.Exp).then_inc(ex_ok, 1)
            decays(0, 0)

            def step(T, u, more):
                if more:
                    decays(T + 1, 1 - u)
            steps(act, step)
            nc.scalar.activation(gate[:, :], gate[:, :], ACT.Silu).then_inc(gate_ok, 1)

        @block.tensor
        def _(pe):
            def decays(T, u):
                pe.wait_ge(lm_ok, T + 1)
                wait(pe, ex_ok, T - 1)
                for k in range(2):
                    last = nc.tensor.matmul(psD[:, u, k, :], w["after"][:, :],
                                            LM[:, u, 8 * k:8 * k + 8, :].rearrange("p h s -> p (h s)"), start=True, stop=True)
                last.then_inc(d_mm, 1)
            decays(0, 0)

            def step(T, u, more):
                pe.wait_ge(keys_ok, T + 1)
                pe.wait_ge(qb0, T + 1)
                pe.wait_ge(qb1, T + 1)
                wait(pe, st_ok, T)
                for k in range(2):
                    for b in range(2):
                        last = nc.tensor.matmul(psS[S * b:S * b + S, k, :], keys[:, u, S * b:S * b + S],
                                                qbd[:, u, b, 8 * k:8 * k + 8, :].rearrange("p h s -> p (h s)"),
                                                start=True, stop=True)
                last.then_inc(s_mm, 1)
                if more:
                    decays(T + 1, 1 - u)
                pe.wait_ge(st_ok, T + 1)
                pe.wait_ge(values_ok, T + 1)
                wait(pe, mo_ok, T - 1)
                for b in range(2):
                    for g in range(4):
                        last = nc.tensor.matmul(psO[32 * g:32 * g + 32, u, 4 * S * b:4 * S * (b + 1)],
                                                values[:, u, b, 32 * g:32 * g + 32],
                                                ST[:, u, 4 * g:4 * g + 4, :].rearrange("p h s -> p (h s)"),
                                                start=True, stop=True)
                last.then_inc(o_mm, 1)
            steps(pe, step)

        @block.vector
        def _(dve):
            def logs(T, u):
                wait(dve, d_mm, T - 1)
                nc.vector.tensor_tensor(LM[:, u, :, :], one_tile(la[:, bass.ds(T, 1), :]).unsqueeze(2).broadcast_to([P, H, S]),
                                        w["upto"][:, :].unsqueeze(1).broadcast_to([P, H, S]), ALU.mult).then_inc(lm_ok, 1)

            def operands(T, u):
                wait(dve, s_mm, T - 1)
                block_diagonal(nc.vector, T, u, 0, qb0)
                k = qk[:, 1, bass.ds(T * P, P)]
                nc.vector.tensor_tensor(keys[:, u, :], k, k, ALU.max).then_inc(keys_ok, 1)

            logs(0, 0)
            operands(0, 0)
            logs(1, 1)

            def step(T, u, more):
                dve.wait_ge(exm_ok, T + 1)
                dve.wait_ge(s_mm, T + 1)
                wait(dve, o_mm, T - 1)
                nc.vector.tensor_tensor(ST[:, u, :, :], psS[:, :, :].rearrange("p a (h s) -> p (a h) s", s=S),
                                        Ex[:, u, :, :], ALU.mult).then_inc(st_ok, 1)
                if more:
                    operands(T + 1, 1 - u)
                if more > 1:
                    logs(T + 2, u)
                dve.wait_ge(o_mm, T + 1)
                nc.vector.tensor_tensor(mo[:, u, :, :, :], psO[:, u, :].rearrange("p (b h s) -> p b h s", b=2, s=S),
                                        w["hlmask"][:, :].unsqueeze(1).unsqueeze(3).broadcast_to([P, 2, 4, S]),
                                        ALU.mult).then_inc(mo_ok, 1)
                dve.wait_ge(mo_ok, T + 1)
                nc.vector.reduce_sum(oT[:, bass.ds(T * P, P)].rearrange("p (b s) -> p b s", s=S),
                                     mo[:, u, :, :, :].rearrange("p b h s -> p b s h"), AX.X).then_inc(oT_ok, 1)
            steps(dve, step)


def linear_attention_output(nc, X, w, gate, oT):
    with ExitStack() as ctx:
        def sb(name, shape, dt=F32):
            return ctx.enter_context(nc.sbuf_tensor("lo_" + name, shape, dt))

        own = []

        def sem(name):
            own.append(ctx.enter_context(nc.semaphore("lo_" + name)))
            return own[-1]

        sq, ms, rms, on, y = (sb(n, [P, 2, GT]) for n in ("sq", "ms", "rms", "on", "y"))
        ps = ctx.enter_context(nc.psum_tensor("lo_ps", [P, 4, 512], F32))
        sq_ok, s_mm, ms_ok, root_ok, rms_ok, on_ok, y_ok, out_mm, x_ok = (sem(n) for n in (
            "sq_ok", "s_mm", "ms_ok", "root_ok", "rms_ok", "on_ok", "y_ok", "out_mm", "x_ok"))
        ctx.callback(clear, nc, own)
        block = ctx.enter_context(nc.Block())
        group = lambda a, i: a[:, i * GT:(i + 1) * GT]

        @block.scalar
        def _(act):
            def squares(i):
                if i >= 2:
                    act.wait_ge(s_mm, i - 1)
                nc.scalar.activation(sq[:, i % 2, :], group(oT, i), ACT.Square).then_inc(sq_ok, 1)
            squares(0)
            for i in range(NG):
                if i + 1 < NG:
                    squares(i + 1)
                act.wait_ge(s_mm, i + 1)
                if i >= 2:
                    act.wait_ge(on_ok, i - 1)
                nc.scalar.activation(ms[:, i % 2, :], ps[:, i % 2, :], ACT.Copy, scale=1.0 / DH, bias=1e-6).then_inc(ms_ok, 1)
                act.wait_ge(ms_ok, i + 1)
                nc.scalar.activation(rms[:, i % 2, :], ms[:, i % 2, :], ACT.Sqrt).then_inc(root_ok, 1)

        @block.tensor
        def _(pe):
            def sums(i):
                pe.wait_ge(sq_ok, i + 1)
                if i >= 2:
                    pe.wait_ge(ms_ok, i - 1)
                nc.tensor.matmul(ps[:, i % 2, :], w["blockones"][:, :], sq[:, i % 2, :], start=True, stop=True).then_inc(s_mm, 1)
            sums(0)
            for i in range(NG):
                if i + 1 < NG:
                    sums(i + 1)
                pe.wait_ge(y_ok, i + 1)
                if i >= 2:
                    pe.wait_ge(x_ok, i - 1)
                for t in range(G):
                    last = nc.tensor.matmul(ps[:, 2 + i % 2, t * P:(t + 1) * P], y[:, i % 2, t * P:(t + 1) * P], w["wo2"][:, :],
                                            start=True, stop=True)
                last.then_inc(out_mm, 1)

        @block.vector
        def _(dve):
            def gated(i):
                dve.wait_ge(root_ok, i + 1)
                nc.vector.reciprocal(rms[:, i % 2, :], rms[:, i % 2, :]).then_inc(rms_ok, 1)
                dve.wait_ge(rms_ok, i + 1)
                nc.vector.scalar_tensor_tensor(out=on[:, i % 2, :], in0=group(oT, i), scalar=w["rmsw"][:, :],
                                               in1=rms[:, i % 2, :], op0=ALU.mult, op1=ALU.mult).then_inc(on_ok, 1)
                dve.wait_ge(on_ok, i + 1)
                if i >= 2:
                    dve.wait_ge(out_mm, i - 1)
                nc.vector.tensor_tensor(y[:, i % 2, :], on[:, i % 2, :], group(gate, i), ALU.mult).then_inc(y_ok, 1)
            gated(0)
            for i in range(NG):
                if i + 1 < NG:
                    gated(i + 1)
                dve.wait_ge(out_mm, i + 1)
                nc.vector.tensor_tensor(tiles_of(X, i), ps[:, 2 + i % 2, :].rearrange("p (t d) -> p t d", t=G), tiles_of(X, i),
                                        ALU.add).then_inc(x_ok, 1)


def first_experts(nc, d, X):
    with ExitStack() as ctx:
        def sb(name, shape, dt=F32):
            return ctx.enter_context(nc.sbuf_tensor("m1_" + name, shape, dt))

        own = []

        def sem(name):
            own.append(ctx.enter_context(nc.semaphore("m1_" + name)))
            return own[-1]

        names = ("ident", "gate1", "ebias", "before8")
        w = {n: sb(n, list(d[n].shape)) for n in names}
        ln = Norm(nc, sb, sem, "ln")
        xn = sb("xn", [P, 2, G, D])
        xnT = sb("xnT", [P, TOK])
        xhi, xlo = sb("xhi", [P, TOK], F32R), sb("xlo", [P, TOK], F32R)
        whi, wlo = sb("whi", [P, 2, 2 * P], F32R), sb("wlo", [P, 2, 2 * P], F32R)
        sc, bi, rank, w2 = (sb(n, [P, NT, E1]) for n in ("sc", "bi", "rank", "w2"))
        gt, eq = sb("gt", [P, NT, E1, E1]), sb("eq", [P, NT, E1, E1])
        up = sb("up", [P, 2, 2 * P])
        down = sb("down", [P, 2, 2, D])
        relu = sb("relu", [P, 4, GT])
        h = sb("h", [P, 4, GT])
        ps = ctx.enter_context(nc.psum_tensor("m1_ps", [P, 8, 512], F32))
        w_in, xn_ok, tr_mm, xnT_ok, xhi_ok, xlo_ok, whi_ok, wlo_ok, lg_mm, sg, rt, h_mm, relu_ok, h_ok, out_mm, x_ok = (sem(n) for n in (
            "w_in", "xn_ok", "tr_mm", "xnT_ok", "xhi_ok", "xlo_ok", "whi_ok", "wlo_ok", "lg_mm", "sg", "rt", "h_mm", "relu_ok", "h_ok", "out_mm", "x_ok"))
        raw_in, ex_in = [sem("raw_in0"), sem("raw_in1")], [sem("ex_in0"), sem("ex_in1")]
        ctx.callback(clear, nc, own)
        block = ctx.enter_context(nc.Block())
        loaded = 16 * len(names)
        PAIRS = E1 // 2

        def wait(eng, s, v):
            if not isinstance(v, int) or v > 0:
                eng.wait_ge(s, v)

        def pairs_of_experts(eng, body):
            body(0, False)
            with eng.Fori(1, PAIRS - 1) as i:
                body(i, False)
            body(PAIRS - 1, True)

        @block.sync
        def _(sp):
            load_all(nc, sp, [(w[n], d[n]) for n in names], w_in)

            def body(i, last):
                for u in range(2):
                    wait(sp, wlo_ok, i * 2 + u - 1)
                    e = bass.ds(i * 2 + u, 1)
                    sp.dma_start(up[:, u, :], d["up1"][e, :, :].rearrange("o p k -> (o p) k")).then_inc(raw_in[u], 16)
                    wait(sp, out_mm, i * 8 + 4 * u - 4)
                    sp.dma_start(down[:, u, :, :], d["down1"][e, :, :, :].rearrange("o p k c -> (o p) k c")).then_inc(ex_in[u], 16)
            pairs_of_experts(sp, body)

        @block.gpsimd
        def _(pool):
            def lower_tokens(i):
                pool.wait_ge(xhi_ok, i + 1)
                g = slice(i * GT, (i + 1) * GT)
                nc.gpsimd.tensor_tensor(xlo[:, g], xnT[:, g], xhi[:, g].bitcast(F32), ALU.subtract).then_inc(xlo_ok, 1)

            def lower(e, u):
                pool.wait_ge(whi_ok, e + 1)
                nc.gpsimd.tensor_tensor(wlo[:, u, :], up[:, u, :], whi[:, u, :].bitcast(F32), ALU.subtract).then_inc(wlo_ok, 1)

            ln.prepare(pool)
            for i in range(NG):
                ln.root(pool, i)
                if i > 0:
                    lower_tokens(i - 1)
            lower_tokens(NG - 1)
            lower(0, 0)

            def body(i, last):
                for q in range(16):
                    n, m = i * 16 + q, i * 8 + q // 2
                    if q in (4, 12) and not (last and q == 12):
                        lower(i * 2 + q // 8 + 1, 1 - q // 8)
                    pool.wait_ge(relu_ok, n + 1)
                    wait(pool, out_mm, m - 1)
                    nc.gpsimd.tensor_tensor(h[:, q % 4, :], relu[:, q % 4, :], relu[:, q % 4, :], ALU.mult).then_inc(h_ok, 1)
            pairs_of_experts(pool, body)

        @block.scalar
        def _(act):
            def upper(u, rounds):
                act.wait_ge(raw_in[u], rounds * 16 + 16)
                nc.scalar.activation(whi[:, u, :], up[:, u, :], ACT.Copy).then_inc(whi_ok, 1)

            for i in range(NG):
                act.wait_ge(tr_mm, i + 1)
                nc.scalar.activation(xnT[:, i * GT:(i + 1) * GT], ps[:, i % 2, :], ACT.Copy).then_inc(xnT_ok, 1)
                nc.scalar.activation(xhi[:, i * GT:(i + 1) * GT], ps[:, i % 2, :], ACT.Copy).then_inc(xhi_ok, 1)
            upper(0, 0)
            act.wait_ge(lg_mm, 1)
            nc.scalar.activation(sc[:, :, :], ps[:, 2, 0:NT * E1].rearrange("p (t e) -> p t e", e=E1),
                                 ACT.Sigmoid).then_inc(sg, 1)

            def body(i, last):
                for q in range(16):
                    n = i * 16 + q
                    if q in (2, 10) and not (last and q == 10):
                        upper(1 - q // 8, i + q // 8)
                    act.wait_ge(h_mm, n + 1)
                    wait(act, h_ok, n - 3)
                    nc.scalar.activation(relu[:, q % 4, :], ps[:, 4 + q % 4, :], ACT.Relu).then_inc(relu_ok, 1)
            pairs_of_experts(act, body)

        @block.tensor
        def _(pe):
            pe.wait_ge(w_in, loaded)
            for i in range(NG):
                if i >= 2:
                    pe.wait_ge(xhi_ok, i - 1)
                for t in range(G):
                    pe.wait_ge(xn_ok, i * G + t + 1)
                    last = nc.tensor.transpose(ps[:, i % 2, t * P:(t + 1) * P], xn[:, i % 2, t, :], w["ident"][:, :])
                last.then_inc(tr_mm, 1)
            pe.wait_ge(xhi_ok, NG)
            pe.wait_ge(xlo_ok, NG)
            for t in range(NT):
                last = nc.tensor.matmul(ps[:, 2, t * E1:(t + 1) * E1], xnT[:, t * P:(t + 1) * P], w["gate1"][:, :],
                                        start=True, stop=True)
            last.then_inc(lg_mm, 1)

            def hidden(i, q):
                u, c = q // 4 % 2, q % 4
                if c == 0:
                    wait(pe, wlo_ok, i * 2 + q // 4 + 1)
                    pe.wait_ge(ex_in[u], i * 16 + (16 if q < 8 else 32))
                for k in range(2):
                    n = i * 16 + 2 * q + k
                    wait(pe, relu_ok, n - 3)
                    for j, (wp, xp) in enumerate(((whi, xhi), (wlo, xhi), (whi, xlo))):
                        last = nc.tensor.matmul(ps[:, 4 + (2 * q + k) % 4, :], wp[:, u, k * P:(k + 1) * P],
                                                xp[:, c * GT:(c + 1) * GT], start=(j == 0), stop=(j == 2))
                    last.then_inc(h_mm, 1)

            def body(i, last_pair):
                for q in range(8):
                    m = i * 8 + q
                    if not (last_pair and q == 7):
                        hidden(i, q + 1)
                    pe.wait_ge(h_ok, m * 2 + 2)
                    wait(pe, x_ok, m * 4 - 4)
                    for t in range(G):
                        for k in range(2):
                            last = nc.tensor.matmul(ps[:, 2 + q % 2, t * P:(t + 1) * P],
                                                    h[:, (2 * q + k) % 4, t * P:(t + 1) * P], down[:, q // 4, k, :],
                                                    start=(k == 0), stop=(k == 1))
                    last.then_inc(out_mm, 1)
            pe.wait_ge(sg, 1)
            hidden(0, 0)
            pairs_of_experts(pe, body)

        @block.vector
        def _(dve):
            for i in range(NG):
                ln.moments(dve, i, lambda t: X[:, i * G + t, :])
                if i >= 2:
                    dve.wait_ge(tr_mm, i - 1)
                for t in range(G):
                    ln.apply(xn[:, i % 2, t, :], X[:, i * G + t, :], t).then_inc(xn_ok, 1)
            dve.wait_ge(sg, 1)
            rows = lambda a: a[:, :].unsqueeze(1).broadcast_to([P, NT, E1])
            nc.vector.tensor_tensor(bi[:, :, :], sc[:, :, :], rows(w["ebias"]), ALU.add).then_inc(rt, 1)
            dve.wait_ge(rt, 1)
            other, own = bi[:, :, :].unsqueeze(2).broadcast_to([P, NT, E1, E1]), bi[:, :, :].unsqueeze(3).broadcast_to([P, NT, E1, E1])
            nc.vector.tensor_tensor(gt[:, :, :, :], other, own, ALU.is_gt).then_inc(rt, 1)
            nc.vector.tensor_tensor(eq[:, :, :, :], other, own, ALU.is_equal).then_inc(rt, 1)
            dve.wait_ge(rt, 3)
            nc.vector.tensor_tensor(eq[:, :, :, :], eq[:, :, :, :],
                                    w["before8"][:, :, :].unsqueeze(1).broadcast_to([P, NT, E1, E1]), ALU.mult).then_inc(rt, 1)
            dve.wait_ge(rt, 4)
            nc.vector.tensor_tensor(gt[:, :, :, :], gt[:, :, :, :], eq[:, :, :, :], ALU.add).then_inc(rt, 1)
            dve.wait_ge(rt, 5)
            nc.vector.reduce_sum(rank[:, :, :], gt[:, :, :, :], AX.X).then_inc(rt, 1)
            dve.wait_ge(rt, 6)
            nc.vector.scalar_tensor_tensor(out=w2[:, :, :], in0=rank[:, :, :], scalar=float(TOP1), in1=sc[:, :, :],
                                           op0=ALU.is_lt, op1=ALU.mult).then_inc(rt, 1)
            dve.wait_ge(rt, 7)
            nc.vector.tensor_tensor(w2[:, :, :], w2[:, :, :], w2[:, :, :], ALU.mult).then_inc(rt, 1)
            dve.wait_ge(rt, 8)

            def body(i, last):
                for q in range(8):
                    m = i * 8 + q
                    dve.wait_ge(out_mm, m + 1)
                    wait(dve, x_ok, m * 4 - 12)
                    for t in range(G):
                        x = X[:, G * (q % 4) + t, :]
                        we = w2[:, G * (q % 4) + t, bass.ds(i * 2 + q // 4, 1)]
                        nc.vector.scalar_tensor_tensor(out=x, in0=ps[:, 2 + q % 2, t * P:(t + 1) * P], scalar=we, in1=x,
                                                       op0=ALU.mult, op1=ALU.add).then_inc(x_ok, 1)
            pairs_of_experts(dve, body)


def row_tiles(a):
    return a[:, :].unsqueeze(1).broadcast_to([P, G, D])


ROTATION = 3
LAST = K - 12 * P


def load_context(nc, sp, d, C, c_in, j, u):
    for b in range(2):
        c = d["ctx"][bass.ds(j * 2 + b, 1), :, :].rearrange("o k d -> (o k) d")
        sp.dma_start(C[:, u, b, 0:12, :], c[0:12 * P, :].rearrange("(p t) d -> p t d", t=12)).then_inc(c_in[u], 16)
        sp.dma_start(C[0:LAST, u, b, 12, :], c[12 * P:K, :]).then_inc(c_in[u], 16)


def decoder_self_attention(nc, d, X, Y, YT, C, c_in):
    with ExitStack() as ctx:
        def sb(name, shape, dt=F32):
            return ctx.enter_context(nc.sbuf_tensor("sa_" + name, shape, dt))

        own = []

        def sem(name):
            own.append(ctx.enter_context(nc.semaphore("sa_" + name)))
            return own[-1]

        names = ("ident", "causal2", "g1", "beta1")
        w = {n: sb(n, list(d[n].shape)) for n in names}
        ln, ln1 = Norm(nc, sb, sem, "ln"), Norm(nc, sb, sem, "ln1")
        y = sb("y", [P, 2, G, D])
        sm, pm, y1p, n1, y1 = (sb(n, [P, G, D]) for n in ("sm", "pm", "y1p", "n1", "y1"))
        yT, pmT = sb("yT", [P, GT]), sb("pmT", [P, GT])
        mx, nb, sums, rs = (sb(n, [P, G]) for n in ("mx", "nb", "sums", "rs"))
        ps = ctx.enter_context(nc.psum_tensor("sa_ps", [P, 8, 512], F32))
        (w_in, y_ok, tr_mm, yT_ok, s_mm, sm_ok, mx_ok, nb_ok, p_ok, pt_mm, pmT_ok, sa_mm, rs_ok, y1p_ok, n1_ok, m_ok, y1_ok,
         y1t_mm, yt_ok, yy_ok) = (sem(n) for n in (
            "w_in", "y_ok", "tr_mm", "yT_ok", "s_mm", "sm_ok", "mx_ok", "nb_ok", "p_ok", "pt_mm", "pmT_ok", "sa_mm",
            "rs_ok", "y1p_ok", "n1_ok", "m_ok", "y1_ok", "y1t_mm", "yt_ok", "yy_ok"))
        ctx.callback(clear, nc, own)
        block = ctx.enter_context(nc.Block())
        loaded = 16 * len(names)

        @block.sync
        def _(sp):
            load_all(nc, sp, [(w[n], d[n]) for n in names], w_in)
            for u in range(ROTATION):
                load_context(nc, sp, d, C, c_in, u, u)

        @block.gpsimd
        def _(pool):
            ln.prepare(pool)
            ln1.prepare(pool)
            ln.root(pool, 0)
            for i in range(NG):
                if i + 1 < NG:
                    ln.root(pool, i + 1)
                ln1.root(pool, i)

        @block.scalar
        def _(act):
            def tokens(i):
                act.wait_ge(tr_mm, i + 1)
                nc.scalar.activation(yT[:, :], ps[:, 0, :], ACT.Copy).then_inc(yT_ok, 1)
            tokens(0)
            for i in range(NG):
                act.wait_ge(nb_ok, i + 1)
                for t in range(G):
                    nc.scalar.activation(pm[:, t, :], sm[:, t, :], ACT.Exp, bias=nb[:, t:t + 1], scale=SCALE1,
                                         accum_out=sums[:, t:t + 1]).then_inc(p_ok, 1)
                act.wait_ge(pt_mm, i + 1)
                nc.scalar.activation(pmT[:, :], ps[:, 2, :], ACT.Copy).then_inc(pmT_ok, 1)
                if i + 1 < NG:
                    tokens(i + 1)
                act.wait_ge(y1t_mm, i + 1)
                nc.scalar.activation(YT[:, i * GT:(i + 1) * GT], ps[:, 4, :], ACT.Copy).then_inc(yt_ok, 1)

        @block.tensor
        def _(pe):
            def tokens(i):
                for t in range(G):
                    pe.wait_ge(y_ok, i * G + t + 1)
                    last = nc.tensor.transpose(ps[:, 0, t * P:(t + 1) * P], y[:, i % 2, t, :], w["ident"][:, :])
                last.then_inc(tr_mm, 1)

            def scores(i):
                pe.wait_ge(yT_ok, i + 1)
                for t in range(G):
                    yt = yT[:, t * P:(t + 1) * P]
                    last = nc.tensor.matmul(ps[:, 1, t * P:(t + 1) * P], yt, yt, start=True, stop=True)
                last.then_inc(s_mm, 1)

            pe.wait_ge(w_in, loaded)
            tokens(0)
            scores(0)
            for i in range(NG):
                for t in range(G):
                    pe.wait_ge(p_ok, i * G + t + 1)
                    last = nc.tensor.transpose(ps[:, 2, t * P:(t + 1) * P], pm[:, t, :], w["ident"][:, :])
                last.then_inc(pt_mm, 1)
                pe.wait_ge(pmT_ok, i + 1)
                for t in range(G):
                    last = nc.tensor.matmul(ps[:, 3, t * P:(t + 1) * P], pmT[:, t * P:(t + 1) * P], y[:, i % 2, t, :],
                                            start=True, stop=True)
                last.then_inc(sa_mm, 1)
                if i + 1 < NG:
                    tokens(i + 1)
                    scores(i + 1)
                pe.wait_ge(y1_ok, i + 1)
                for t in range(G):
                    last = nc.tensor.transpose(ps[:, 4, t * P:(t + 1) * P], y1[:, t, :], w["ident"][:, :])
                last.then_inc(y1t_mm, 1)

        @block.vector
        def _(dve):
            def tokens(i):
                ln.moments(dve, i, lambda t: X[:, i * G + t, :])
                for t in range(G):
                    ln.apply(y[:, i % 2, t, :], X[:, i * G + t, :], t).then_inc(y_ok, 1)

            dve.wait_ge(w_in, loaded)
            tokens(0)
            for i in range(NG):
                dve.wait_ge(s_mm, i + 1)
                nc.vector.tensor_tensor(sm[:, :, :], ps[:, 1, :].rearrange("p (t d) -> p t d", t=G), row_tiles(w["causal2"]),
                                        ALU.add).then_inc(sm_ok, 1)
                dve.wait_ge(sm_ok, i + 1)
                nc.vector.reduce_max(mx[:, :], sm[:, :, :], AX.X).then_inc(mx_ok, 1)
                dve.wait_ge(mx_ok, i + 1)
                nc.vector.tensor_scalar(nb[:, :], mx[:, :], -SCALE1, None, ALU.mult).then_inc(nb_ok, 1)
                if i + 1 < NG:
                    tokens(i + 1)
                dve.wait_ge(p_ok, i * G + G)
                nc.vector.reciprocal(rs[:, :], sums[:, :]).then_inc(rs_ok, 1)
                dve.wait_ge(rs_ok, i + 1)
                dve.wait_ge(sa_mm, i + 1)
                for t in range(G):
                    nc.vector.scalar_tensor_tensor(out=y1p[:, t, :], in0=ps[:, 3, t * P:(t + 1) * P], scalar=rs[:, t:t + 1],
                                                   in1=y[:, i % 2, t, :], op0=ALU.mult, op1=ALU.add).then_inc(y1p_ok, 1)
                dve.wait_ge(y1p_ok, i * G + G)
                ln1.moments(dve, i, lambda t: y1p[:, t, :])
                for t in range(G):
                    ln1.apply(n1[:, t, :], y1p[:, t, :], t).then_inc(n1_ok, 1)
                dve.wait_ge(n1_ok, i * G + G)
                nc.vector.tensor_tensor(n1[:, :, :], n1[:, :, :], row_tiles(w["g1"]), ALU.mult).then_inc(m_ok, 1)
                dve.wait_ge(m_ok, i + 1)
                nc.vector.tensor_tensor(y1[:, :, :], n1[:, :, :], row_tiles(w["beta1"]), ALU.add).then_inc(y1_ok, 1)
                nc.vector.tensor_tensor(Y[:, i * G:(i + 1) * G, :], n1[:, :, :], row_tiles(w["beta1"]), ALU.add).then_inc(yy_ok, 1)
                dve.wait_ge(yy_ok, i + 1)


def decoder_cross_attention(nc, d, Y, YT, C, c_in):
    with ExitStack() as ctx:
        def sb(name, shape, dt=F32):
            return ctx.enter_context(nc.sbuf_tensor("ca_" + name, shape, dt))

        own = list(c_in)

        def sem(name):
            own.append(ctx.enter_context(nc.semaphore("ca_" + name)))
            return own[-1]

        R = ROTATION
        ident = sb("ident", [P, P])
        cT = sb("cT", [P, R, 2, KT * P])
        yT = sb("yT", [P, R, P])
        E = sb("E", [P, R, KPAD])
        PT = sb("PT", [P, KT, P])
        mx, sums = sb("mx", [P, R, 4]), sb("sums", [P, R, 4])
        m, nb, tot, rs = (sb(n, [P, R, 1]) for n in ("m", "nb", "tot", "rs"))
        psS = ctx.enter_context(nc.psum_tensor("ca_psS", [P, 4, 512], F32))
        psT = ctx.enter_context(nc.psum_tensor("ca_psT", [P, 2, 512], F32))
        psO = ctx.enter_context(nc.psum_tensor("ca_psO", [P, 512], F32))
        (w_in, y_ok, s_mm, mx_ok, m_ok, nb_ok, p_ok, t_mm, ta, td, o_mm, tot_ok, rs_ok, o_ok) = (sem(n) for n in (
            "w_in", "y_ok", "s_mm", "mx_ok", "m_ok", "nb_ok", "p_ok", "t_mm", "ta", "td", "o_mm", "tot_ok", "rs_ok",
            "o_ok"))
        ctx.callback(clear, nc, own)
        block = ctx.enter_context(nc.Block())
        SUMS = [range(0, 3), range(3, 8), range(8, KT), range(0, 0)]

        def wait(eng, s, v):
            if not isinstance(v, int) or v > 0:
                eng.wait_ge(s, v)

        def steps(eng, step):
            for j in range(R):
                step(j, j, 0, j > 0, True, True)
            with eng.Fori(1, NT // R) as i:
                for u in range(R):
                    step(i * R + u, u, i, True, True, True)
            for j in range(NT - 1, NT + 1):
                step(j, j % R, j // R, True, j < NT, False)

        def half(j):
            if isinstance(j, int):
                return 0 if j < 0 else 4 if j == 0 else 6 * j + 2 if j < NT else 6 * j - 2
            return j * 6 + 2

        @block.sync
        def _(sp):
            sp.dma_start(ident[:, :], d["ident"]).then_inc(w_in, 16)

            def load(j, u):
                wait(sp, o_mm, j - R + 1)
                load_context(nc, sp, d, C, c_in, j, u)
            with sp.Fori(1, NT // R) as i:
                for u in range(R):
                    load(i * R + u, u)
            load(NT - 1, (NT - 1) % R)

        @block.tensor
        def _(pe):
            def context(n, k, u):
                wait(pe, (ta, td)[k % 2], n + k // 2)
                for t in range(4 * (k // 2), min(4 * (k // 2) + 4, KT)):
                    rows = P if t < 12 else LAST
                    s = t % 4 * P
                    last = nc.tensor.transpose(psT[:, k % 2, s:s + rows], C[0:rows, u, k % 2, t, :], ident[0:rows, 0:rows])
                last.then_inc(t_mm, 1)

            def weights(n, k, u):
                wait(pe, (ta, td)[k % 2], n + k // 2)
                for t in range(4 * k, min(4 * k + 4, KT)):
                    rows = P if t < 12 else LAST
                    last = nc.tensor.transpose(psT[0:rows, k % 2, t % 4 * P:t % 4 * P + P], E[:, u, t * P:t * P + rows],
                                               ident[:, :])
                last.then_inc(t_mm, 1)

            def scores(j, u, n):
                wait(pe, p_ok, 4 * j - 4 + n + 1)
                pe.wait_ge(ta, half(j) - 3 + n)
                pe.wait_ge(td, half(j) - 3 + n)
                k0, k1 = n * 400, n * 400 + 400 if n < 3 else K
                for b in range(2):
                    last = nc.tensor.matmul(psS[S * b:S * b + S, n, 0:k1 - k0], yT[:, u, S * b:S * b + S],
                                            cT[:, u, b, k0:k1], start=True, stop=True)
                last.then_inc(s_mm, 1)

            pe.wait_ge(w_in, 16)
            pe.wait_ge(c_in[0], 64)
            for k in range(8):
                context(0, k, 0)

            def step(j, u, i, behind, live, ahead):
                if live:
                    pe.wait_ge(y_ok, j + 1)
                for n in range(4):
                    if live:
                        scores(j, u, n)
                    if behind and n == 0:
                        pe.wait_ge(p_ok, 4 * j)
                    if behind and n < 3:
                        weights(half(j), n, (u - 1) % R)
                    if behind and n == 2:
                        weights(half(j), 3, (u - 1) % R)
                if behind:
                    pe.wait_ge(ta, half(j) + 2)
                    pe.wait_ge(td, half(j) + 2)
                    wait(pe, o_ok, j - 1)
                if ahead:
                    pe.wait_ge(c_in[(u + 1) % R], (i + (u + 1) // R) * 64 + 64)
                for part in range(4):
                    if behind:
                        for t in SUMS[part]:
                            n = P if t < 12 else LAST
                            for b in range(2):
                                last = nc.tensor.matmul(psO[S * b:S * b + S, 0:D], PT[0:n, t, S * b:S * b + S],
                                                        C[0:n, (u - 1) % R, b, t, :], start=(t == 0), stop=(t == KT - 1))
                        if KT - 1 in SUMS[part]:
                            last.then_inc(o_mm, 1)
                    if ahead:
                        for k in (2 * part, 2 * part + 1):
                            context(half(j) + (2 if behind else 0), k, (u + 1) % R)
            steps(pe, step)

        def move_context(eng, done, copy, n, k, u):
            eng.wait_ge(t_mm, n + k + 1)
            width = 4 * P if k < 6 else LAST
            copy(cT[:, u, k % 2, 512 * (k // 2):512 * (k // 2) + width], psT[:, k % 2, 0:width]).then_inc(done, 1)

        def move_weights(eng, done, copy, n, k):
            eng.wait_ge(t_mm, n + k + 1)
            rows, tiles = (P, 4) if k < 3 else (LAST, 1)
            copy(PT[0:rows, 4 * k:4 * k + tiles, :],
                 psT[0:rows, k % 2, 0:tiles * P].rearrange("p (t q) -> p t q", t=tiles)).then_inc(done, 1)

        @block.scalar
        def _(act):
            def copy(dst, src):
                return nc.scalar.activation(dst, src, ACT.Copy)

            def ahead_context(j, k, u, behind):
                move_context(act, ta, copy, 2 * half(j) + (4 if behind else 0), k, (u + 1) % R)

            for k in range(0, 8, 2):
                move_context(act, ta, copy, 0, k, 0)

            def step(j, u, i, behind, live, ahead):
                if behind:
                    wait(act, o_mm, j - 1)
                    for k in (0, 2):
                        move_weights(act, ta, copy, 2 * half(j), k)
                if ahead:
                    ahead_context(j, 0, u, behind)
                if live:
                    act.wait_ge(nb_ok, j + 1)
                    for n in range(4):
                        k0, k1 = n * 400, n * 400 + 400 if n < 3 else K
                        nc.scalar.activation(E[:, u, k0:k1], psS[:, n, 0:k1 - k0], ACT.Exp, bias=nb[:, u, :], scale=SCALE1,
                                             accum_out=sums[:, u, n:n + 1]).then_inc(p_ok, 1)
                if ahead:
                    for k in range(2, 8, 2):
                        ahead_context(j, k, u, behind)
            steps(act, step)

        @block.vector
        def _(dve):
            copy = nc.vector.tensor_copy

            def queries(j, u):
                wait(dve, s_mm, 4 * (j - 2))
                ytile = YT[:, bass.ds(j * P, P)]
                nc.vector.tensor_tensor(yT[:, u, :], ytile, ytile, ALU.max).then_inc(y_ok, 1)

            def ahead_context(j, k, u, behind):
                move_context(dve, td, copy, 2 * half(j) + (4 if behind else 0), k, (u + 1) % R)

            queries(0, 0)
            for k in range(1, 8, 2):
                move_context(dve, td, copy, 0, k, 0)

            def step(j, u, i, behind, live, ahead):
                w = (u - 1) % R
                if ahead:
                    queries(j + 1, (u + 1) % R)
                if behind:
                    dve.wait_ge(p_ok, 4 * j)
                    nc.vector.reduce_sum(tot[:, w, :], sums[:, w, :], AX.X).then_inc(tot_ok, 1)
                    dve.wait_ge(tot_ok, j)
                    nc.vector.reciprocal(rs[:, w, :], tot[:, w, :]).then_inc(rs_ok, 1)
                for n in range(4):
                    if live:
                        k0, k1 = n * 400, n * 400 + 400 if n < 3 else K
                        dve.wait_ge(s_mm, 4 * j + n + 1)
                        nc.vector.reduce_max(mx[:, u, n:n + 1], psS[:, n, 0:k1 - k0], AX.X).then_inc(mx_ok, 1)
                    if behind and n in (1, 2):
                        move_weights(dve, td, copy, 2 * half(j), 2 * n - 1)
                if live:
                    dve.wait_ge(mx_ok, 4 * j + 4)
                    nc.vector.reduce_max(m[:, u, :], mx[:, u, :], AX.X).then_inc(m_ok, 1)
                    dve.wait_ge(m_ok, j + 1)
                    nc.vector.tensor_scalar(nb[:, u, :], m[:, u, :], -SCALE1, None, ALU.mult).then_inc(nb_ok, 1)
                if ahead:
                    for k in (1, 3, 5):
                        ahead_context(j, k, u, behind)
                if behind:
                    dve.wait_ge(rs_ok, j)
                    dve.wait_ge(o_mm, j)
                    yj = Y[:, bass.ds(j - 1, 1), :].rearrange("p a b -> p (a b)")
                    nc.vector.scalar_tensor_tensor(out=yj, in0=psO[:, 0:D], scalar=rs[:, w, :], in1=yj, op0=ALU.mult,
                                                   op1=ALU.add).then_inc(o_ok, 1)
                if ahead:
                    ahead_context(j, 7, u, behind)
            steps(dve, step)


def decoder_feed_forward(nc, d, X, Y):
    with ExitStack() as ctx:
        def sb(name, shape, dt=F32):
            return ctx.enter_context(nc.sbuf_tensor("ff_" + name, shape, dt))

        own = []

        def sem(name):
            own.append(ctx.enter_context(nc.semaphore("ff_" + name)))
            return own[-1]

        names = ("ident", "g2", "beta2", "g3", "beta3", "b2", "b1", "w1", "w2")
        w = {n: sb(n, list(d[n].shape)) for n in names}
        NF = 4
        ln2, ln3 = Norm(nc, sb, sem, "ln2"), Norm(nc, sb, sem, "ln3")
        y2, y2b = sb("y2", [P, G, D]), sb("y2b", [P, 2, G, D])
        n2, y3p, n3 = (sb(n, [P, G, D]) for n in ("n2", "y3p", "n3"))
        yT, hT = sb("yT", [P, GT]), sb("hT", [P, NF, GT])
        ps = ctx.enter_context(nc.psum_tensor("ff_ps", [P, 8, 512], F32))
        (w_in, n2_ok, m2_ok, m_ok, y2_ok, b_ok, tr_mm, yT_ok, h_mm, h_ok, f_mm, y3_ok, n3_ok, x_ok) = (sem(n) for n in (
            "w_in", "n2_ok", "m2_ok", "m_ok", "y2_ok", "b_ok", "tr_mm", "yT_ok", "h_mm", "h_ok", "f_mm", "y3_ok", "n3_ok", "x_ok"))
        ctx.callback(clear, nc, own)
        block = ctx.enter_context(nc.Block())
        loaded = 16 * len(names)

        @block.sync
        def _(sp):
            load_all(nc, sp, [(w[n], d[n]) for n in names], w_in)

        @block.gpsimd
        def _(pool):
            def second(i):
                ln2.root(pool, i)
                pool.wait_ge(y2_ok, i + 1)
                if i >= 2:
                    pool.wait_ge(y3_ok, i - 1)
                nc.gpsimd.tensor_tensor(y2b[:, i % 2, :, :], y2[:, :, :], row_tiles(w["b2"]), ALU.add).then_inc(b_ok, 1)
            ln2.prepare(pool)
            ln3.prepare(pool)
            pool.wait_ge(w_in, loaded)
            second(0)
            for i in range(NG):
                if i + 1 < NG:
                    second(i + 1)
                ln3.root(pool, i)

        @block.scalar
        def _(act):
            def tokens(i):
                act.wait_ge(tr_mm, i + 1)
                nc.scalar.activation(yT[:, :], ps[:, 0, :], ACT.Copy).then_inc(yT_ok, 1)

            act.wait_ge(w_in, loaded)
            tokens(0)
            for i in range(NG):
                for f in range(NF):
                    act.wait_ge(h_mm, i * NF + f + 1)
                    if i > 0:
                        act.wait_ge(f_mm, i)
                    nc.scalar.activation(hT[:, f, :], ps[:, 1 + f, :], ACT.Relu, bias=w["b1"][:, f:f + 1]).then_inc(h_ok, 1)
                if i + 1 < NG:
                    tokens(i + 1)

        @block.tensor
        def _(pe):
            def tokens(i):
                pe.wait_ge(y2_ok, i + 1)
                for t in range(G):
                    last = nc.tensor.transpose(ps[:, 0, t * P:(t + 1) * P], y2[:, t, :], w["ident"][:, :])
                last.then_inc(tr_mm, 1)

            pe.wait_ge(w_in, loaded)
            tokens(0)
            for i in range(NG):
                pe.wait_ge(yT_ok, i + 1)
                for f in range(NF):
                    nc.tensor.matmul(ps[:, 1 + f, :], w["w1"][:, f * P:(f + 1) * P], yT[:, :], start=True,
                                     stop=True).then_inc(h_mm, 1)
                if i + 1 < NG:
                    tokens(i + 1)
                pe.wait_ge(h_ok, i * NF + NF)
                if i > 0:
                    pe.wait_ge(y3_ok, i)
                for t in range(G):
                    for f in range(NF):
                        last = nc.tensor.matmul(ps[:, 5, t * P:(t + 1) * P], hT[:, f, t * P:(t + 1) * P], w["w2"][:, f, :],
                                                start=(f == 0), stop=(f == NF - 1))
                last.then_inc(f_mm, 1)

        @block.vector
        def _(dve):
            def second(i):
                ln2.moments(dve, i, lambda t: Y[:, i * G + t, :])
                for t in range(G):
                    ln2.apply(n2[:, t, :], Y[:, i * G + t, :], t).then_inc(n2_ok, 1)
                dve.wait_ge(n2_ok, i * G + G)
                nc.vector.tensor_tensor(n2[:, :, :], n2[:, :, :], row_tiles(w["g2"]), ALU.mult).then_inc(m2_ok, 1)
                dve.wait_ge(m2_ok, i + 1)
                if i > 0:
                    dve.wait_ge(tr_mm, i)
                    dve.wait_ge(b_ok, i)
                nc.vector.tensor_tensor(y2[:, :, :], n2[:, :, :], row_tiles(w["beta2"]), ALU.add).then_inc(y2_ok, 1)
                dve.wait_ge(y2_ok, i + 1)

            dve.wait_ge(w_in, loaded)
            second(0)
            for i in range(NG):
                if i + 1 < NG:
                    second(i + 1)
                dve.wait_ge(b_ok, i + 1)
                dve.wait_ge(f_mm, i + 1)
                nc.vector.tensor_tensor(y3p[:, :, :], ps[:, 5, :].rearrange("p (t d) -> p t d", t=G), y2b[:, i % 2, :, :],
                                        ALU.add).then_inc(y3_ok, 1)
                dve.wait_ge(y3_ok, i + 1)
                ln3.moments(dve, i, lambda t: y3p[:, t, :])
                for t in range(G):
                    ln3.apply(n3[:, t, :], y3p[:, t, :], t).then_inc(n3_ok, 1)
                dve.wait_ge(n3_ok, i * G + G)
                nc.vector.tensor_tensor(n3[:, :, :], n3[:, :, :], row_tiles(w["g3"]), ALU.mult).then_inc(m_ok, 1)
                dve.wait_ge(m_ok, i * 2 + 1)
                nc.vector.tensor_tensor(n3[:, :, :], n3[:, :, :], row_tiles(w["beta3"]), ALU.add).then_inc(m_ok, 1)
                dve.wait_ge(m_ok, i * 2 + 2)
                x = X[:, i * G:(i + 1) * G, :]
                nc.vector.tensor_tensor(x, n3[:, :, :], x, ALU.add).then_inc(x_ok, 1)
                dve.wait_ge(x_ok, i + 1)


def decoder_layer(nc, d, X):
    with ExitStack() as ctx:
        Y = ctx.enter_context(nc.sbuf_tensor("Y", [P, NT, D], F32))
        YT = ctx.enter_context(nc.sbuf_tensor("YT", [P, TOK], F32))
        C = ctx.enter_context(nc.sbuf_tensor("C", [P, ROTATION, 2, KT, D], F32))
        c_in = [ctx.enter_context(nc.semaphore("c_in%d" % u)) for u in range(ROTATION)]
        decoder_self_attention(nc, d, X, Y, YT, C, c_in)
        decoder_cross_attention(nc, d, Y, YT, C, c_in)
        decoder_feed_forward(nc, d, X, Y)


def windowed_attention(nc, d, X):
    with ExitStack() as ctx:
        def sb(name, shape, dt=F32):
            return ctx.enter_context(nc.sbuf_tensor("wa_" + name, shape, dt))

        names = ("ident", "wout", "window", "headmask")
        w = {n: sb(n, list(d[n].shape)) for n in names}
        qT, kT = sb("qT", [P, TOK]), sb("kT", [P, TOK])
        V = sb("V", [P, B, NPAIR, 18])
        windowed_attention_project(nc, d, X, w, names, qT, kT, V)
        windowed_attention_tiles(nc, X, w, qT, kT, V)


def windowed_attention_project(nc, d, X, shared, shared_names, qT, kT, V):
    with ExitStack() as ctx:
        def sb(name, shape, dt=F32):
            return ctx.enter_context(nc.sbuf_tensor("wp_" + name, shape, dt))

        own = []

        def sem(name):
            own.append(ctx.enter_context(nc.semaphore("wp_" + name)))
            return own[-1]

        names = ("wq3", "wk3", "wv3")
        w = {n: sb(n, list(d[n].shape)) for n in names}
        ln = Norm(nc, sb, sem, "ln")
        xn = sb("xn", [P, 2, G, D])
        xnT = sb("xnT", [P, 2, GT])
        ps = ctx.enter_context(nc.psum_tensor("wp_ps", [P, 8, 512], F32))
        w_in, zeroed, xn_ok, tr_mm, xnT_ok, q_mm, k_mm, q_ok, k_ok, v_mm, v_ok = (sem(n) for n in (
            "w_in", "zeroed", "xn_ok", "tr_mm", "xnT_ok", "q_mm", "k_mm", "q_ok", "k_ok", "v_mm", "v_ok"))
        ctx.callback(clear, nc, own)
        block = ctx.enter_context(nc.Block())
        loads = [(w[n], d[n]) for n in names] + [(shared[n], d[n]) for n in shared_names]
        loaded = 16 * len(loads)

        @block.sync
        def _(sp):
            load_all(nc, sp, loads, w_in)

        @block.gpsimd
        def _(pool):
            ln.prepare(pool)
            ln.root(pool, 0)
            nc.gpsimd.memset(V[:, :, :, :], 0.0).then_inc(zeroed, 1)
            pool.wait_ge(zeroed, 1)
            for half in range(2):
                nc.gpsimd.memset(V[S * half:S * half + S, :, :, 16 + half:17 + half], 1.0).then_inc(zeroed, 1)
                pool.wait_ge(zeroed, 2 + half)
            for i in range(1, NG):
                ln.root(pool, i)

        @block.scalar
        def _(act):
            for i in range(NG):
                act.wait_ge(tr_mm, i + 1)
                if i >= 2:
                    act.wait_ge(v_mm, i - 1)
                nc.scalar.activation(xnT[:, i % 2, :], ps[:, 0, :], ACT.Copy).then_inc(xnT_ok, 1)
                act.wait_ge(k_mm, i + 1)
                nc.scalar.activation(kT[:, i * GT:(i + 1) * GT], ps[:, 2, :], ACT.Copy).then_inc(k_ok, 1)
                act.wait_ge(v_mm, i + 1)
                act.wait_ge(zeroed, 3)
                for half in range(2):
                    r, c = slice(S * half, S * half + S), slice(DH * half, DH * half + DH)
                    nc.scalar.activation(V[r, 2 * G * i:2 * G * (i + 1), :, c],
                                         ps[r, 3:5, :].rearrange("p a (b g e) -> p (a b) g e", b=4, e=16)[:, :, :, c],
                                         ACT.Copy).then_inc(v_ok, 1)

        @block.tensor
        def _(pe):
            def transposes(i):
                if i > 0:
                    pe.wait_ge(xnT_ok, i)
                for t in range(G):
                    pe.wait_ge(xn_ok, i * G + t + 1)
                    last = nc.tensor.transpose(ps[:, 0, t * P:(t + 1) * P], xn[:, i % 2, t, :], shared["ident"][:, :])
                last.then_inc(tr_mm, 1)

            pe.wait_ge(w_in, loaded)
            transposes(0)
            for i in range(NG):
                pe.wait_ge(xnT_ok, i + 1)
                if i > 0:
                    pe.wait_ge(q_ok, i)
                nc.tensor.matmul(ps[:, 1, :], w["wq3"][:, :], xnT[:, i % 2, :], start=True, stop=True).then_inc(q_mm, 1)
                if i > 0:
                    pe.wait_ge(k_ok, i)
                nc.tensor.matmul(ps[:, 2, :], w["wk3"][:, :], xnT[:, i % 2, :], start=True, stop=True).then_inc(k_mm, 1)
                if i + 1 < NG:
                    transposes(i + 1)
                if i > 0:
                    pe.wait_ge(v_ok, 2 * i)
                for b in range(2 * G):
                    for half in range(2):
                        last = nc.tensor.matmul(ps[S * half:S * half + S, 3 + b // 4, b % 4 * P:(b % 4 + 1) * P],
                                                xnT[:, i % 2, b * S:(b + 1) * S], w["wv3"][:, :], start=True, stop=True)
                last.then_inc(v_mm, 1)

        @block.vector
        def _(dve):
            def tokens(i):
                ln.moments(dve, i, lambda t: X[:, i * G + t, :])
                if i >= 2:
                    dve.wait_ge(tr_mm, i - 1)
                for t in range(G):
                    ln.apply(xn[:, i % 2, t, :], X[:, i * G + t, :], t).then_inc(xn_ok, 1)

            tokens(0)
            for i in range(NG):
                if i + 1 < NG:
                    tokens(i + 1)
                dve.wait_ge(q_mm, i + 1)
                nc.vector.tensor_scalar(qT[:, i * GT:(i + 1) * GT], ps[:, 1, :], QSCALE, None, ALU.mult).then_inc(q_ok, 1)


def windowed_attention_tiles(nc, X, w, qT, kT, V):
    with ExitStack() as ctx:
        def sb(name, shape, dt=F32):
            return ctx.enter_context(nc.sbuf_tensor("wt_" + name, shape, dt))

        own = []

        def sem(name):
            own.append(ctx.enter_context(nc.semaphore("wt_" + name)))
            return own[-1]

        queries = sb("queries", [P, 2, P])
        keys = sb("keys", [P, 2, 2, H, S])
        values = sb("values", [P, 2, 2, NPAIR, 18])
        ones = sb("ones", [P, 1])
        E = sb("E", [P, 2, H, S])
        PT = sb("PT", [P, NPAIR, P])
        mx = sb("mx", [P, 2, H])
        rs = sb("rs", [P, 2, NPAIR, 2])
        O = sb("O", [P, 2, D])
        OT = sb("OT", [P, 2, P])
        psS = ctx.enter_context(nc.psum_tensor("wt_psS", [P, 2, 2, 512], F32))
        psT = ctx.enter_context(nc.psum_tensor("wt_psT", [P, 2, 512], F32))
        psO = ctx.enter_context(nc.psum_tensor("wt_psO", [P, 512], F32))
        psX = ctx.enter_context(nc.psum_tensor("wt_psX", [P, 512], F32))
        (ones_set, q_ok, keys_ok, values_ok, s_mm, sm_ok, mx_ok, sub_ok, e_ok, t_mm, pt_ok, o_mm, rs_ok, on_ok, ot_mm, ot_ok,
         out_mm, x_ok) = (sem(n) for n in (
            "ones_set", "q_ok", "keys_ok", "values_ok", "s_mm", "sm_ok", "mx_ok", "sub_ok", "e_ok", "t_mm", "pt_ok",
            "o_mm", "rs_ok", "on_ok", "ot_mm", "ot_ok", "out_mm", "x_ok"))
        ctx.callback(clear, nc, own)
        block = ctx.enter_context(nc.Block())
        heads = lambda a: a.unsqueeze(2).broadcast_to([P, H, S])

        def wait(eng, s, n):
            if not isinstance(n, int) or n > 0:
                eng.wait_ge(s, n)

        def steps(eng, step):
            step(0, 0)
            step(1, 1)
            with eng.Fori(1, NT // 2 - 2) as i:
                step(i * 2, 0)
                step(i * 2 + 1, 1)
            for T in range(NT - 4, NT + 2):
                step(T, T % 2)

        def tile(T):
            return not isinstance(T, int) or 0 <= T < NT

        @block.gpsimd
        def _(pool):
            def take_keys(T, u):
                wait(pool, s_mm, T - 1)
                for b in range(2):
                    k = kT[:, bass.ds(T * P + b * S, S)].unsqueeze(1).broadcast_to([P, H, S])
                    nc.gpsimd.tensor_tensor(keys[:, u, b, :, :], heads(w["headmask"][:, :]), k, ALU.mult).then_inc(keys_ok, 1)

            def take_values(T, u):
                wait(pool, o_mm, T - 1)
                nc.gpsimd.tensor_tensor(values[:, u, :, :, :].rearrange("p b g e -> p (b g e)"),
                                        V[:, bass.ds(T * 2, 2), :, :].rearrange("p b g e -> p (b g e)"),
                                        ones[:, :].broadcast_to([P, 2 * NPAIR * 18]), ALU.mult).then_inc(values_ok, 1)
            nc.gpsimd.memset(ones[:, :], 1.0).then_inc(ones_set, 1)
            pool.wait_ge(ones_set, 1)
            take_keys(0, 0)
            take_keys(1, 1)
            take_values(0, 0)
            take_keys(2, 0)

            def step(T, u):
                if tile(T + 1):
                    take_values(T + 1, 1 - u)
                if tile(T + 3):
                    take_keys(T + 3, 1 - u)
            steps(pool, step)

        @block.scalar
        def _(act):
            def step(T, u):
                if tile(T):
                    act.wait_ge(sub_ok, T + 1)
                    nc.scalar.activation(E[:, u, :, :], E[:, u, :, :], ACT.Exp).then_inc(e_ok, 1)
                    act.wait_ge(t_mm, T + 1)
                    wait(act, o_mm, T)
                    nc.scalar.activation(PT[:, :, :], psT[:, :, :].rearrange("p a (b q) -> p (a b) q", q=P),
                                         ACT.Copy).then_inc(pt_ok, 1)
                if tile(T - 1):
                    act.wait_ge(ot_mm, T)
                    nc.scalar.activation(OT[:, 1 - u, :], psX[:, 0:P], ACT.Copy).then_inc(ot_ok, 1)
            steps(act, step)

        @block.tensor
        def _(pe):
            def scores(T, u):
                pe.wait_ge(q_ok, T + 1)
                pe.wait_ge(keys_ok, T * 2 + 2)
                wait(pe, sm_ok, T - 1)
                for k in range(2):
                    for b in range(2):
                        last = nc.tensor.matmul(psS[S * b:S * b + S, u, k, :], queries[:, u, S * b:S * b + S],
                                                keys[:, u, b, 8 * k:8 * k + 8, :].rearrange("p h s -> p (h s)"),
                                                start=True, stop=True)
                last.then_inc(s_mm, 1)
            scores(0, 0)
            scores(1, 1)

            def step(T, u):
                if tile(T):
                    pe.wait_ge(e_ok, T + 1)
                    wait(pe, pt_ok, T)
                    for p in range(NPAIR):
                        last = nc.tensor.transpose(psT[:, p // 4, p % 4 * P:(p % 4 + 1) * P],
                                                   E[:, u, 2 * p:2 * p + 2, :].rearrange("p h s -> p (h s)"),
                                                   w["ident"][:, :])
                    last.then_inc(t_mm, 1)
                if tile(T - 1):
                    pe.wait_ge(on_ok, T)
                    wait(pe, x_ok, T - 1)
                    nc.tensor.transpose(psX[:, 0:P], O[:, 1 - u, :], w["ident"][:, :]).then_inc(ot_mm, 1)
                if tile(T + 2):
                    scores(T + 2, u)
                if tile(T):
                    pe.wait_ge(pt_ok, T + 1)
                    pe.wait_ge(values_ok, T + 1)
                    wait(pe, on_ok, T)
                    for b in range(2):
                        for p in range(NPAIR):
                            last = nc.tensor.matmul(psO[S * b:S * b + S, 32 * p:32 * p + 18], PT[:, p, S * b:S * b + S],
                                                    values[:, u, b, p, :], start=True, stop=True)
                    last.then_inc(o_mm, 1)
                if tile(T - 1):
                    pe.wait_ge(ot_ok, T)
                    nc.tensor.matmul(psX[:, P:2 * P], OT[:, 1 - u, :], w["wout"][:, :], start=True, stop=True).then_inc(out_mm, 1)
            steps(pe, step)

        @block.vector
        def _(dve):
            def take_queries(T, u):
                wait(dve, s_mm, T - 1)
                q = qT[:, bass.ds(T * P, P)]
                nc.vector.tensor_tensor(queries[:, u, :], q, q, ALU.max).then_inc(q_ok, 1)
            take_queries(0, 0)
            take_queries(1, 1)
            take_queries(2, 0)

            def step(T, u):
                if tile(T):
                    dve.wait_ge(s_mm, T + 1)
                    wait(dve, t_mm, T - 1)
                    nc.vector.tensor_tensor(E[:, u, :, :], psS[:, u, :, :].rearrange("p a (h s) -> p (a h) s", s=S),
                                            w["window"][:, :].unsqueeze(1).broadcast_to([P, H, S]), ALU.add).then_inc(sm_ok, 1)
                    dve.wait_ge(sm_ok, T + 1)
                    nc.vector.reduce_max(mx[:, u, :], E[:, u, :, :], AX.X).then_inc(mx_ok, 1)
                    dve.wait_ge(mx_ok, T + 1)
                    nc.vector.tensor_tensor(E[:, u, :, :], E[:, u, :, :], heads(mx[:, u, :]), ALU.subtract).then_inc(sub_ok, 1)
                if tile(T - 1):
                    dve.wait_ge(o_mm, T)
                    sums = psO[:, 0:32 * NPAIR].rearrange("p (g e) -> p g e", g=NPAIR)
                    nc.vector.reciprocal(rs[:, 1 - u, :, :], sums[:, :, 16:18]).then_inc(rs_ok, 1)
                    dve.wait_ge(rs_ok, T)
                    nc.vector.tensor_tensor(O[:, 1 - u, :].rearrange("p (g h e) -> p g h e", g=NPAIR, h=2),
                                            sums[:, :, 0:16].rearrange("p g (h e) -> p g h e", h=2),
                                            rs[:, 1 - u, :, :].unsqueeze(3).broadcast_to([P, NPAIR, 2, DH]),
                                            ALU.mult).then_inc(on_ok, 1)
                if tile(T - 2):
                    dve.wait_ge(out_mm, T - 1)
                    x = X[:, bass.ds(T - 2, 1), :].rearrange("p a b -> p (a b)")
                    nc.vector.tensor_tensor(x, psX[:, P:2 * P], x, ALU.add).then_inc(x_ok, 1)
                if tile(T + 3):
                    take_queries(T + 3, 1 - u)
            steps(dve, step)


def second_experts(nc, d, X):
    with ExitStack() as ctx:
        def sb(name, shape, dt=F32):
            return ctx.enter_context(nc.sbuf_tensor("m2_" + name, shape, dt))

        own = []

        def sem(name):
            own.append(ctx.enter_context(nc.semaphore("m2_" + name)))
            return own[-1]

        names = ("ident", "gate2", "before8", "upto128", "ones")
        w = {n: sb(n, list(d[n].shape)) for n in names}
        ln = Norm(nc, sb, sem, "ln")
        xn = sb("xn", [P, 2, G, D])
        xnT = sb("xnT", [P, TOK])
        xhi, xlo = sb("xhi", [P, TOK], F32R), sb("xlo", [P, TOK], F32R)
        whi, wlo = sb("whi", [P, 2, 2 * P], F32R), sb("wlo", [P, 2, 2 * P], F32R)
        sc, mk, gtm, ties, pa, pb_ = (sb(n, [P, NT, E2]) for n in ("sc", "mk", "gtm", "ties", "pa", "pb"))
        wt = sb("wt", [P, NT, E2 + 1])
        mx, tot, rs, need = (sb(n, [P, NT]) for n in ("mx", "tot", "rs", "need"))
        gm, grank, kept = (sb(n, [P, NT, G2]) for n in ("gm", "grank", "kept"))
        gt, eq = sb("gt", [P, NT, G2, G2]), sb("eq", [P, NT, G2, G2])
        best = sb("best", [P, NT, 8])
        w13 = sb("w13", [P, 2, 2 * P])
        w2 = sb("w2", [P, 2, D])
        sl, h = sb("sl", [P, 2, GT]), sb("h", [P, 2, GT])
        ps = ctx.enter_context(nc.psum_tensor("m2_ps", [P, 8, 512], F32))
        w_in, xn_ok, tr_mm, xnT_ok, xhi_ok, xlo_ok, whi_ok, wlo_ok, lg_mm, sub_ok, e_ok, rt, sel_ok, cum_mm, h_mm, sl_ok, h_ok, out_mm, x_ok = (
            sem(n) for n in ("w_in", "xn_ok", "tr_mm", "xnT_ok", "xhi_ok", "xlo_ok", "whi_ok", "wlo_ok", "lg_mm", "sub_ok", "e_ok", "rt", "sel_ok", "cum_mm", "h_mm",
                             "sl_ok", "h_ok", "out_mm", "x_ok"))
        raw_in, ex_in = [sem("raw_in0"), sem("raw_in1")], [sem("ex_in0"), sem("ex_in1")]
        ctx.callback(clear, nc, own)
        block = ctx.enter_context(nc.Block())
        loaded = 16 * len(names)
        PAIRS = E2 // 2

        def wait(eng, s, v):
            if not isinstance(v, int) or v > 0:
                eng.wait_ge(s, v)

        def all_experts(eng, body):
            body(0, 8)
            with eng.Fori(1, PAIRS) as i:
                body(i, 8)
            body(PAIRS, 4)

        @block.sync
        def _(sp):
            load_all(nc, sp, [(w[n], d[n]) for n in names], w_in)

            def body(i, n):
                for u in range(n // 4):
                    wait(sp, wlo_ok, i * 2 + u - 1)
                    e = bass.ds(i * 2 + u, 1)
                    sp.dma_start(w13[:, u, :], d["w13"][e, :, :].rearrange("o p k -> (o p) k")).then_inc(raw_in[u], 16)
                    wait(sp, out_mm, i * 8 + 4 * u - 4)
                    sp.dma_start(w2[:, u, :], d["w2e"][e, :, :].rearrange("o p k -> (o p) k")).then_inc(ex_in[u], 16)
            all_experts(sp, body)

        @block.gpsimd
        def _(pool):
            def lower_tokens(i):
                pool.wait_ge(xhi_ok, i + 1)
                g = slice(i * GT, (i + 1) * GT)
                nc.gpsimd.tensor_tensor(xlo[:, g], xnT[:, g], xhi[:, g].bitcast(F32), ALU.subtract).then_inc(xlo_ok, 1)

            def lower(e, u):
                pool.wait_ge(whi_ok, e + 1)
                nc.gpsimd.tensor_tensor(wlo[:, u, :], w13[:, u, :], whi[:, u, :].bitcast(F32), ALU.subtract).then_inc(wlo_ok, 1)

            ln.prepare(pool)
            for i in range(NG):
                ln.root(pool, i)
                if i > 0:
                    lower_tokens(i - 1)
            lower_tokens(NG - 1)
            lower(0, 0)

            def body(i, n):
                for u in range(n // 4):
                    if n == 8:
                        lower(i * 2 + u + 1, 1 - u)
            all_experts(pool, body)

        @block.scalar
        def _(act):
            def upper(u, rounds):
                act.wait_ge(raw_in[u], rounds * 16 + 16)
                nc.scalar.activation(whi[:, u, :], w13[:, u, :], ACT.Copy).then_inc(whi_ok, 1)

            for i in range(NG):
                act.wait_ge(tr_mm, i + 1)
                nc.scalar.activation(xnT[:, i * GT:(i + 1) * GT], ps[:, i % 2, :], ACT.Copy).then_inc(xnT_ok, 1)
                nc.scalar.activation(xhi[:, i * GT:(i + 1) * GT], ps[:, i % 2, :], ACT.Copy).then_inc(xhi_ok, 1)
            upper(0, 0)
            act.wait_ge(sub_ok, 1)
            nc.scalar.activation(sc[:, :, :], sc[:, :, :], ACT.Exp).then_inc(e_ok, 1)

            def body(i, n):
                for q in range(n):
                    m = i * 8 + q
                    if q in (1, 5) and n == 8:
                        upper(1 - q // 4, i + q // 4)
                    act.wait_ge(h_mm, m * 2 + 1)
                    wait(act, h_ok, m - 1)
                    nc.scalar.activation(sl[:, q % 2, :], ps[:, 4 + (2 * q) % 4, :], ACT.Silu).then_inc(sl_ok, 1)
            all_experts(act, body)

        @block.tensor
        def _(pe):
            pe.wait_ge(w_in, loaded)
            for i in range(NG):
                if i >= 2:
                    pe.wait_ge(xhi_ok, i - 1)
                for t in range(G):
                    pe.wait_ge(xn_ok, i * G + t + 1)
                    last = nc.tensor.transpose(ps[:, i % 2, t * P:(t + 1) * P], xn[:, i % 2, t, :], w["ident"][:, :])
                last.then_inc(tr_mm, 1)
            pe.wait_ge(xhi_ok, NG)
            pe.wait_ge(xlo_ok, NG)
            for t in range(NT):
                last = nc.tensor.matmul(ps[:, 2, t * E2:(t + 1) * E2], xnT[:, t * P:(t + 1) * P], w["gate2"][:, :],
                                        start=True, stop=True)
            last.then_inc(lg_mm, 1)

            def hidden(i, q):
                u, c = q // 4 % 2, q % 4
                if c == 0:
                    wait(pe, wlo_ok, i * 2 + q // 4 + 1)
                    pe.wait_ge(ex_in[u], i * 16 + (16 if q < 8 else 32))
                wait(pe, h_ok, i * 8 + q - 1)
                for k in range(2):
                    for j, (wp, xp) in enumerate(((whi, xhi), (wlo, xhi), (whi, xlo))):
                        last = nc.tensor.matmul(ps[:, 4 + (2 * q + k) % 4, :], wp[:, u, k * P:(k + 1) * P],
                                                xp[:, c * GT:(c + 1) * GT], start=(j == 0), stop=(j == 2))
                    last.then_inc(h_mm, 1)

            hidden(0, 0)
            pe.wait_ge(sel_ok, 1)
            sel = gtm[:, :, :].rearrange("p t e -> p (t e)")
            nc.tensor.matmul(ps[:, 0, :], w["upto128"][:, :], sel, start=True, stop=True).then_inc(cum_mm, 1)
            nc.tensor.matmul(ps[:, 1, :], w["ones"][:, :], sel, start=True, stop=True).then_inc(cum_mm, 1)

            def body(i, n):
                for q in range(n):
                    m = i * 8 + q
                    if n == 8 or q < n - 1:
                        hidden(i, q + 1)
                    pe.wait_ge(h_ok, m + 1)
                    wait(pe, x_ok, m * 4 - 4)
                    for t in range(G):
                        last = nc.tensor.matmul(ps[:, 2 + q % 2, t * P:(t + 1) * P], h[:, q % 2, t * P:(t + 1) * P],
                                                w2[:, q // 4, :], start=True, stop=True)
                    last.then_inc(out_mm, 1)
            all_experts(pe, body)

        @block.vector
        def _(dve):
            v = nc.vector
            steps = [0]

            def then(instruction):
                steps[0] += 1
                instruction.then_inc(rt, 1)
                dve.wait_ge(rt, steps[0])

            for i in range(NG):
                ln.moments(dve, i, lambda t: X[:, i * G + t, :])
                if i >= 2:
                    dve.wait_ge(tr_mm, i - 1)
                for t in range(G):
                    ln.apply(xn[:, i % 2, t, :], X[:, i * G + t, :], t).then_inc(xn_ok, 1)
            dve.wait_ge(w_in, loaded)
            each = lambda a, n: a.unsqueeze(2).broadcast_to([P, NT, n])
            dve.wait_ge(lg_mm, 1)
            logits = ps[:, 2, :].rearrange("p (t e) -> p t e", e=E2)
            then(v.reduce_max(mx[:, :], logits, AX.X))
            v.tensor_tensor(sc[:, :, :], logits, each(mx[:, :], E2), ALU.subtract).then_inc(sub_ok, 1)
            dve.wait_ge(e_ok, 1)
            then(v.reduce_sum(tot[:, :], sc[:, :, :], AX.X))
            then(v.reciprocal(rs[:, :], tot[:, :]))
            then(v.tensor_tensor(sc[:, :, :], sc[:, :, :], each(rs[:, :], E2), ALU.mult))
            then(v.reduce_max(gm[:, :, :], sc[:, :, :].rearrange("p t (g e) -> p t g e", g=G2), AX.X))
            square = [P, NT, G2, G2]
            other, own = gm[:, :, :].unsqueeze(2).broadcast_to(square), gm[:, :, :].unsqueeze(3).broadcast_to(square)
            then(v.tensor_tensor(gt[:, :, :, :], other, own, ALU.is_gt))
            then(v.tensor_tensor(eq[:, :, :, :], other, own, ALU.is_equal))
            then(v.tensor_tensor(eq[:, :, :, :], eq[:, :, :, :], w["before8"][:, :, :].unsqueeze(1).broadcast_to(square),
                                 ALU.mult))
            then(v.tensor_tensor(gt[:, :, :, :], gt[:, :, :, :], eq[:, :, :, :], ALU.add))
            then(v.reduce_sum(grank[:, :, :], gt[:, :, :, :], AX.X))
            then(v.tensor_scalar(kept[:, :, :], grank[:, :, :], float(LG2), None, ALU.is_lt))
            in_groups = lambda a: a[:, :, :].rearrange("p t (g e) -> p t g e", g=G2)
            kept4 = kept[:, :, :].unsqueeze(3).broadcast_to([P, NT, G2, E2 // G2])
            then(v.tensor_tensor(in_groups(mk), in_groups(sc), kept4, ALU.mult))
            then(v.tensor_scalar(kept[:, :, :], kept[:, :, :], 1.0, None, ALU.subtract))
            then(v.tensor_tensor(in_groups(mk), in_groups(mk), kept4, ALU.add))
            for t in range(NT):
                last = v.max(best[:, t, :], mk[:, t, :])
                last.then_inc(rt, 1)
                steps[0] += 1
            dve.wait_ge(rt, steps[0])
            fourth = best[:, :, TOP2 - 1:TOP2].broadcast_to([P, NT, E2])
            then(v.tensor_tensor(gtm[:, :, :], mk[:, :, :], fourth, ALU.is_gt))
            then(v.tensor_tensor(ties[:, :, :], mk[:, :, :], fourth, ALU.is_equal))
            then(v.reduce_sum(tot[:, :], gtm[:, :, :], AX.X))
            then(v.tensor_scalar(need[:, :], tot[:, :], -1.0, float(TOP2), ALU.mult, ALU.add))
            src, dst, k = ties, pa, 1
            while k < E2:
                then(v.tensor_copy(dst[:, :, 0:k], src[:, :, 0:k]))
                then(v.tensor_tensor(dst[:, :, k:E2], src[:, :, k:E2], src[:, :, 0:E2 - k], ALU.add))
                src, dst, k = dst, (pb_ if dst is pa else pa), 2 * k
            then(v.tensor_tensor(dst[:, :, :], src[:, :, :], each(need[:, :], E2), ALU.is_le))
            then(v.tensor_tensor(dst[:, :, :], dst[:, :, :], ties[:, :, :], ALU.mult))
            v.tensor_tensor(gtm[:, :, :], gtm[:, :, :], dst[:, :, :], ALU.add).then_inc(sel_ok, 1)
            dve.wait_ge(sel_ok, 1)
            then(v.tensor_tensor(mk[:, :, :], sc[:, :, :], gtm[:, :, :], ALU.mult))
            then(v.reduce_sum(tot[:, :], mk[:, :, :], AX.X))
            then(v.tensor_scalar(tot[:, :], tot[:, :], 1e-9, None, ALU.add))
            then(v.reciprocal(rs[:, :], tot[:, :]))
            then(v.tensor_tensor(mk[:, :, :], mk[:, :, :], each(rs[:, :], E2), ALU.mult))
            dve.wait_ge(cum_mm, 2)
            then(v.memset(pa[:, 0:1, :], 0.0))
            then(v.tensor_copy(pa[:, 1:NT, :], ps[:, 1, 0:(NT - 1) * E2].rearrange("p (t e) -> p t e", e=E2)))
            src, dst, k = pa, pb_, 1
            while k < NT:
                then(v.tensor_copy(dst[:, 0:k, :], src[:, 0:k, :]))
                then(v.tensor_tensor(dst[:, k:NT, :], src[:, k:NT, :], src[:, 0:NT - k, :], ALU.add))
                src, dst, k = dst, (pb_ if dst is pa else pa), 2 * k
            then(v.tensor_tensor(dst[:, :, :], ps[:, 0, :].rearrange("p (t e) -> p t e", e=E2), src[:, :, :], ALU.add))
            then(v.scalar_tensor_tensor(out=wt[:, :, 0:E2], in0=dst[:, :, :], scalar=float(CAP), in1=mk[:, :, :],
                                        op0=ALU.is_le, op1=ALU.mult))
            then(v.memset(wt[:, :, E2:E2 + 1], 1.0))

            def gated(i, q):
                m = i * 8 + q
                dve.wait_ge(sl_ok, m + 1)
                dve.wait_ge(h_mm, m * 2 + 2)
                wait(dve, out_mm, m - 1)
                v.tensor_tensor(h[:, q % 2, :], ps[:, 4 + (2 * q + 1) % 4, :], sl[:, q % 2, :], ALU.mult).then_inc(h_ok, 1)

            gated(0, 0)

            def body(i, n):
                for q in range(n):
                    m = i * 8 + q
                    if n == 8 or q < n - 1:
                        gated(i, q + 1)
                    dve.wait_ge(out_mm, m + 1)
                    wait(dve, x_ok, m * 4 - 12)
                    for t in range(G):
                        x = X[:, G * (q % 4) + t, :]
                        we = wt[:, G * (q % 4) + t, bass.ds(i * 2 + q // 4, 1)]
                        v.scalar_tensor_tensor(out=x, in0=ps[:, 2 + q % 2, t * P:(t + 1) * P], scalar=we, in1=x,
                                               op0=ALU.mult, op1=ALU.add).then_inc(x_ok, 1)
            all_experts(dve, body)


def build(nc, d, out):
    with ExitStack() as ctx:
        X = ctx.enter_context(nc.sbuf_tensor("X", [P, NT, D], F32))
        first_cross_attention(nc, d, X)
        linear_attention(nc, d, X)
        first_experts(nc, d, X)
        decoder_layer(nc, d, X)
        windowed_attention(nc, d, X)
        second_experts(nc, d, X)
        stored = ctx.enter_context(nc.semaphore("stored"))
        block = ctx.enter_context(nc.Block())

        @block.sync
        def _(sp):
            sp.dma_start(out.rearrange("(t p) d -> p t d", p=P), X[:, :, :]).then_inc(stored, 16)
            sp.wait_ge(stored, 16)


def layouts(i):
    import numpy as np
    a = {k: np.asarray(v) for k, v in i.items()}
    f = np.float32
    g = {"x": a["x"].reshape(TOK, D), "ctxT": a["ctx_1024"].transpose(0, 2, 1)}
    flat = lambda w: w.transpose(1, 0, 2).reshape(D, D)
    g["wq"], g["wv"] = flat(a["L0_xattn_Wq"]), flat(a["L0_xattn_Wv"])
    g["wkT"] = flat(a["L0_xattn_Wk"]).T
    g["wp"] = a["L0_xattn_Wp"]
    for n in ("bq", "bk", "bv"):
        g[n] = a["L0_xattn_" + n].reshape(P, 1)
    g["bp_rows"] = np.broadcast_to(a["L0_xattn_bp"], (P, D))
    rows = np.zeros((4, 32, 2, 2, D), f)
    w = a["L0_xattn_Wp"].reshape(2, 4, 2, DH, D)
    for h in range(2):
        rows[:, DH * h:DH * h + DH, :, h, :] = w[:, :, h].transpose(1, 2, 0, 3)
    g["wp_rows"] = rows.reshape(P, 2, 2, D)
    g["ident"] = np.eye(P, dtype=f)
    r = np.arange(P)
    g["headmask"] = (r[:, None] // DH == np.arange(H)[None]).astype(f)
    g["densel"] = ((r[:, None] % 32 == 16) & (r[:, None] // 32 == r[None] // 32)).astype(f)
    for n in ("q", "k", "g", "v", "o"):
        g["w" + n + "2"] = a["L0_attn_W" + n]
    g["wa"] = a["L0_attn_Wa"]
    g["dtb"], g["alog"] = np.broadcast_to(a["L0_attn_dt_bias"], (P, H)), np.broadcast_to(a["L0_attn_A_log"], (P, H))
    g["rmsw"] = np.tile(a["L0_attn_rms_w"], H).reshape(P, 1)
    s = np.arange(S)
    g["upto"] = (r[:, None] % S <= s[None]).astype(f)
    g["after"] = ((r[:, None] // S == r[None] // S) & (r[:, None] > r[None])).astype(f)
    g["hlmask"] = (r[:, None] // DH % 4 == np.arange(4)[None]).astype(f)
    g["halves"] = (r[:, None] // S == np.arange(2)[None]).astype(f)
    g["blockones"] = (r[:, None] // DH == r[None] // DH).astype(f)
    g["gate1"] = a["L0_ffn_gate_w"].T
    g["ebias"] = np.broadcast_to(a["L0_ffn_expert_bias"], (P, E1))
    e = np.arange(E1)
    g["before8"] = np.broadcast_to((e[None] < e[:, None]).astype(f), (P, E1, E1))
    g["up1"] = a["L0_ffn_w_up"].transpose(0, 2, 1)
    g["down1"] = a["L0_ffn_w_down"].transpose(0, 2, 1).reshape(E1, 2, P, D).transpose(0, 2, 1, 3)
    for n in ("g1", "g2", "g3", "beta1", "beta2", "beta3", "b2"):
        g[n] = np.broadcast_to(a["L1_xattn_" + n], (P, D))
    g["w1"] = a["L1_xattn_w1"]
    g["b1"] = a["L1_xattn_b1"].reshape(4, P).T
    g["w2"] = a["L1_xattn_w2"].reshape(4, P, D).transpose(1, 0, 2)
    g["ctx"] = a["ctx_1024"]
    allowed = (r[:, None] // S == r[None] // S) & (r[None] <= r[:, None])
    g["causal2"] = np.where(allowed, 0, NEVER).astype(f)
    for n, c in zip("qkv", range(3)):
        g["w" + n + "3"] = a["L1_attn_W_qkv"][:, c * D:(c + 1) * D]
    g["wout"] = a["L1_attn_W_out"]
    i, j = r[:, None] % S, s[None]
    g["window"] = np.where((j <= i) & (j > i - WINDOW), 0, NEVER).astype(f)
    g["gate2"] = a["L1_ffn_wg"].T
    both = lambda n, s: np.concatenate([a["L1_ffn_" + n], a["L1_ffn_" + s][None]])
    g["w13"] = np.concatenate([both("w1", "sw1"), both("w3", "sw3")], axis=2)
    g["w2e"] = both("w2", "sw2")
    g["upto128"] = (r[:, None] <= r[None]).astype(f)
    g["ones"] = np.ones((P, P), f)
    return {k: np.ascontiguousarray(v) for k, v in g.items()}


def kernel(**inputs):
    import concourse.bacc as bacc
    from concourse.bass_utils import run_bass_kernel_spmd
    nc = bacc.Bacc("TRN2", target_bir_lowering=False, num_devices=1)
    arrays = layouts(inputs)
    d = {n: nc.dram_tensor("in_" + n, v.shape, mybir.dt.from_np(v.dtype), kind="ExternalInput").ap()
         for n, v in arrays.items()}
    out = nc.dram_tensor("out", (TOK, D), F32, kind="ExternalOutput").ap()
    build(nc, d, out)
    r = run_bass_kernel_spmd(nc, [{"in_" + n: v for n, v in arrays.items()}], core_ids=[0])
    return r.results[0]["out"].reshape(B, S, D)
```
